# Optimizing a Trainium2 kernel written in Bass

```python
import numpy as np
import jax
import jax.numpy as jnp

def _softmax(x, axis=-1):
    return jax.nn.softmax(x, axis=axis)

def _gelu(x):
    return jax.nn.gelu(x, approximate=True)

def _silu(x):
    return jax.nn.silu(x)

def _sigmoid(x):
    return jax.nn.sigmoid(x)

def _layernorm(x, axis=-1, eps=1e-05):
    m = jnp.mean(x, axis=axis, keepdims=True)
    v = jnp.var(x, axis=axis, keepdims=True)
    return (x - m) / jnp.sqrt(v + eps)

def _scatter_add(tgt, idx, src, axis=0):
    return tgt.at[idx].add(src)

def _segment_sum(src, seg, n):
    return jax.ops.segment_sum(src, seg, n)
kernel_name = 'mk_xattn_ffn_d1_seqx_r4_c97a85'

def setup_inputs(seed: int=0):
    np.random.seed(seed)
    _w = jnp.asarray

    def _rec_inputs():
        import jax
        import jax.numpy as jnp
        _rk = jax.random.key(seed)
        x = -0.0002928 + 1 * jax.random.normal(jax.random.fold_in(_rk, 1), (8, 512, 256), jnp.float32)
        _lenS = 512 - jax.random.randint(jax.random.fold_in(_rk, 7), (8,), 0, max(1, 512 // 4) + 1, jnp.int32)
        _lenS2 = 512 - jax.random.randint(jax.random.fold_in(_rk, 8), (8,), 0, max(1, 512 // 4) + 1, jnp.int32)
        _ctx_1024P = jax.random.normal(jax.random.fold_in(_rk, 11), (8, 16, 256), jnp.float32)
        _ctx_1024c = jax.random.dirichlet(jax.random.fold_in(_rk, 511), 0.3 * jnp.ones((16,), jnp.float32), (8, 512))
        _ctx_1024t = jnp.einsum('bsk,bkd->bsd', _ctx_1024c, _ctx_1024P)
        _ctx_1024t = _ctx_1024t * jax.lax.rsqrt(jnp.mean(jnp.square(_ctx_1024t)) + 1e-12) * 0.953939
        ctx_1024 = -1.39393e-06 + 0.999914 * (_ctx_1024t + 0.3 * jax.random.normal(jax.random.fold_in(_rk, 611), (8, 512, 256), jnp.float32))
        return (x, ctx_1024)
    x, ctx_1024 = _rec_inputs()

    def _L0_xattn_setup():
        import math
        import jax, jax.numpy as jnp
        import numpy as np
        B, S, H, NH = (2, 512, 256, 4)
        DH = H // NH

        def _mlstm_parallel(qh, kh, vh, ig, fg, eps=1e-06):
            b, nh, s, dh = qh.shape
            log_f = jax.nn.log_sigmoid(fg)
            pcs = jnp.pad(jnp.cumsum(log_f, axis=-1), ((0, 0), (0, 0), (1, 0)))
            mat = pcs[..., :, None] - pcs[..., None, :]
            ltr = jnp.tril(jnp.ones((s, s), dtype=bool))
            log_fg_matrix = jnp.where(ltr, mat[..., 1:, 1:], -jnp.inf)
            log_D = log_fg_matrix + ig[..., None, :]
            max_log_D = jnp.max(log_D, axis=-1, keepdims=True)
            D = jnp.exp(log_D - max_log_D)
            qk = jnp.einsum('bhsd,bhtd->bhst', qh, kh) / math.sqrt(dh)
            C = qk * D
            normalizer = jnp.maximum(jnp.abs(C.sum(axis=-1, keepdims=True)), jnp.exp(-max_log_D))
            Cn = C / (normalizer + eps)
            return jnp.einsum('bhst,bhtd->bhsd', Cn, vh)
        key = jax.random.key(seed)
        ks = jax.random.split(key, 8)
        gate_std = 1.0 / math.sqrt(3 * H)
        return {'q': jax.random.normal(ks[0], (B, S, H), jnp.float32), 'k': jax.random.normal(ks[1], (B, S, H), jnp.float32), 'v': jax.random.normal(ks[2], (B, S, H), jnp.float32), 'w_igate': jax.random.normal(ks[3], (NH, 3 * H), jnp.float32) * gate_std, 'b_igate': jax.random.normal(ks[4], (NH,), jnp.float32) * 0.1, 'w_fgate': jax.random.normal(ks[5], (NH, 3 * H), jnp.float32) * gate_std, 'b_fgate': jnp.linspace(3.4, 6.0, NH, dtype=jnp.float32), 'ln_weight': jnp.zeros((H,), jnp.float32)}
    _L0_xattn_all = _L0_xattn_setup()
    _L0_xattn_in = {k: v for k, v in _L0_xattn_all.items() if k in ('w_igate', 'b_igate', 'w_fgate', 'b_fgate', 'ln_weight')}
    del _L0_xattn_all

    def _L0_ffn_setup():
        import jax, jax.numpy as jnp
        import numpy as np
        BLOCK = 32
        W_BITS = 4
        ACT_BITS = 16

        def act_qdq(x):
            qmax = 2.0 ** (ACT_BITS - 1) - 1.0
            scale = jnp.maximum(jnp.max(jnp.abs(x)) / qmax, 1e-12)
            return jnp.clip(jnp.round(x / scale), -qmax - 1.0, qmax) * scale

        def fixed_qdq_u16(x):
            scale = 1.0 / 65536.0
            return jnp.clip(jnp.round(x / scale), 0.0, 65535.0) * scale

        def lpbq_dequant(w):
            O, I = w.shape
            qmax = 2.0 ** (W_BITS - 1) - 1.0
            wb = w.reshape(O, I // BLOCK, BLOCK)
            s = jnp.maximum(jnp.max(jnp.abs(wb), axis=-1, keepdims=True) / qmax, 1e-12)
            wq = jnp.clip(jnp.round(wb / s), -qmax - 1.0, qmax) * s
            return wq.reshape(O, I)
        key = jax.random.key(seed)
        k1, k2, k3, k4 = jax.random.split(key, 4)
        B, S, H, I = (2, 1024, 256, 768)
        x = jax.random.normal(k1, (B, S, H), jnp.float32)
        w_gate = jax.random.normal(k2, (I, H), jnp.float32) * 0.02
        w_up = jax.random.normal(k3, (I, H), jnp.float32) * 0.02
        w_down = jax.random.normal(k4, (H, I), jnp.float32) * 0.02
        return {'x': x, 'w_gate': w_gate, 'w_up': w_up, 'w_down': w_down}
    _L0_ffn_all = _L0_ffn_setup()
    _L0_ffn_in = {k: v for k, v in _L0_ffn_all.items() if k in ('w_gate', 'w_up', 'w_down')}
    del _L0_ffn_all
    return {'x': x, 'ctx_1024': ctx_1024, 'L0_xattn_w_igate': _L0_xattn_in['w_igate'], 'L0_xattn_b_igate': _L0_xattn_in['b_igate'], 'L0_xattn_w_fgate': _L0_xattn_in['w_fgate'], 'L0_xattn_b_fgate': _L0_xattn_in['b_fgate'], 'L0_xattn_ln_weight': _L0_xattn_in['ln_weight'], 'L0_ffn_w_gate': _L0_ffn_in['w_gate'], 'L0_ffn_w_up': _L0_ffn_in['w_up'], 'L0_ffn_w_down': _L0_ffn_in['w_down']}

def reference(x, ctx_1024, L0_xattn_w_igate, L0_xattn_b_igate, L0_xattn_w_fgate, L0_xattn_b_fgate, L0_xattn_ln_weight, L0_ffn_w_gate, L0_ffn_w_up, L0_ffn_w_down):
    import jax
    import jax.numpy as jnp

    def _L0_xattn_ref(q, k, v, w_igate, b_igate, w_fgate, b_fgate, ln_weight):
        import math
        import jax, jax.numpy as jnp
        import numpy as np
        B, S, H, NH = (2, 512, 256, 4)
        DH = H // NH

        def _mlstm_parallel(qh, kh, vh, ig, fg, eps=1e-06):
            b, nh, s, dh = qh.shape
            log_f = jax.nn.log_sigmoid(fg)
            pcs = jnp.pad(jnp.cumsum(log_f, axis=-1), ((0, 0), (0, 0), (1, 0)))
            mat = pcs[..., :, None] - pcs[..., None, :]
            ltr = jnp.tril(jnp.ones((s, s), dtype=bool))
            log_fg_matrix = jnp.where(ltr, mat[..., 1:, 1:], -jnp.inf)
            log_D = log_fg_matrix + ig[..., None, :]
            max_log_D = jnp.max(log_D, axis=-1, keepdims=True)
            D = jnp.exp(log_D - max_log_D)
            qk = jnp.einsum('bhsd,bhtd->bhst', qh, kh) / math.sqrt(dh)
            C = qk * D
            normalizer = jnp.maximum(jnp.abs(C.sum(axis=-1, keepdims=True)), jnp.exp(-max_log_D))
            Cn = C / (normalizer + eps)
            return jnp.einsum('bhst,bhtd->bhsd', Cn, vh)
        b, s, h = q.shape
        nh = b_igate.shape[0]
        dh = h // nh
        gin = jnp.concatenate([q, k, v], axis=-1)
        ig = jnp.einsum('bsd,hd->bhs', gin, w_igate) + b_igate[None, :, None]
        fg = jnp.einsum('bsd,hd->bhs', gin, w_fgate) + b_fgate[None, :, None]
        qh = q.reshape(b, s, nh, dh).transpose(0, 2, 1, 3)
        kh = k.reshape(b, s, nh, dh).transpose(0, 2, 1, 3)
        vh = v.reshape(b, s, nh, dh).transpose(0, 2, 1, 3)
        hst = _mlstm_parallel(qh, kh, vh, ig, fg)
        mean = hst.mean(axis=-1, keepdims=True)
        var = hst.var(axis=-1, keepdims=True)
        hn = (hst - mean) / jnp.sqrt(var + 1e-05)
        scale = (1.0 + ln_weight).reshape(nh, dh)
        hn = hn * scale[None, :, None, :]
        return hn.transpose(0, 2, 1, 3).reshape(b, s, h)

    def _L0_ffn_ref(x, w_gate, w_up, w_down):
        import jax, jax.numpy as jnp
        import numpy as np
        BLOCK = 32
        W_BITS = 4
        ACT_BITS = 16

        def act_qdq(x):
            qmax = 2.0 ** (ACT_BITS - 1) - 1.0
            scale = jnp.maximum(jnp.max(jnp.abs(x)) / qmax, 1e-12)
            return jnp.clip(jnp.round(x / scale), -qmax - 1.0, qmax) * scale

        def fixed_qdq_u16(x):
            scale = 1.0 / 65536.0
            return jnp.clip(jnp.round(x / scale), 0.0, 65535.0) * scale

        def lpbq_dequant(w):
            O, I = w.shape
            qmax = 2.0 ** (W_BITS - 1) - 1.0
            wb = w.reshape(O, I // BLOCK, BLOCK)
            s = jnp.maximum(jnp.max(jnp.abs(wb), axis=-1, keepdims=True) / qmax, 1e-12)
            wq = jnp.clip(jnp.round(wb / s), -qmax - 1.0, qmax) * s
            return wq.reshape(O, I)
        x = act_qdq(x)
        up = act_qdq(x @ lpbq_dequant(w_up).T)
        gate = act_qdq(x @ lpbq_dequant(w_gate).T)
        sig = fixed_qdq_u16(jax.nn.sigmoid(gate))
        gate = act_qdq(gate * sig)
        o = act_qdq(gate * up)
        return o @ lpbq_dequant(w_down).T
    x = x + _L0_xattn_ref(_layernorm(x, axis=-1), ctx_1024, ctx_1024, L0_xattn_w_igate, L0_xattn_b_igate, L0_xattn_w_fgate, L0_xattn_b_fgate, L0_xattn_ln_weight)
    x = x + _L0_ffn_ref(_layernorm(x, axis=-1), L0_ffn_w_gate, L0_ffn_w_up, L0_ffn_w_down)
    return x

_drawn_inputs = setup_inputs


def setup_inputs(seed=0):
    import zlib

    import numpy as np

    out = dict(_drawn_inputs(seed))
    spreads = {'L0_xattn_ln_weight': (0.0, 0.1)}
    factors = {'L0_xattn_b_igate': 64.0,
     'L0_ffn_w_gate': 3.081,
     'L0_ffn_w_up': 2.953,
     'L0_ffn_w_down': 2.955}
    for name, (base, spread) in spreads.items():
        noise = np.random.default_rng([zlib.crc32(name.encode()), seed]).standard_normal(out[name].shape)
        drawn = base * np.exp(spread * noise) if base else spread * noise
        out[name] = jnp.asarray(drawn.astype(out[name].dtype))
    for name, factor in factors.items():
        out[name] = (out[name] * factor).astype(out[name].dtype)
    return out
```

```python
import concourse.bass as bass
from concourse import mybir
from contextlib import ExitStack


def attention_ffn(nc, x, ctx_1024, w_igate, b_igate, w_fgate, b_fgate, ln_weight,
                  w_gate, w_up, w_down, out):
    F32, F16 = mybir.dt.float32, mybir.dt.float16
    I16, U16, I32 = mybir.dt.int16, mybir.dt.uint16, mybir.dt.int32
    ALU, ACT, AX = mybir.AluOpType, mybir.ActivationFunctionType, mybir.AxisListType.X
    RMAX = bass.bass_isa.ReduceOp.max
    ds = bass.ds

    P = 128
    B, S, H = x.shape
    NH = w_igate.shape[0]
    DH = H // NH
    NC = S // P
    KH = H // P
    HP = NH // KH
    FF = w_gate.shape[0]
    FT = FF // P
    BW = FT * S
    VA = DH + 1
    QMAX = 32767.0
    WBLOCK, WQMAX = 32, 7.0
    LN_EPS, NORM_EPS, MIN_SCALE = 1e-5, 1e-6, 1e-12

    W_AT = {1: 0, 2: NH, 3: 3 * NH}
    E_AT = 6 * NH
    N_AT = 9 * NH
    ARGS = 13 * NH

    h_dram = nc.dram_tensor("h_rows", [B, S, H], F32, kind="Internal").ap()

    with ExitStack() as stack:
        def sem(name):
            return stack.enter_context(nc.semaphore(name))

        ARENA = 53200
        arena = stack.enter_context(nc.sbuf_tensor("arena", [P, ARENA], F32))

        def view(at, *dims, dt=F32):
            n = 1
            for d in dims:
                n *= d
            words = n if dt in (F32, I32) else n // 2
            assert at + words <= ARENA, (at, words)
            v = arena[:, at:at + words]
            if dt is not F32:
                v = v.bitcast(dt)
            if len(dims) == 2:
                v = v.rearrange("p (a b) -> p a b", b=dims[1])
            if len(dims) == 3:
                v = v.rearrange("p (a b c) -> p a b c", b=dims[1], c=dims[2])
            if len(dims) == 4:
                v = v.rearrange("p (a b c d) -> p a b c d", b=dims[1], c=dims[2], d=dims[3])
            return v

        class Space:
            def __init__(self, at, end):
                self.at, self.end = at, end

            def take(self, *dims, dt=F32):
                n = 1
                for d in dims:
                    n *= d
                v = view(self.at, *dims, dt=dt)
                self.at += (n if dt in (F32, I32) else n // 2)
                self.at += self.at % 2
                assert self.at <= self.end, (self.at, self.end)
                return v

        HALF = BW // 2
        GU_AT, GQ_AT = 0, HALF + B * BW
        XS_AT = GQ_AT + B * HALF
        KEEP_AT = XS_AT + KH * B * S
        gu = view(GU_AT + HALF, B, BW)
        uq = view(GU_AT, B * 2, BW, dt=I16)
        gq = view(GQ_AT, B, BW, dt=I16)
        x2T = view(GQ_AT, KH, B * S)
        xs = view(XS_AT, 2, KH, B * S, dt=F16)
        keep = Space(KEEP_AT, ARENA)
        wgT = keep.take(2, KH, FF, dt=F16)
        wuT = keep.take(2, KH, FF, dt=F16)
        wdT = keep.take(2, FT, H, dt=F16)
        xmax = keep.take(B)
        sc = keep.take(64)
        gmax = keep.take(B)
        umax = keep.take(B)
        pmax = keep.take(3 * B)
        omax = keep.take(3 * B)
        TW = BW // 3
        sig = keep.take(TW)
        sq = keep.take(TW, dt=U16)
        os_ = view(XS_AT, 4, BW, dt=F16)
        at = Space(0, GQ_AT)
        x_nat = [at.take(NC, H) for _ in range(2)]
        c_nat = [at.take(NC, H) for _ in range(2)]
        ctx = [at.take(NC, NH, VA) for _ in range(2)]
        q_nat = at.take(NC, H)
        qT = [at.take(KH, S) for _ in range(2)]
        kT = [at.take(KH, S) for _ in range(2)]
        gsb = at.take(NC, 2 * NH)
        nabs = at.take(NC, NH)
        e_f = at.take(NC, NH)
        l_f = at.take(NC, NH)
        logf = at.take(NC, NH)
        f_sb = at.take(NC, NH)
        a_pad = [at.take(NC, NH, P // NH) for _ in range(2)]
        m_row = at.take(S)
        m_bc = [at.take(NH, S) for _ in range(2)]
        args = at.take(ARGS)
        wexp = [at.take(ARGS) for _ in range(2)]
        dec = [at.take(NH, P) for _ in range(2)]
        prob = [at.take(NH, P) for _ in range(2)]
        kw = at.take(3, NH, DH)
        state = at.take(KH, HP, VA)
        inter = at.take(NH, VA)
        num = at.take(NC, NH, VA)
        nstat = at.take(NC, NH, 6)
        cen = at.take(NC, H)
        h_nat = [at.take(NC, H) for _ in range(2)]
        x2 = cen
        st1, mv1, rs1, nm1, v1 = at.take(NC, 6), at.take(NC, 2), at.take(NC), at.take(NC), at.take(NC)
        st2, mv2, rs2, nm2, v2 = at.take(NC, 6), at.take(NC, 2), at.take(NC), at.take(NC), at.take(NC)
        t1, t2, t3, t4, t5, t6 = (at.take(NC, NH) for _ in range(6))
        rr, gg = at.take(NC, NH), at.take(NC, NH)
        mhalf = at.take(NC * NH)
        ident = at.take(P)
        tri = at.take(P)
        ones = at.take(P)
        zeros = at.take(2)
        hsel = at.take(NH)
        misc = Space(GQ_AT + KH * B * S, XS_AT)
        w8 = misc.take(3 * H)
        w8T = misc.take(3 * KH, 2 * NH)
        wgq = misc.take(KH, 2 * NH)
        wgkv = misc.take(KH, 2 * NH)
        bias8 = misc.take(2 * NH)
        lnw = misc.take(H)
        ident16 = misc.take(P, dt=F16)
        WN = 2 * FT * H + KH * FF
        WB = WN // WBLOCK
        prep = Space(XS_AT, KEEP_AT)
        w_nat = prep.take(WN)
        w_lo = prep.take(WN, dt=F16)
        w_int = misc.take(WN, dt=I16)
        bmax = prep.take(WB)
        binv = prep.take(WB)
        w_hi = w_int.bitcast(F16)
        tmx = keep.take(4)
        pw2 = keep.take(4)
        amp = keep.take(4)

        psum = stack.enter_context(nc.psum_tensor("psum", [P, 8, 512], F32))
        T0, T1, G, SE, SO, OB, IB, ST = range(8)

        h_back_buf = [view(GU_AT + p * BW + HALF, NC, H) for p in range(2)]
        y_buf = [view(GU_AT + (2 + p) * BW + HALF, NC, H) for p in range(2)]

        psum16 = psum[:, T0:T0 + 2, :].bitcast(F16)
        wflat = [w.rearrange("p a b c -> p (a b c)") for w in (wgT, wuT, wdT)]
        w_parts = [wflat[n // 3][:, (n % 3) * 1024:(n % 3 + 1) * 1024] for n in range(9)]

        names = ("const_ready gates_in bias_in w_in lnw_in "
                 "w_max_ready w_max_all w_split w_tr w_tr_out "
                 "gw_tr gw_sb gw_ready "
                 "ln1_var ln1_rstd ln1_nm ln1_out ktr k_out qtr q_out gates_ps gates_sb "
                 "nabs_ready logf_e logf_l logf_ready fsum_ps f_out a_ready a_tr m_scan m_bcast "
                 "m_masked m_nat args_ready wexp_ready "
                 "scores dec_ready prob_ready intra kw_ready state_ps state_sb inter_ps num_ready "
                 "norm_var norm_rstd cen_ready scaled_ready h_ready ln2_var ln2_rstd ln2_nm ln2_out "
                 "x2tr x2_out x2_max "
                 "xmax_row xmax_all xhi xs_ready mm_gate gate_out gate_max gmax_row gmax_all "
                 "scales_ready gq_ready sig_ready sq_ready p_ready p_done pmax_row pmax_all mm_up up_out up_max "
                 "umax_row umax_all uq_ready o_ready o_max omax_row omax_all o_int o_hi o_split mm_down down_out "
                 "lnw_ready ctx_ones held "
                 "chain_w chain_a chain_b chain_f")
        s = {n: sem(n) for n in names.split()}
        x_in = [sem(f"x_in{p}") for p in range(2)]
        ctx_in = [sem(f"ctx_in{p}") for p in range(2)]
        h_stored = [sem(f"h_stored{p}") for p in range(2)]
        h_back = [sem(f"h_back{p}") for p in range(2)]
        y_stored = [sem(f"y_stored{p}") for p in range(2)]

        def wait(eng, sm, value):
            if isinstance(value, int) and value <= 0:
                return
            eng.wait_ge(s[sm] if isinstance(sm, str) else sm, value)

        def hold(eng):
            eng.sem_inc(s["held"], 1)

        class Chain:
            def __init__(self, eng, name, base=0):
                self.eng, self.name, self.base, self.n = eng, name, base, 0

            def link(self, ins):
                self.n += 1
                ins.then_inc(s[self.name], 1)
                self.eng.wait_ge(s[self.name], self.base + self.n)

        class Row:
            def __init__(self, half, par):
                self.b, self.half, self.par = 2 * half + par, half, par

        def steps(eng, step):
            step(Row(0, 0), None)
            step(Row(0, 1), Row(0, 0))
            with eng.Fori(0, B // 2 - 1) as i:
                step(Row(i + 1, 0), Row(i, 1))
                step(Row(i + 1, 1), Row(i + 1, 0))
            step(None, Row(B // 2 - 1, 1))

        CHAIN_A, CHAIN_B = 4, 12
        block = stack.enter_context(nc.Block())

        @block.sync
        def _(sp):
            def load(r):
                x_rows = x[ds(r.b, 1)].rearrange("o (c p) h -> p (o c) h", p=P)
                c_rows = ctx_1024[ds(r.b, 1)].rearrange("o (c p) h -> p (o c) h", p=P)
                sp.dma_start(x_nat[r.par], x_rows).then_inc(x_in[r.par], 16)
                sp.dma_start(c_nat[r.par], c_rows).then_inc(ctx_in[r.par], 16)

            load(Row(0, 0))
            w3 = w_nat.rearrange("p (t c) -> p t c", c=H)
            sp.dma_start(w3[:, 0:FT, :], w_gate.rearrange("(t p) c -> p t c", p=P)).then_inc(s["w_in"], 16)
            sp.dma_start(w3[:, FT:2 * FT, :], w_up.rearrange("(t p) c -> p t c", p=P)).then_inc(s["w_in"], 16)
            sp.dma_start(w_nat[:, 2 * FT * H:WN].rearrange("p (t c) -> p t c", c=FF),
                         w_down.rearrange("(t p) c -> p t c", p=P)).then_inc(s["w_in"], 16)
            load(Row(0, 1))
            for p in range(2):
                sp.sem_inc(h_stored[p], 16)

            def store_h(r):
                wait(sp, "h_ready", r.b + 1)
                hold(sp)
                sp.dma_start(h_dram[ds(r.b, 1)].rearrange("o (c p) h -> p (o c) h", p=P),
                             h_nat[r.par]).then_inc(h_stored[r.par], 16)

            def reload(r, half):
                wait(sp, "h_ready", r.b + 1)
                hold(sp)
                wait(sp, "intra", NC * (r.b + 1))
                hold(sp)
                load(Row(half, r.par))

            with sp.Fori(0, B // 2 - 1) as i:
                for p in range(2):
                    r = Row(i, p)
                    store_h(r)
                    reload(r, i + 1)
            for p in range(2):
                store_h(Row(B // 2 - 1, p))
            for p in range(2):
                wait(sp, h_stored[p], 16 * (B // 2 + 1))

            def fetch(b, p):
                sp.dma_start(h_back_buf[p], h_dram[ds(b, 1)].rearrange("o (c p) h -> p (o c) h", p=P))\
                    .then_inc(h_back[p], 16)

            def store_y(b, p):
                sp.wait_ge(s["down_out"], 2 * (b + 1) + 4)
                hold(sp)
                sp.dma_start(out[ds(b, 1)].rearrange("o (c p) h -> p (o c) h", p=P), y_buf[p])\
                    .then_inc(y_stored[p], 16)

            for p in range(2):
                sp.sem_inc(y_stored[p], 16)
            sp.wait_ge(s["uq_ready"], 3 * B)
            for p in range(2):
                fetch(p, p)
            with sp.Fori(0, B // 2 - 1) as i:
                for p in range(2):
                    store_y(2 * i + p, p)
                    fetch(2 * i + p + 2, p)
            for p in range(2):
                store_y(B - 2 + p, p)
            for p in range(2):
                sp.wait_ge(y_stored[p], 16 * (B // 2) + 16)

        @block.gpsimd
        def _(pool):
            for t in (ident, tri, a_pad[0].rearrange("p a b c -> p (a b c)"),
                      a_pad[1].rearrange("p a b c -> p (a b c)"), zeros, hsel, ident16,
                      state.rearrange("p a b c -> p (a b c)")):
                pool.memset(t, 0.0)
            pool.memset(ones, 1.0)
            pool.memset(mhalf, -0.5)
            for p in range(2):
                pool.memset(ctx[p][:, :, :, DH:VA], 1.0)
            pool.drain().then_inc(s["const_ready"], 1)
            pool.wait_ge(s["const_ready"], 1)
            pool.affine_select(out=ident, in_=ident, compare_op=ALU.not_equal, fill=1.0, base=0,
                               pattern=[[-1, P]], channel_multiplier=1)
            pool.affine_select(out=ident16, in_=ident16, compare_op=ALU.not_equal, fill=1.0, base=0,
                               pattern=[[-1, P]], channel_multiplier=1)
            pool.affine_select(out=tri, in_=tri, compare_op=ALU.is_gt, fill=1.0, base=0,
                               pattern=[[-1, P]], channel_multiplier=1)
            pool.affine_select(out=hsel, in_=hsel, compare_op=ALU.not_equal, fill=1.0, base=0,
                               pattern=[[-(P // NH), NH]], channel_multiplier=1)
            pool.drain().then_inc(s["const_ready"], 1)
            pool.dma_start(w8[0:NH, :], w_igate).then_inc(s["gates_in"], 16)
            pool.dma_start(w8[NH:2 * NH, :], w_fgate).then_inc(s["gates_in"], 16)
            pool.dma_start(bias8[0:1, 0:NH], b_igate.rearrange("(o n) -> o n", o=1)).then_inc(s["bias_in"], 16)
            pool.dma_start(bias8[0:1, NH:2 * NH], b_fgate.rearrange("(o n) -> o n", o=1)).then_inc(s["bias_in"], 16)
            pool.dma_start(lnw, ln_weight.rearrange("(o n) -> o n", o=1).to_broadcast([P, H])).then_inc(s["lnw_in"], 16)

            pool.wait_ge(s["w_max_ready"], 1)
            pool.partition_all_reduce(pw2[:, 0:3], tmx[:, 0:3], P, RMAX).then_inc(s["w_max_all"], 1)

            def front(r):
                pool.wait_ge(s["ln1_var"], r.b + 1)
                wait(pool, "ln1_out", r.b)
                hold(pool)
                pool.tensor_tensor(out=rs1, in0=v1, in1=mhalf[:, 0:NC], op=ALU.pow)\
                    .then_inc(s["ln1_rstd"], 1)

            def front_ctx(r):
                pool.wait_ge(ctx_in[r.par], 16 * (r.half + 1))
                wait(pool, "intra", NC * (r.b - 1))
                hold(pool)
                pool.tensor_copy(ctx[r.par][:, :, :, 0:DH],
                                 c_nat[r.par].rearrange("p c (h d) -> p c h d", d=DH))\
                    .then_inc(s["ctx_ones"], 1)

            def front_max(r):
                pool.wait_ge(s["m_scan"], r.b + 1)
                wait(pool, "dec_ready", NC * (r.b - 1))
                pool.wait_ge(s["ctx_ones"], r.b + 1)
                hold(pool)
                for h in range(NH):
                    last = pool.partition_broadcast(m_bc[r.par][:, h, :],
                                                    m_row[h * (P // NH):h * (P // NH) + 1, :])
                last.then_inc(s["m_bcast"], 1)
                pool.wait_ge(s["m_bcast"], r.b + 1)
                hold(pool)
                v = m_bc[r.par].rearrange("p h (c t) -> p (h c) t", t=P)
                pool.affine_select(out=v, in_=v, compare_op=ALU.is_ge, fill=1e30, base=0,
                                   pattern=[[0, NH * NC], [1, P]], channel_multiplier=-1)\
                    .then_inc(s["m_masked"], 1)

            def back_norm(r):
                pool.wait_ge(s["norm_var"], r.b + 1)
                hold(pool)
                pool.tensor_tensor(out=t6.rearrange("p a b -> p (a b)"),
                                   in0=t5.rearrange("p a b -> p (a b)"), in1=mhalf, op=ALU.pow)\
                    .then_inc(s["norm_rstd"], 1)
                pool.wait_ge(s["lnw_ready"], 1)
                pool.wait_ge(s["cen_ready"], r.b + 1)
                pool.wait_ge(h_stored[r.par], 16 * (r.half + 1))
                hold(pool)
                pool.tensor_tensor(out=h_nat[r.par], in0=cen,
                                   in1=lnw.unsqueeze(1).to_broadcast([P, NC, H]), op=ALU.mult)\
                    .then_inc(s["scaled_ready"], 1)
                pool.wait_ge(s["ln2_var"], r.b + 1)
                wait(pool, "ln2_out", r.b)
                hold(pool)
                pool.tensor_tensor(out=rs2, in0=v2, in1=mhalf[:, 0:NC], op=ALU.pow)\
                    .then_inc(s["ln2_rstd"], 1)

            pool.wait_ge(s["lnw_in"], 16)
            pool.tensor_scalar(lnw, lnw, 1.0, None, ALU.add).then_inc(s["lnw_ready"], 1)

            def step(f, b):
                if f:
                    front(f)
                    front_ctx(f)
                    front_max(f)
                if b:
                    back_norm(b)

            steps(pool, step)

            def reduce_all(col, src, n, row, done, v=1):
                pool.wait_ge(s[row], v)
                pool.partition_all_reduce(sc[:, col:col + n], sc[:, src:src + n], P, RMAX)\
                    .then_inc(s[done], 1)

            reduce_all(1, 0, 1, "xmax_row", "xmax_all")
            reduce_all(11, 10, 1, "gmax_row", "gmax_all")
            reduce_all(21, 20, 1, "pmax_row", "pmax_all")
            reduce_all(31, 30, 1, "umax_row", "umax_all")
            reduce_all(41, 40, 1, "omax_row", "omax_all")

        @block.scalar
        def _(act):
            act.preload_act_table_set("natural_log_exp_and_others")

            def weights_out():
                for n in range(9):
                    act.wait_ge(s["w_tr"], n + 1)
                    nc.scalar.activation(w_parts[n], psum16[:, n % 2, :], ACT.Copy)\
                        .then_inc(s["w_tr_out"], 1)

            def front_ln(r):
                act.wait_ge(s["ln1_nm"], r.b + 1)
                wait(act, "qtr", 2 * r.b)
                for c in range(NC):
                    last = nc.scalar.activation(q_nat[:, c, :], x_nat[r.par][:, c, :], ACT.Identity,
                                                scale=rs1[:, c:c + 1], bias=nm1[:, c:c + 1])
                last.then_inc(s["ln1_out"], 1)

            def front_q(r):
                wait(act, "inter_ps", 3 * (r.b - 1))
                wait(act, "scores", NC * (r.b - 1))
                for k in range(KH):
                    act.wait_ge(s["qtr"], 2 * r.b + k + 1)
                    nc.scalar.activation(qT[r.par][:, k, :], psum[:, T0 + k, :], ACT.Copy)\
                        .then_inc(s["q_out"], 1)

            def front_logf(r):
                act.wait_ge(s["nabs_ready"], r.b + 1)
                nc.scalar.activation(e_f, nabs, ACT.Exp).then_inc(s["logf_e"], 1)
                act.wait_ge(s["logf_e"], r.b + 1)
                wait(act, "logf_ready", r.b)
                nc.scalar.activation(l_f, e_f, ACT.Ln, bias=1.0).then_inc(s["logf_l"], 1)

            def front_exp(r):
                act.wait_ge(s["args_ready"], r.b + 1)
                wait(act, "num_ready", NC * (r.b - 1))
                wait(act, "norm_var", r.b - 1)
                nc.scalar.activation(wexp[r.par], args, ACT.Exp).then_inc(s["wexp_ready"], 1)

            def decay(r, c):
                if c == 0:
                    act.wait_ge(s["m_masked"], r.b + 1)
                wait(act, "prob_ready", 2 * (NC * r.b + c - 1))
                for h in range(NH):
                    last = nc.scalar.activation(dec[c % 2][:, h, :], m_bc[r.par][:, h, c * P:(c + 1) * P],
                                                ACT.Exp, scale=-1.0, bias=a_pad[r.par][:, c, h, 0:1])
                last.then_inc(s["dec_ready"], 1)

            def state_out(r, i):
                act.wait_ge(s["state_ps"], 3 * r.b + i)
                wait(act, "inter_ps", 3 * r.b + i - 1)
                for j in range(HP):
                    rows = slice(j * DH, (j + 1) * DH)
                    v = psum[rows, ST, 0:KH * HP * VA].rearrange("p (k j v) -> p k j v", k=KH, j=HP)
                    last = nc.scalar.activation(state[rows, :, j, :], v[:, :, j, :], ACT.Copy,
                                                scale=DH ** -0.5)
                last.then_inc(s["state_sb"], 1)

            def back_ln(r):
                act.wait_ge(s["ln2_nm"], r.b + 1)
                wait(act, "x2tr", 2 * r.b)
                wait(act, "x2_max", r.b)
                for c in range(NC):
                    last = nc.scalar.activation(x2[:, c, :], h_nat[r.par][:, c, :], ACT.Identity,
                                                scale=rs2[:, c:c + 1], bias=nm2[:, c:c + 1])
                last.then_inc(s["ln2_out"], 1)

            def back_x2(r):
                for k in range(KH):
                    act.wait_ge(s["x2tr"], 2 * r.b + k + 1)
                    nc.scalar.activation(x2T[:, k, ds(r.b * S, S)], psum[:, T0 + k, :], ACT.Copy)\
                        .then_inc(s["x2_out"], 1)

            def step(f, b):
                if f:
                    front_ln(f)
                if b:
                    decay(b, 0)
                    decay(b, 1)
                if f:
                    front_q(f)
                if b:
                    state_out(b, 1)
                    decay(b, 2)
                if f:
                    front_logf(f)
                if b:
                    state_out(b, 2)
                    decay(b, 3)
                    state_out(b, 3)
                if f:
                    front_exp(f)
                if b:
                    back_ln(b)
                    back_x2(b)

            weights_out()
            steps(act, step)

            def evacuate(tb, mm, done):
                for t in range(3):
                    act.wait_ge(s[mm], 3 * tb + t + 1)
                    nc.scalar.activation(gu[:, tb, t * TW:(t + 1) * TW],
                                         psum[:, 2 * t:2 * t + 2, :].rearrange("p a b -> p (a b)"),
                                         ACT.Copy).then_inc(s[done], 1)

            with act.Fori(0, B) as tb:
                evacuate(tb, "mm_gate", "gate_out")
            act.preload_act_table_set("sigmoid_and_others")

            def sigmoid(tb, which):
                for t in range(3):
                    n = 3 * tb + t + which * 3 * B
                    act.wait_ge(s["gq_ready"], tb + 1)
                    act.wait_ge(s["p_done"], n + 1)
                    nc.scalar.activation(sig, gq[:, tb, t * TW:(t + 1) * TW], ACT.Sigmoid,
                                         scale=sc[:, 13:14]).then_inc(s["sig_ready"], 1)

            act.sem_inc(s["p_done"], 1)
            with act.Fori(0, B) as tb:
                sigmoid(tb, 0)
                evacuate(tb, "mm_up", "up_out")
            with act.Fori(0, B) as tb:
                sigmoid(tb, 1)
            act.wait_ge(s["scales_ready"], 4)
            with act.Fori(0, B) as tb:
                for t in range(3):
                    nc.scalar.activation(uq[:, 2 * tb, t * TW:(t + 1) * TW],
                                         gu[:, tb, t * TW:(t + 1) * TW], ACT.Copy,
                                         scale=sc[:, 32:33]).then_inc(s["uq_ready"], 1)
                    act.wait_ge(s["uq_ready"], 3 * tb + t + 1)

        @block.tensor
        def _(pe):
            pe.wait_ge(s["const_ready"], 2)
            pe.wait_ge(s["gates_in"], 32)
            for k in range(3 * KH):
                last = nc.tensor.transpose(psum[:, G, k * 2 * NH:(k + 1) * 2 * NH],
                                           w8[0:2 * NH, k * P:(k + 1) * P], ident[0:2 * NH, 0:2 * NH])
            last.then_inc(s["gw_tr"], 1)
            pe.wait_ge(s["w_split"], 1)
            n = 0
            for w in range(3):
                nk, nt = (KH, FT) if w < 2 else (FT, KH)
                width = H if w < 2 else FF
                for part in (w_hi, w_lo):
                    for k in range(nk):
                        for t in range(nt):
                            if n % 8 == 0 and n >= 16:
                                pe.wait_ge(s["w_tr_out"], n // 8 - 1)
                            src = part[:, w * FT * H + t * width + k * P:w * FT * H + t * width + (k + 1) * P]
                            last = nc.tensor.transpose(psum16[:, (n // 8) % 2, (n % 8) * P:(n % 8 + 1) * P],
                                                       src, ident16)
                            n += 1
                            if n % 8 == 0:
                                last.then_inc(s["w_tr"], 1)
            pe.wait_ge(s["w_tr_out"], 9)
            pe.wait_ge(s["gw_ready"], 1)
            pe.wait_ge(s["bias_in"], 32)

            def front_k(r):
                pe.wait_ge(ctx_in[r.par], 16 * (r.half + 1))
                wait(pe, "q_out", 2 * r.b)
                wait(pe, "x2_out", 2 * (r.b - 1))
                for k in range(KH):
                    for c in range(NC):
                        last = nc.tensor.transpose(psum[:, T0 + k, c * P:(c + 1) * P],
                                                   c_nat[r.par][:, c, k * P:(k + 1) * P], ident)
                    last.then_inc(s["ktr"], 1)

            def front_q(r):
                pe.wait_ge(s["ln1_out"], r.b + 1)
                for k in range(KH):
                    pe.wait_ge(s["k_out"], 2 * r.b + k + 1)
                    for c in range(NC):
                        last = nc.tensor.transpose(psum[:, T0 + k, c * P:(c + 1) * P],
                                                   q_nat[:, c, k * P:(k + 1) * P], ident)
                    last.then_inc(s["qtr"], 1)

            def front_gates(r):
                pe.wait_ge(s["q_out"], 2 * (r.b + 1))
                wait(pe, "args_ready", r.b)
                for c in range(NC):
                    to = psum[:, G, c * 2 * NH:(c + 1) * 2 * NH]
                    at_c = slice(c * P, (c + 1) * P)
                    nc.tensor.matmul(to, ones[0:1, :], bias8[0:1, :], start=True, stop=False)
                    for k in range(KH):
                        nc.tensor.matmul(to, qT[r.par][:, k, at_c], wgq[:, k, :], start=False, stop=False)
                    for k in range(KH):
                        last = nc.tensor.matmul(to, kT[r.par][:, k, at_c], wgkv[:, k, :],
                                                start=False, stop=k == KH - 1)
                last.then_inc(s["gates_ps"], 1)

            def front_fsum(r):
                pe.wait_ge(s["logf_ready"], r.b + 1)
                to = psum[:, G, 0:NC * NH].rearrange("p (c h) -> p c h", h=NH)
                nc.tensor.matmul(to, tri, logf, start=True, stop=False)
                for c in range(NC - 1):
                    last = nc.tensor.matmul(to[:, c + 1:NC, :], ones,
                                            logf[:, c:c + 1, :].to_broadcast([P, NC - 1 - c, NH]),
                                            start=False, stop=c == NC - 2)
                last.then_inc(s["fsum_ps"], 1)

            def front_atr(r):
                pe.wait_ge(s["a_ready"], r.b + 1)
                for c in range(NC):
                    last = nc.tensor.transpose(psum[:, G, c * P:(c + 1) * P],
                                               a_pad[r.par][:, c, :, :].rearrange("p h z -> p (h z)"), ident)
                last.then_inc(s["a_tr"], 1)

            def front_mnat(r):
                pe.wait_ge(s["m_scan"], r.b + 1)
                for c in range(NC):
                    last = nc.tensor.matmul(psum[:, G, c * NH:(c + 1) * NH], m_row[:, c * P:(c + 1) * P],
                                            hsel, start=True, stop=True)
                last.then_inc(s["m_nat"], 1)

            def scores(r, c):
                if c == 0:
                    pe.wait_ge(s["ctx_ones"], r.b + 1)
                    pe.wait_ge(s["q_out"], 2 * (r.b + 1))
                wait(pe, "prob_ready", 2 * (NC * r.b + c))
                at_c = slice(c * P, (c + 1) * P)
                for k in range(KH):
                    for j in range(HP):
                        rows = slice(j * DH, (j + 1) * DH)
                        last = nc.tensor.matmul(psum[:, SE + j, k * P:(k + 1) * P], kT[r.par][rows, k, at_c],
                                                qT[r.par][rows, k, at_c], start=True, stop=True)
                last.then_inc(s["scores"], 1)

            def intra(r, c):
                pe.wait_ge(s["prob_ready"], 2 * (NC * r.b + c + 1))
                wait(pe, "num_ready", NC * r.b + c)
                for h in range(NH):
                    last = nc.tensor.matmul(psum[:, OB, h * VA:(h + 1) * VA], prob[c % 2][:, h, :],
                                            ctx[r.par][:, c, h, :], start=True, stop=True)
                last.then_inc(s["intra"], 1)

            def states(r, i):
                pe.wait_ge(s["kw_ready"], 3 * r.b + i)
                wait(pe, "state_sb", 3 * r.b + i - 1)
                for k in range(KH):
                    for c in range(i):
                        heads = slice(k * HP, (k + 1) * HP)
                        last = nc.tensor.matmul(psum[:, ST, k * HP * VA:(k + 1) * HP * VA],
                                                kw[:, c, heads, :].rearrange("p h d -> p (h d)"),
                                                ctx[r.par][:, c, heads, :].rearrange("p h d -> p (h d)"),
                                                start=c == 0, stop=c == i - 1)
                last.then_inc(s["state_ps"], 1)

            def inter_(r, c):
                pe.wait_ge(s["state_sb"], 3 * r.b + c)
                wait(pe, "num_ready", NC * r.b + c)
                for k in range(KH):
                    last = nc.tensor.matmul(psum[:, IB, k * HP * VA:(k + 1) * HP * VA],
                                            qT[r.par][:, k, c * P:(c + 1) * P],
                                            state[:, k, :, :].rearrange("p h d -> p (h d)"),
                                            start=True, stop=True)
                last.then_inc(s["inter_ps"], 1)

            def back_x2(r):
                pe.wait_ge(s["ln2_out"], r.b + 1)
                for k in range(KH):
                    for c in range(NC):
                        last = nc.tensor.transpose(psum[:, T0 + k, c * P:(c + 1) * P],
                                                   x2[:, c, k * P:(k + 1) * P], ident)
                    last.then_inc(s["x2tr"], 1)

            def step(f, b):
                if f:
                    front_k(f)
                if b:
                    scores(b, 0)
                if f:
                    front_q(f)
                if b:
                    intra(b, 0)
                    scores(b, 1)
                    states(b, 1)
                if f:
                    front_gates(f)
                if b:
                    inter_(b, 1)
                    intra(b, 1)
                    scores(b, 2)
                    states(b, 2)
                if f:
                    front_fsum(f)
                if b:
                    inter_(b, 2)
                    intra(b, 2)
                    scores(b, 3)
                    states(b, 3)
                if f:
                    front_atr(f)
                if b:
                    inter_(b, 3)
                    intra(b, 3)
                if f:
                    front_mnat(f)
                if b:
                    back_x2(b)

            steps(pe, step)

            PASSES = ((0, 0), (0, 1), (1, 0))

            def project(tb, wT, mm, out_done, before):
                for t in range(3):
                    pe.wait_ge(s[out_done], 3 * tb + t + 1 + before)
                    for m in (2 * t, 2 * t + 1):
                        n = 0
                        for wp, xp in PASSES:
                            for k in range(KH):
                                last = nc.tensor.matmul(psum[:, m, :], wT[:, wp, k, m * P:(m + 1) * P],
                                                        xs[:, xp, k, ds(tb * S, S)],
                                                        start=n == 0, stop=n == 3 * KH - 1)
                                n += 1
                    last.then_inc(s[mm], 1)

            wait(pe, "x2_out", 2 * B)
            pe.sem_inc(s["gate_out"], 3)
            with pe.Fori(0, B) as tb:
                pe.wait_ge(s["xs_ready"], tb + 1)
                project(tb, wgT, "mm_gate", "gate_out", 0)
            pe.wait_ge(s["gate_out"], 3 * B + 3)
            pe.sem_inc(s["up_out"], 3)
            with pe.Fori(0, B) as tb:
                pe.wait_ge(s["gq_ready"], tb + 1)
                project(tb, wuT, "mm_up", "up_out", 0)
            pe.wait_ge(s["up_out"], 3 * B + 3)
            pe.sem_inc(s["down_out"], 4)

            with pe.Fori(0, B // 2) as i:
                for p in range(2):
                    b = 2 * i + p
                    pe.wait_ge(s["o_split"], b + 1)
                    for half in range(2):
                        pe.wait_ge(s["down_out"], 2 * b + half + 1)
                        for c in (2 * half, 2 * half + 1):
                            n = 0
                            for op, wp in ((0, 0), (0, 1), (1, 0)):
                                for t in range(FT):
                                    last = nc.tensor.matmul(
                                        psum[:, 2 * p + half, (c % 2) * H:(c % 2 + 1) * H],
                                        os_[:, 2 * p + op, t * S + c * P:t * S + (c + 1) * P],
                                        wdT[:, wp, t, :], start=n == 0, stop=n == 3 * FT - 1)
                                    n += 1
                        last.then_inc(s["mm_down"], 1)

        @block.vector
        def _(dve):
            V = nc.vector
            cw = Chain(dve, "chain_w")
            dve.wait_ge(s["gw_tr"], 1)
            cw.link(V.tensor_copy(w8T.rearrange("p a b -> p (a b)"), psum[:, G, 0:3 * KH * 2 * NH]))
            cw.link(V.tensor_copy(wgq, w8T[:, 0:KH, :]))
            V.tensor_tensor(wgkv, w8T[:, KH:2 * KH, :], w8T[:, 2 * KH:3 * KH, :], ALU.add)\
                .then_inc(s["gw_ready"], 1)
            dve.wait_ge(s["w_in"], 48)
            wv = w_nat.rearrange("p (n e) -> p n e", e=WBLOCK)
            cw.link(V.tensor_reduce(bmax, wv, AX, ALU.max, apply_absolute_value=True))
            cw.link(V.tensor_scalar(bmax, bmax, 1.0 / WQMAX, MIN_SCALE, ALU.mult, ALU.max))
            cw.link(V.reciprocal(binv, bmax))
            V.tensor_tensor(w_int.rearrange("p (n e) -> p n e", e=WBLOCK), wv,
                            binv.unsqueeze(2).to_broadcast([P, WB, WBLOCK]), ALU.mult)
            n1 = FT * H // WBLOCK
            cw.link(V.tensor_reduce(tmx[:, 0:3], bmax.rearrange("p (w n) -> p w n", n=n1), AX, ALU.max))
            V.tensor_scalar(tmx[:, 0:3], tmx[:, 0:3], WQMAX, None, ALU.mult).then_inc(s["w_max_ready"], 1)
            cw.link(V.tensor_tensor(wv, w_int.rearrange("p (n e) -> p n e", e=WBLOCK),
                                    bmax.unsqueeze(2).to_broadcast([P, WB, WBLOCK]), ALU.mult))
            dve.wait_ge(s["w_max_all"], 1)
            cw.link(V.tensor_scalar(pw2[:, 0:3].bitcast(I32), pw2[:, 0:3].bitcast(I32), 0x7F800000, None,
                                    ALU.bitwise_and))
            cw.link(V.tensor_scalar(pw2[:, 0:3], pw2[:, 0:3], 2.0 ** -100, None, ALU.max))
            cw.link(V.reciprocal(amp[:, 0:3], pw2[:, 0:3]))
            cw.link(V.tensor_scalar(amp[:, 0:3], amp[:, 0:3], 2.0 ** 14, None, ALU.mult))
            for w in range(3):
                cols = slice(w * FT * H, (w + 1) * FT * H)
                last = V.tensor_scalar(w_hi[:, cols], w_nat[:, cols], amp[:, w:w + 1], None, ALU.mult)
            cw.link(last)
            for w in range(3):
                cols = slice(w * FT * H, (w + 1) * FT * H)
                last = V.scalar_tensor_tensor(w_lo[:, cols], w_nat[:, cols], amp[:, w:w + 1], w_hi[:, cols],
                                              ALU.mult, ALU.subtract)
            last.then_inc(s["w_split"], 1)

            def front_stats(r, ch):
                dve.wait_ge(x_in[r.par], 16 * (r.half + 1))
                for c in range(NC):
                    last = V.bn_stats(st1[:, c, :], x_nat[r.par][:, c, :])
                ch.link(last)
                wait(dve, "ln1_out", r.b)
                hold(dve)
                for c in range(NC):
                    last = V.bn_aggr(mv1[:, c, :], st1[:, c, :])
                ch.link(last)
                V.tensor_scalar(v1, mv1[:, :, 1], LN_EPS, None, ALU.add).then_inc(s["ln1_var"], 1)

            def front_nm(r):
                dve.wait_ge(s["ln1_rstd"], r.b + 1)
                V.scalar_tensor_tensor(nm1, mv1[:, :, 0], -1.0, rs1, ALU.mult, ALU.mult)\
                    .then_inc(s["ln1_nm"], 1)

            def front_k(r):
                wait(dve, "scores", NC * (r.b - 1))
                for k in range(KH):
                    dve.wait_ge(s["ktr"], 2 * r.b + k + 1)
                    V.tensor_copy(kT[r.par][:, k, :], psum[:, T0 + k, :]).then_inc(s["k_out"], 1)

            def front_gates(r):
                dve.wait_ge(s["gates_ps"], r.b + 1)
                V.tensor_copy(gsb, psum[:, G, 0:NC * 2 * NH].rearrange("p (c g) -> p c g", g=2 * NH))\
                    .then_inc(s["gates_sb"], 1)
                dve.wait_ge(s["gates_sb"], r.b + 1)
                f = gsb[:, :, NH:2 * NH]
                V.scalar_tensor_tensor(nabs, f, -1.0, f, ALU.mult, ALU.min)\
                    .then_inc(s["nabs_ready"], 1)

            def front_logf(r):
                dve.wait_ge(s["logf_l"], r.b + 1)
                V.scalar_tensor_tensor(logf, gsb[:, :, NH:2 * NH], 0.0, l_f, ALU.min, ALU.subtract)\
                    .then_inc(s["logf_ready"], 1)

            def front_a(r):
                dve.wait_ge(s["fsum_ps"], r.b + 1)
                wait(dve, "dec_ready", NC * (r.b - 1))
                fsum = psum[:, G, 0:NC * NH].rearrange("p (c h) -> p c h", h=NH)
                V.tensor_copy(f_sb, fsum)
                V.tensor_tensor(a_pad[r.par][:, :, :, 0], gsb[:, :, 0:NH], fsum, ALU.subtract)\
                    .then_inc(s["a_ready"], 1)

            def front_scan(r):
                dve.wait_ge(s["a_tr"], r.b + 1)
                wait(dve, "m_bcast", r.b)
                V.tensor_tensor_scan(m_row, psum[:, G, :], zeros[:, 0:1].to_broadcast([P, S]), -3.0e38, ALU.max, ALU.add)\
                    .then_inc(s["m_scan"], 1)

            def front_args(r, ch):
                dve.wait_ge(s["m_nat"], r.b + 1)
                dve.wait_ge(s["m_masked"], r.b + 1)
                wait(dve, "wexp_ready", r.b)
                a = a_pad[r.par][:, :, :, 0]
                mn = psum[:, G, 0:NC * NH].rearrange("p (c h) -> p c h", h=NH)
                ends = m_bc[r.par].rearrange("p h (c t) -> p c h t", t=P)[:, :, :, P - 1]
                for i in range(1, NC):
                    V.tensor_tensor(args[:, W_AT[i]:W_AT[i] + i * NH].rearrange("p (c h) -> p c h", h=NH),
                                    a[:, 0:i, :], ends[:, i - 1:i, :].to_broadcast([P, i, NH]), ALU.subtract)
                V.tensor_tensor(args[:, E_AT:N_AT].rearrange("p (c h) -> p c h", h=NH),
                                ends[:, 0:NC - 1, :], mn[:, 1:NC, :], ALU.subtract)
                V.scalar_tensor_tensor(args[:, N_AT:ARGS].rearrange("p (c h) -> p c h", h=NH),
                                       mn, -1.0, f_sb, ALU.mult, ALU.subtract).then_inc(s["args_ready"], 1)

            def probs(r, c):
                dve.wait_ge(s["scores"], NC * r.b + c + 1)
                dve.wait_ge(s["dec_ready"], NC * r.b + c + 1)
                wait(dve, "intra", NC * r.b + c - 1)
                for j in range(HP):
                    V.scalar_tensor_tensor(prob[c % 2].rearrange("p (k j) t -> p j k t", j=HP)[:, j],
                                           psum[:, SE + j, 0:KH * P].rearrange("p (k t) -> p k t", t=P),
                                           DH ** -0.5,
                                           dec[c % 2].rearrange("p (k j) t -> p j k t", j=HP)[:, j],
                                           ALU.mult, ALU.mult).then_inc(s["prob_ready"], 1)

            def weigh_keys(r, i):
                if i == 1:
                    dve.wait_ge(s["wexp_ready"], r.b + 1)
                    dve.wait_ge(ctx_in[r.par], 16 * (r.half + 1))
                wait(dve, "state_ps", 3 * r.b + i - 1)
                w = wexp[r.par][:, W_AT[i]:W_AT[i] + i * NH].rearrange("p (n o) -> p n o", o=1)
                V.tensor_tensor(kw.rearrange("p c h d -> p (c h) d")[:, 0:i * NH, :],
                                c_nat[r.par].rearrange("p c (h d) -> p (c h) d", d=DH)[:, 0:i * NH, :],
                                w.to_broadcast([P, i * NH, DH]), ALU.mult).then_inc(s["kw_ready"], 1)

            def numerators(r, c, ch):
                dve.wait_ge(s["intra"], NC * r.b + c + 1)
                o = psum[:, OB, 0:NH * VA].rearrange("p (h v) -> p h v", v=VA)
                if c == 0:
                    V.tensor_copy(num[:, c], o).then_inc(s["num_ready"], 1)
                else:
                    dve.wait_ge(s["inter_ps"], 3 * r.b + c)
                    e = wexp[r.par][:, E_AT + (c - 1) * NH:E_AT + c * NH].unsqueeze(2)
                    ch.link(V.tensor_tensor(inter, psum[:, IB, 0:NH * VA].rearrange("p (h v) -> p h v", v=VA),
                                            e.to_broadcast([P, NH, VA]), ALU.mult))
                    V.tensor_tensor(num[:, c], o, inter, ALU.add).then_inc(s["num_ready"], 1)
                dve.wait_ge(s["num_ready"], NC * r.b + c + 1)
                for h in range(NH):
                    last = V.bn_stats(nstat[:, c, h, :], num[:, c, h, 0:DH])
                ch.link(last)

            def normalise(r, ch):
                dve.wait_ge(s["wexp_ready"], r.b + 1)
                enm = wexp[r.par][:, N_AT:ARGS].rearrange("p (c h) -> p c h", h=NH)
                me, mo = nstat[:, :, :, 1], nstat[:, :, :, 4]
                V.scalar_tensor_tensor(t1, num[:, :, :, DH], -1.0, num[:, :, :, DH], ALU.mult, ALU.max)
                V.tensor_tensor(t2, me, mo, ALU.add)
                ch.link(V.tensor_tensor(t3, me, mo, ALU.subtract))
                V.tensor_tensor(t1, t1, enm, ALU.max)
                V.tensor_tensor(t4, nstat[:, :, :, 2], nstat[:, :, :, 5], ALU.add)
                ch.link(V.tensor_tensor(t3, t3, t3, ALU.mult))
                V.tensor_scalar(t1, t1, NORM_EPS, None, ALU.add)
                V.tensor_scalar(t2, t2, 0.5, None, ALU.mult)
                ch.link(V.tensor_scalar(t4, t4, 4.0 / DH, None, ALU.mult))
                V.reciprocal(rr, t1)
                ch.link(V.tensor_tensor(t4, t4, t3, ALU.add))
                ch.link(V.tensor_tensor(t3, rr, rr, ALU.mult))
                ch.link(V.scalar_tensor_tensor(t4, t4, 0.25, t3, ALU.mult, ALU.mult))
                V.tensor_scalar(t5, t4, LN_EPS, None, ALU.add).then_inc(s["norm_var"], 1)
                dve.wait_ge(s["norm_rstd"], r.b + 1)
                ch.link(V.tensor_tensor(gg, rr, t6, ALU.mult))
                wait(dve, "x2tr", 2 * r.b)
                for c in range(NC):
                    for h in range(NH):
                        last = V.tensor_scalar(cen[:, c, h * DH:(h + 1) * DH], num[:, c, h, 0:DH],
                                               t2[:, c, h:h + 1], gg[:, c, h:h + 1],
                                               ALU.subtract, ALU.mult)
                last.then_inc(s["cen_ready"], 1)

            def residual(r, ch):
                dve.wait_ge(s["scaled_ready"], r.b + 1)
                V.tensor_tensor(h_nat[r.par], h_nat[r.par], x_nat[r.par], ALU.add).then_inc(s["h_ready"], 1)
                dve.wait_ge(s["h_ready"], r.b + 1)
                for c in range(NC):
                    last = V.bn_stats(st2[:, c, :], h_nat[r.par][:, c, :])
                ch.link(last)
                hold(dve)
                for c in range(NC):
                    last = V.bn_aggr(mv2[:, c, :], st2[:, c, :])
                ch.link(last)
                V.tensor_scalar(v2, mv2[:, :, 1], LN_EPS, None, ALU.add).then_inc(s["ln2_var"], 1)
                dve.wait_ge(s["ln2_rstd"], r.b + 1)
                V.scalar_tensor_tensor(nm2, mv2[:, :, 0], -1.0, rs2, ALU.mult, ALU.mult)\
                    .then_inc(s["ln2_nm"], 1)

            def largest(r):
                dve.wait_ge(s["ln2_out"], r.b + 1)
                V.tensor_reduce(xmax[:, ds(r.b, 1)], x2.rearrange("p c h -> p (c h)"), AX, ALU.max,
                                apply_absolute_value=True).then_inc(s["x2_max"], 1)

            NA, NB = 2, NC - 1 + NC + 9

            def step(f, b):
                if f:
                    ca = Chain(dve, "chain_a", NA * f.b)
                    front_stats(f, ca)
                    front_k(f)
                    front_nm(f)
                if b:
                    cb = Chain(dve, "chain_b", NB * b.b)
                    probs(b, 0)
                    weigh_keys(b, 1)
                    numerators(b, 0, cb)
                    probs(b, 1)
                if f:
                    front_gates(f)
                if b:
                    weigh_keys(b, 2)
                    numerators(b, 1, cb)
                    probs(b, 2)
                if f:
                    front_logf(f)
                if b:
                    weigh_keys(b, 3)
                    numerators(b, 2, cb)
                if f:
                    front_a(f)
                if b:
                    probs(b, 3)
                if f:
                    front_scan(f)
                if b:
                    numerators(b, 3, cb)
                    normalise(b, cb)
                if f:
                    front_args(f, ca)
                    assert ca.n == NA, ca.n
                if b:
                    residual(b, cb)
                    largest(b)
                    assert cb.n == NB, cb.n

            steps(dve, step)

            cf = Chain(dve, "chain_f")

            def col(n):
                return sc[:, n:n + 1]

            dve.wait_ge(s["x2_max"], B)
            V.tensor_reduce(col(0), xmax, AX, ALU.max).then_inc(s["xmax_row"], 1)
            dve.wait_ge(s["xmax_all"], 1)
            cf.link(V.tensor_scalar(col(2), col(1), 1.0 / QMAX, MIN_SCALE, ALU.mult, ALU.max))
            cf.link(V.reciprocal(col(3), col(2)))
            cf.link(V.reciprocal(amp[:, 0:3], amp[:, 0:3]))
            V.tensor_tensor(col(14), col(2), amp[:, 0:1], ALU.mult)
            cf.link(V.tensor_tensor(col(34), col(2), amp[:, 1:2], ALU.mult))

            x16 = view(GU_AT + HALF + 7 * BW, KH, S, dt=I16)
            for p in range(2):
                dve.wait_ge(h_stored[p], 16 * (B // 2 + 1))
            dve.wait_ge(s["x2_out"], KH * B)
            with dve.Fori(0, B) as tb:
                src = x2T[:, :, ds(tb * S, S)]
                V.tensor_scalar(x16, src, col(3), QMAX, ALU.mult, ALU.min).then_inc(s["xhi"], 1)
                dve.wait_ge(s["xhi"], 2 * tb + 1)
                V.tensor_copy(xs[:, 0, :, ds(tb * S, S)], x16).then_inc(s["xhi"], 1)
                dve.wait_ge(s["xhi"], 2 * tb + 2)
                V.tensor_tensor(xs[:, 1, :, ds(tb * S, S)], x16, xs[:, 0, :, ds(tb * S, S)],
                                ALU.subtract).then_inc(s["xs_ready"], 1)
                dve.wait_ge(s["xs_ready"], tb + 1)

            def block_max(dst, tb, done, maxed):
                dve.wait_ge(s[done], 3 * tb + 3 + 3)
                V.tensor_reduce(dst[:, ds(tb, 1)], gu[:, tb, :], AX, ALU.max,
                                apply_absolute_value=True).then_inc(s[maxed], 1)

            with dve.Fori(0, B) as tb:
                block_max(gmax, tb, "gate_out", "gate_max")
            dve.wait_ge(s["gate_max"], B)
            V.tensor_reduce(col(10), gmax, AX, ALU.max).then_inc(s["gmax_row"], 1)
            dve.wait_ge(s["gmax_all"], 1)
            cf.link(V.tensor_tensor(col(15), col(11), col(14), ALU.mult))
            cf.link(V.tensor_scalar(col(13), col(15), 1.0 / QMAX, MIN_SCALE, ALU.mult, ALU.max))
            cf.link(V.reciprocal(col(16), col(13)))
            cf.link(V.tensor_tensor(col(12), col(16), col(14), ALU.mult))
            V.tensor_scalar(col(17), col(13), 1.0 / 65536.0, None, ALU.mult).then_inc(s["scales_ready"], 1)
            dve.wait_ge(s["scales_ready"], 1)

            def sig16(tb, t, which):
                n = 3 * tb + t + which * 3 * B
                dve.wait_ge(s["sig_ready"], n + 1)
                V.tensor_scalar(sq, sig, 65536.0, 65535.0, ALU.mult, ALU.min).then_inc(s["sq_ready"], 1)
                dve.wait_ge(s["sq_ready"], n + 1)
                return gq[:, tb, t * TW:(t + 1) * TW]

            with dve.Fori(0, B) as tb:
                V.tensor_scalar(gq[:, tb, :], gu[:, tb, :], col(12), QMAX, ALU.mult, ALU.min)\
                    .then_inc(s["gq_ready"], 1)
                dve.wait_ge(s["gq_ready"], tb + 1)
                for t in range(3):
                    g = sig16(tb, t, 0)
                    V.tensor_tensor(sig, g, sq, ALU.mult).then_inc(s["p_ready"], 1)
                    dve.wait_ge(s["p_ready"], 3 * tb + t + 1)
                    V.tensor_reduce(pmax[:, ds(3 * tb + t, 1)], sig, AX, ALU.max,
                                    apply_absolute_value=True).then_inc(s["p_done"], 1)
                block_max(umax, tb, "up_out", "up_max")
            dve.wait_ge(s["p_done"], 3 * B + 1)
            V.tensor_reduce(col(20), pmax, AX, ALU.max).then_inc(s["pmax_row"], 1)
            dve.wait_ge(s["pmax_all"], 1)
            cf.link(V.tensor_tensor(col(25), col(21), col(17), ALU.mult))
            cf.link(V.tensor_scalar(col(22), col(25), 1.0 / QMAX, MIN_SCALE, ALU.mult, ALU.max))
            cf.link(V.reciprocal(col(23), col(22)))
            V.tensor_tensor(col(24), col(23), col(17), ALU.mult).then_inc(s["scales_ready"], 1)
            dve.wait_ge(s["scales_ready"], 2)
            dve.wait_ge(s["up_max"], B)
            V.tensor_reduce(col(30), umax, AX, ALU.max).then_inc(s["umax_row"], 1)
            with dve.Fori(0, B) as tb:
                for t in range(3):
                    g = sig16(tb, t, 1)
                    V.scalar_tensor_tensor(g, g, col(24), sq, ALU.mult, ALU.mult).then_inc(s["p_done"], 1)
            dve.wait_ge(s["umax_all"], 1)
            cf.link(V.tensor_tensor(col(35), col(31), col(34), ALU.mult))
            cf.link(V.tensor_scalar(col(33), col(35), 1.0 / QMAX, MIN_SCALE, ALU.mult, ALU.max))
            cf.link(V.reciprocal(col(36), col(33)))
            cf.link(V.tensor_tensor(col(32), col(36), col(34), ALU.mult))
            V.tensor_tensor(col(44), col(33), col(22), ALU.mult).then_inc(s["scales_ready"], 2)
            dve.wait_ge(s["p_done"], 6 * B + 1)

            with dve.Fori(0, B) as tb:
                for t in range(3):
                    dve.wait_ge(s["uq_ready"], 3 * tb + t + 1)
                    V.tensor_tensor(sig, gq[:, tb, t * TW:(t + 1) * TW], uq[:, 2 * tb, t * TW:(t + 1) * TW],
                                    ALU.mult).then_inc(s["o_ready"], 1)
                    dve.wait_ge(s["o_ready"], 3 * tb + t + 1)
                    V.tensor_reduce(omax[:, ds(3 * tb + t, 1)], sig, AX, ALU.max,
                                    apply_absolute_value=True).then_inc(s["o_max"], 1)
                    dve.wait_ge(s["o_max"], 3 * tb + t + 1)
            V.tensor_reduce(col(40), omax, AX, ALU.max).then_inc(s["omax_row"], 1)
            dve.wait_ge(s["omax_all"], 1)
            cf.link(V.tensor_tensor(col(47), col(41), col(44), ALU.mult))
            cf.link(V.tensor_scalar(col(42), col(47), 1.0 / QMAX, MIN_SCALE, ALU.mult, ALU.max))
            cf.link(V.reciprocal(col(43), col(42)))
            V.tensor_tensor(col(46), col(42), amp[:, 2:3], ALU.mult)
            cf.link(V.tensor_tensor(col(45), col(43), col(44), ALU.mult))

            o16 = view(GU_AT + HALF + 7 * BW, BW, dt=I16)

            def split(b, p):
                V.scalar_tensor_tensor(o16, gq[:, b, :], col(45), uq[:, 2 * b, :], ALU.mult, ALU.mult)\
                    .then_inc(s["o_int"], 1)
                dve.wait_ge(s["o_int"], b + 1)
                V.tensor_copy(os_[:, 2 * p, :], o16).then_inc(s["o_hi"], 1)
                dve.wait_ge(s["o_hi"], b + 1)
                V.tensor_tensor(os_[:, 2 * p + 1, :], o16, os_[:, 2 * p, :], ALU.subtract)\
                    .then_inc(s["o_split"], 1)
                dve.wait_ge(s["o_split"], b + 1)

            def result(i, p):
                dve.wait_ge(h_back[p], 16 * (i + 1))
                dve.wait_ge(y_stored[p], 16 * (i + 1))
                for half in range(2):
                    dve.wait_ge(s["mm_down"], 2 * (2 * i + p) + half + 1)
                    cols = slice(2 * half, 2 * half + 2)
                    V.scalar_tensor_tensor(y_buf[p][:, cols, :].rearrange("p c h -> p (c h)"),
                                           psum[:, 2 * p + half, :], col(46),
                                           h_back_buf[p][:, cols, :].rearrange("p c h -> p (c h)"),
                                           ALU.mult, ALU.add).then_inc(s["down_out"], 1)

            split(0, 0)
            split(1, 1)
            with dve.Fori(0, B // 2 - 1) as i:
                for p in range(2):
                    result(i, p)
                    split(2 * i + p + 2, p)
            for p in range(2):
                result(B // 2 - 1, p)


_INS = ["x", "ctx_1024", "L0_xattn_w_igate", "L0_xattn_b_igate", "L0_xattn_w_fgate", "L0_xattn_b_fgate",
        "L0_xattn_ln_weight", "L0_ffn_w_gate", "L0_ffn_w_up", "L0_ffn_w_down"]


def kernel(**inputs):
    import numpy as _np
    import concourse.bacc as _bacc
    from concourse import mybir as _mybir
    from concourse.bass_utils import run_bass_kernel_spmd as _run

    nc = _bacc.Bacc("TRN2", target_bir_lowering=False, num_devices=1)
    arrays, args = {}, []
    for name in _INS:
        a = _np.ascontiguousarray(inputs[name])
        arrays[f"in_{name}"] = a
        args.append(nc.dram_tensor(f"in_{name}", a.shape, _mybir.dt.from_np(a.dtype), kind="ExternalInput").ap())
    shape = inputs["x"].shape
    y = nc.dram_tensor("out_y", shape, _mybir.dt.float32, kind="ExternalOutput").ap()
    attention_ffn(nc, *args, y)
    r = _run(nc, [arrays], core_ids=[0])
    return r.results[0]["out_y"]
```

```python
import concourse.bass as bass
from concourse import mybir
from contextlib import ExitStack


def attention_ffn(nc, x, ctx_1024, w_igate, b_igate, w_fgate, b_fgate, ln_weight,
                  w_gate, w_up, w_down, out):
    F32, F16 = mybir.dt.float32, mybir.dt.float16
    I16, U16, I32 = mybir.dt.int16, mybir.dt.uint16, mybir.dt.int32
    ALU, ACT, AX = mybir.AluOpType, mybir.ActivationFunctionType, mybir.AxisListType.X
    RMAX = bass.bass_isa.ReduceOp.max
    ds = bass.ds

    P = 128
    B, S, H = x.shape
    NH = w_igate.shape[0]
    DH = H // NH
    NC = S // P
    KH = H // P
    HP = NH // KH
    FF = w_gate.shape[0]
    FT = FF // P
    BW = FT * S
    VA = DH + 1
    QMAX = 32767.0
    WBLOCK, WQMAX = 32, 7.0
    LN_EPS, NORM_EPS, MIN_SCALE = 1e-5, 1e-6, 1e-12
    NEGATIVE_TOP = 0.279

    W_AT = {1: 0, 2: NH, 3: 3 * NH}
    E_AT = 6 * NH
    N_AT = 9 * NH
    ARGS = 13 * NH

    h_dram = nc.dram_tensor("h_rows", [B, S, H], F32, kind="Internal").ap()

    with ExitStack() as stack:
        def sem(name):
            return stack.enter_context(nc.semaphore(name))

        ARENA = 53200
        arena = stack.enter_context(nc.sbuf_tensor("arena", [P, ARENA], F32))

        def view(at, *dims, dt=F32):
            n = 1
            for d in dims:
                n *= d
            words = n if dt in (F32, I32) else n // 2
            assert at + words <= ARENA, (at, words)
            v = arena[:, at:at + words]
            if dt is not F32:
                v = v.bitcast(dt)
            if len(dims) == 2:
                v = v.rearrange("p (a b) -> p a b", b=dims[1])
            if len(dims) == 3:
                v = v.rearrange("p (a b c) -> p a b c", b=dims[1], c=dims[2])
            if len(dims) == 4:
                v = v.rearrange("p (a b c d) -> p a b c d", b=dims[1], c=dims[2], d=dims[3])
            return v

        class Space:
            def __init__(self, at, end):
                self.at, self.end = at, end

            def take(self, *dims, dt=F32):
                n = 1
                for d in dims:
                    n *= d
                v = view(self.at, *dims, dt=dt)
                self.at += (n if dt in (F32, I32) else n // 2)
                self.at += self.at % 2
                assert self.at <= self.end, (self.at, self.end)
                return v

        HALF = BW // 2
        GU_AT, GQ_AT = 0, B * BW
        XS_AT = GQ_AT + B * HALF
        KEEP_AT = XS_AT + KH * B * S
        gu = view(GU_AT, B, BW)
        gq = view(GQ_AT, B, BW, dt=I16)
        x2T = view(GQ_AT, KH, B * S)
        xs = view(XS_AT, 2, KH, B * S, dt=F16)
        keep = Space(KEEP_AT, ARENA)
        wgT = keep.take(2, KH, FF, dt=F16)
        wuT = keep.take(2, KH, FF, dt=F16)
        wdT = keep.take(2, FT, H, dt=F16)
        xmax = keep.take(B)
        sc = keep.take(64)
        flag = keep.take(2, dt=I32)
        top16 = keep.take(2, dt=I16)[:, 0:1]
        topsq = keep.take(2, dt=U16)[:, 0:1]
        gmax = keep.take(2, B)
        umax = keep.take(3 * B)
        pmax = keep.take(3 * B)
        omax = keep.take(B)
        TW = BW // 3
        SIG_AT = keep.at
        sig = [keep.take(TW) for _ in range(2)]
        sq = [keep.take(TW, dt=U16) for _ in range(2)]
        x16 = view(GU_AT + (B - 1) * BW, 2, KH, S, dt=I16)
        uq = view(XS_AT, 2, BW, dt=I16)
        os_ = view(XS_AT, 4, BW, dt=F16)
        o16 = view(GQ_AT, 2, BW, dt=I16)
        h_back_buf = [view(GQ_AT + BW + p * NC * H, NC, H) for p in range(2)]
        y_buf = [view(GQ_AT + BW + (2 + p) * NC * H, NC, H) for p in range(2)]
        xh = view(XS_AT, B, NC, H)
        at = Space(0, GQ_AT)
        c_nat = [at.take(NC, H) for _ in range(2)]
        ctx = [at.take(NC, NH, VA) for _ in range(2)]
        q_nat = at.take(NC, H)
        qT = [at.take(KH, S) for _ in range(2)]
        kT = [at.take(KH, S) for _ in range(2)]
        gsb = at.take(NC, 2 * NH)
        nabs = at.take(NC, NH)
        e_f = at.take(NC, NH)
        l_f = at.take(NC, NH)
        logf = at.take(NC, NH)
        f_sb = at.take(NC, NH)
        a_pad = [at.take(NC, NH, P // NH) for _ in range(2)]
        m_row = at.take(S)
        g_row = at.take(S)
        m_bc = [at.take(NH, S) for _ in range(2)]
        args = at.take(ARGS)
        wexp = [at.take(ARGS) for _ in range(2)]
        dec = [at.take(NH, P) for _ in range(NC)]
        prob = [at.take(NH, P) for _ in range(2)]
        kw = at.take(3, NH, DH)
        state = at.take(KH, HP, VA)
        inter = at.take(NH, VA)
        num = [at.take(NC, NH, VA) for _ in range(2)]
        nstat = [at.take(NC, NH, 6) for _ in range(2)]
        cen = at.take(NC, H)
        x2 = cen
        st1, mv1, rs1, nm1, v1 = at.take(NC, 6), at.take(NC, 2), at.take(NC), at.take(NC), at.take(NC)
        st2, mv2, rs2, nm2, v2 = at.take(NC, 6), at.take(NC, 2), at.take(NC), at.take(NC), at.take(NC)
        t1, t2, t3, t4, t5, t6 = (at.take(NC, NH) for _ in range(6))
        rr, gg, gm = at.take(NC, NH), at.take(NC, NH), at.take(NC, NH)
        mhalf = at.take(NC * NH)
        ident = at.take(P)
        tri = at.take(P)
        ones = at.take(P)
        zeros = at.take(2)
        hsel = at.take(NH)
        misc = Space(GQ_AT + KH * B * S, XS_AT)
        w8 = misc.take(3 * H)
        w8T = misc.take(3 * KH, 2 * NH)
        wgq = misc.take(KH, 2 * NH)
        wgkv = misc.take(KH, 2 * NH)
        bias8 = misc.take(NC, 2 * NH)
        lnw = misc.take(H)
        ident16 = misc.take(P, dt=F16)
        WN = 2 * FT * H + KH * FF
        WB = WN // WBLOCK
        prep = Space(GQ_AT, GQ_AT + KH * B * S)
        w_nat = prep.take(WN)
        assert WN // 2 <= 3 * TW
        w_lo = view(SIG_AT, WN, dt=F16)
        w_int = misc.take(WN, dt=I16)
        bmax = prep.take(WB)
        binv = prep.take(WB)
        w_hi = w_int.bitcast(F16)
        tmx = keep.take(4)
        pw2 = keep.take(4)
        amp = keep.take(4)

        psum = stack.enter_context(nc.psum_tensor("psum", [P, 8, 512], F32))
        T0, T1, G, SE, SO, OB, IB, ST = range(8)

        psum16 = psum[:, SE:SE + 2, :].bitcast(F16)
        wflat = [w.rearrange("p a b c -> p (a b c)") for w in (wgT, wuT, wdT)]
        w_parts = [wflat[n // 3][:, (n % 3) * 1024:(n % 3 + 1) * 1024] for n in range(9)]

        def col(n):
            return sc[:, n:n + 1]

        names = ("const_ready gates_in bias_in w_in lnw_in "
                 "w_max_ready w_max_all w_split w_tr w_tr_out "
                 "gw_tr gw_sb gw_ready "
                 "ln1_var ln1_rstd ln1_nm ln1_out ktr k_out qtr q_out gates_ps gates_row gates_tr gates_sb "
                 "nabs_ready logf_e logf_l logf_ready fsum_ps f_out a_ready a_tr m_scan m_bcast "
                 "m_masked m_nat args_ready wexp_ready "
                 "scores dec_ready prob_ready intra kw_ready state_ps state_sb inter_ps num_ready "
                 "norm_var norm_rstd norm_ready heads_out scaled_ready h_ready ln2_var ln2_rstd ln2_nm ln2_out "
                 "x2tr x2_out x2_max "
                 "xmax_row xmax_all x16_ready xhi_ready xs_ready mm_gate gate_out gate_max "
                 "gmax_row gmax_all gate_scale top_q top_sig top_ready flag_ready "
                 "all_q all_sig all_sq all_p all_max pmax_row pmax_all p_scale "
                 "gq_ready sig_ready sq_ready p_ready mm_up up_out up_max umax_row umax_all up_scale "
                 "uq_ready o_ready o_max omax_row omax_all o_scale o_int o_hi o_split mm_down down_out "
                 "lnw_ready ctx_ready held "
                 "chain_w chain_a chain_b chain_c chain_f "
                 "h_stored x_rest")
        s = {n: sem(n) for n in names.split()}
        x_in = [sem(f"x_in{p}") for p in range(2)]
        ctx_in = [sem(f"ctx_in{p}") for p in range(2)]
        START = {"x2tr": 2, "x2_max": 1, "heads_out": 1, "x2_out": 2}
        h_back = [sem(f"h_back{p}") for p in range(2)]
        y_stored = [sem(f"y_stored{p}") for p in range(2)]

        def wait(eng, sm, value):
            if isinstance(value, int) and value <= 0:
                return
            if isinstance(sm, str):
                eng.wait_ge(s[sm], value + START.get(sm, 0))
            else:
                eng.wait_ge(sm, value)

        def hold(eng):
            eng.sem_inc(s["held"], 1)

        def row_of(t, r, c):
            return t[:, ds(r.b, 1), c, :].rearrange("p o h -> p (o h)")

        class Chain:
            def __init__(self, eng, name, base=0):
                self.eng, self.name, self.base, self.n = eng, name, base, 0

            def link(self, ins):
                self.n += 1
                ins.then_inc(s[self.name], 1)
                self.eng.wait_ge(s[self.name], self.base + self.n)

        class Row:
            def __init__(self, half, par):
                self.b, self.half, self.par = 2 * half + par, half, par

        def steps(eng, step):
            last = B // 2 - 1
            step(Row(0, 0), None, None, None)
            step(Row(0, 1), Row(0, 0), None, None)
            step(Row(1, 0), Row(0, 1), Row(0, 0), None)
            with eng.Fori(0, B // 2 - 2) as i:
                step(Row(i + 1, 1), Row(i + 1, 0), Row(i, 1), Row(i, 0))
                step(Row(i + 2, 0), Row(i + 1, 1), Row(i + 1, 0), Row(i, 1))
            step(Row(last, 1), Row(last, 0), Row(last - 1, 1), Row(last - 1, 0))
            step(None, Row(last, 1), Row(last, 0), Row(last - 1, 1))
            step(None, None, Row(last, 1), Row(last, 0))
            step(None, None, None, Row(last, 1))

        block = stack.enter_context(nc.Block())

        @block.sync
        def _(sp):
            for name, n in START.items():
                sp.sem_inc(s[name], n)

            def load_x(first, n, done):
                sp.dma_start(xh[:, first:first + n].rearrange("p b c h -> p (b c) h"),
                             x[first:first + n].rearrange("b (c p) h -> p (b c) h", p=P)).then_inc(done, 16)

            def load_ctx(r):
                sp.dma_start(c_nat[r.par], ctx_1024[ds(r.b, 1)].rearrange("o (c p) h -> p (o c) h", p=P))\
                    .then_inc(ctx_in[r.par], 16)

            load_x(0, 1, x_in[0])
            load_ctx(Row(0, 0))
            w3 = w_nat.rearrange("p (t c) -> p t c", c=H)
            sp.dma_start(w3[:, 0:FT, :], w_gate.rearrange("(t p) c -> p t c", p=P)).then_inc(s["w_in"], 16)
            sp.dma_start(w3[:, FT:2 * FT, :], w_up.rearrange("(t p) c -> p t c", p=P)).then_inc(s["w_in"], 16)
            sp.dma_start(w_nat[:, 2 * FT * H:WN].rearrange("p (t c) -> p t c", c=FF),
                         w_down.rearrange("(t p) c -> p t c", p=P)).then_inc(s["w_in"], 16)
            load_x(1, 1, x_in[1])
            load_ctx(Row(0, 1))
            load_x(2, B - 2, s["x_rest"])

            def reload(r, half):
                wait(sp, "kw_ready", 3 * (r.b + 1))
                hold(sp)
                wait(sp, "ktr", 2 * (r.b + 1))
                hold(sp)
                wait(sp, "ctx_ready", r.b + 1)
                hold(sp)
                load_ctx(Row(half, r.par))

            def store_h(r):
                wait(sp, "h_ready", r.b + 1)
                hold(sp)
                sp.dma_start(h_dram[ds(r.b, 1)].rearrange("o (c p) h -> p (o c) h", p=P),
                             xh[:, ds(r.b, 1)].rearrange("p o c h -> p (o c) h")).then_inc(s["h_stored"], 16)

            reload(Row(0, 0), 1)
            with sp.Fori(0, B // 2 - 2) as i:
                reload(Row(i, 1), i + 1)
                store_h(Row(i, 0))
                reload(Row(i + 1, 0), i + 2)
                store_h(Row(i, 1))
            last = B // 2 - 2
            reload(Row(last, 1), last + 1)
            for half in (last, last + 1):
                for p in range(2):
                    store_h(Row(half, p))
            wait(sp, "h_stored", 16 * B)

            def fetch(b, p):
                sp.dma_start(h_back_buf[p], h_dram[ds(b, 1)].rearrange("o (c p) h -> p (o c) h", p=P))\
                    .then_inc(h_back[p], 16)

            def store_y(b, p):
                sp.wait_ge(s["down_out"], 2 * (b + 1) + 4)
                hold(sp)
                sp.dma_start(out[ds(b, 1)].rearrange("o (c p) h -> p (o c) h", p=P), y_buf[p])\
                    .then_inc(y_stored[p], 16)

            for p in range(2):
                sp.sem_inc(y_stored[p], 16)
            sp.wait_ge(s["o_ready"], B + 2)
            for p in range(2):
                fetch(p, p)
            with sp.Fori(0, B // 2 - 1) as i:
                for p in range(2):
                    store_y(2 * i + p, p)
                    fetch(2 * i + p + 2, p)
            for p in range(2):
                store_y(B - 2 + p, p)
            for p in range(2):
                sp.wait_ge(y_stored[p], 16 * (B // 2) + 16)

        @block.gpsimd
        def _(pool):
            for t in (ident, tri, a_pad[0].rearrange("p a b c -> p (a b c)"),
                      a_pad[1].rearrange("p a b c -> p (a b c)"), zeros, hsel, ident16,
                      state.rearrange("p a b c -> p (a b c)")):
                pool.memset(t, 0.0)
            pool.memset(ones, 1.0)
            pool.memset(mhalf, -0.5)
            for p in range(2):
                pool.memset(ctx[p][:, :, :, DH:VA], 1.0)
            pool.drain().then_inc(s["const_ready"], 1)
            pool.wait_ge(s["const_ready"], 1)
            pool.affine_select(out=ident, in_=ident, compare_op=ALU.not_equal, fill=1.0, base=0,
                               pattern=[[-1, P]], channel_multiplier=1)
            pool.affine_select(out=ident16, in_=ident16, compare_op=ALU.not_equal, fill=1.0, base=0,
                               pattern=[[-1, P]], channel_multiplier=1)
            pool.affine_select(out=tri, in_=tri, compare_op=ALU.is_gt, fill=1.0, base=0,
                               pattern=[[-1, P]], channel_multiplier=1)
            pool.affine_select(out=hsel, in_=hsel, compare_op=ALU.not_equal, fill=1.0, base=0,
                               pattern=[[-(P // NH), NH]], channel_multiplier=1)
            pool.drain().then_inc(s["const_ready"], 1)
            pool.dma_start(w8[0:NH, :], w_igate).then_inc(s["gates_in"], 16)
            pool.dma_start(w8[NH:2 * NH, :], w_fgate).then_inc(s["gates_in"], 16)
            for c in range(NC):
                pool.dma_start(bias8[:, c, 0:NH], b_igate.rearrange("(o n) -> o n", o=1).to_broadcast([P, NH]))\
                    .then_inc(s["bias_in"], 16)
                pool.dma_start(bias8[:, c, NH:2 * NH], b_fgate.rearrange("(o n) -> o n", o=1).to_broadcast([P, NH]))\
                    .then_inc(s["bias_in"], 16)
            pool.dma_start(lnw, ln_weight.rearrange("(o n) -> o n", o=1).to_broadcast([P, H])).then_inc(s["lnw_in"], 16)

            def front(r):
                pool.wait_ge(s["ln1_var"], r.b + 1)
                wait(pool, "ln1_out", r.b)
                hold(pool)
                pool.tensor_tensor(out=rs1, in0=v1, in1=mhalf[:, 0:NC], op=ALU.pow)\
                    .then_inc(s["ln1_rstd"], 1)

            def front_bcast(r):
                pool.wait_ge(s["m_scan"], r.b + 1)
                wait(pool, "dec_ready", NC * (r.b - 1))
                hold(pool)
                for h in range(NH):
                    last = pool.partition_broadcast(m_bc[r.par][:, h, :],
                                                    m_row[h * (P // NH):h * (P // NH) + 1, :])
                last.then_inc(s["m_bcast"], 1)

            def front_mask(r):
                pool.wait_ge(s["m_bcast"], r.b + 1)
                hold(pool)
                v = m_bc[r.par].rearrange("p h (c t) -> p (h c) t", t=P)
                pool.affine_select(out=v, in_=v, compare_op=ALU.is_ge, fill=1e30, base=0,
                                   pattern=[[0, NH * NC], [1, P]], channel_multiplier=-1)\
                    .then_inc(s["m_masked"], 1)

            def back_norm(r):
                pool.wait_ge(s["norm_var"], r.b + 1)
                hold(pool)
                pool.tensor_tensor(out=t6.rearrange("p a b -> p (a b)"),
                                   in0=t5.rearrange("p a b -> p (a b)"), in1=mhalf, op=ALU.pow)\
                    .then_inc(s["norm_rstd"], 1)

            def back_scale(r):
                pool.wait_ge(s["lnw_ready"], 1)
                pool.wait_ge(s["heads_out"], r.b + 1 + START["heads_out"])
                hold(pool)
                pool.tensor_tensor(out=cen, in0=cen, in1=lnw.unsqueeze(1).to_broadcast([P, NC, H]),
                                   op=ALU.mult).then_inc(s["scaled_ready"], 1)

            def back_rstd(r):
                pool.wait_ge(s["ln2_var"], r.b + 1)
                hold(pool)
                pool.tensor_tensor(out=rs2, in0=v2, in1=mhalf[:, 0:NC], op=ALU.pow)\
                    .then_inc(s["ln2_rstd"], 1)

            pool.wait_ge(s["lnw_in"], 16)
            pool.tensor_scalar(lnw, lnw, 1.0, None, ALU.add).then_inc(s["lnw_ready"], 1)

            def step(n, f, m, b):
                if b:
                    back_norm(b)
                if n:
                    front(n)
                if b:
                    back_scale(b)
                    wait(pool, "scaled_ready", b.b + 1)
                    hold(pool)
                elif n:
                    pool.wait_ge(s["ln1_rstd"], n.b + 1)
                if f:
                    front_bcast(f)
                if f and b:
                    pool.wait_ge(s["m_bcast"], f.b + 1)
                    hold(pool)
                if b:
                    back_rstd(b)
                if f:
                    front_mask(f)
                if f and not m:
                    pool.wait_ge(s["m_masked"], 1)
                    pool.wait_ge(s["w_max_ready"], 1)
                    pool.partition_all_reduce(pw2[:, 0:3], tmx[:, 0:3], P, RMAX).then_inc(s["w_max_all"], 1)
                    pool.wait_ge(s["w_max_all"], 1)

            steps(pool, step)

            def reduce_all(col, src, n, row, done, v=1):
                pool.wait_ge(s[row], v)
                pool.partition_all_reduce(sc[:, col:col + n], sc[:, src:src + n], P, RMAX)\
                    .then_inc(s[done], 1)

            reduce_all(1, 0, 1, "xmax_row", "xmax_all")
            reduce_all(12, 10, 2, "gmax_row", "gmax_all")
            pool.wait_ge(s["flag_ready"], 1)
            with pool.If(pool.value_load(flag[0:1, 0:1]) > 0):
                reduce_all(23, 22, 1, "pmax_row", "pmax_all")
            reduce_all(31, 30, 1, "umax_row", "umax_all")
            reduce_all(41, 40, 1, "omax_row", "omax_all")

        @block.scalar
        def _(act):
            act.preload_act_table_set("natural_log_exp_and_others")

            def weights_out():
                for n in range(9):
                    act.wait_ge(s["w_tr"], n + 1)
                    nc.scalar.activation(w_parts[n], psum16[:, n % 2, :], ACT.Copy)\
                        .then_inc(s["w_tr_out"], 1)

            def front_ln(r):
                act.wait_ge(s["ln1_nm"], r.b + 1)
                wait(act, "qtr", 2 * r.b)
                hold(act)
                for c in range(NC):
                    last = nc.scalar.activation(q_nat[:, c, :], row_of(xh, r, c), ACT.Identity,
                                                scale=rs1[:, c:c + 1], bias=nm1[:, c:c + 1])
                last.then_inc(s["ln1_out"], 1)

            def front_k(r, k):
                wait(act, "scores", NC * (r.b - 1))
                act.wait_ge(s["ktr"], 2 * r.b + k + 1)
                nc.scalar.activation(kT[r.par][:, k, :], psum[:, T0 + k, :], ACT.Copy)\
                    .then_inc(s["k_out"], 1)

            def front_q(r, k):
                wait(act, "inter_ps", 3 * (r.b - 1))
                wait(act, "scores", NC * (r.b - 1))
                act.wait_ge(s["qtr"], 2 * r.b + k + 1)
                nc.scalar.activation(qT[r.par][:, k, :], psum[:, T0 + k, :], ACT.Copy)\
                    .then_inc(s["q_out"], 1)

            def front_ctx(r):
                act.wait_ge(ctx_in[r.par], 16 * (r.half + 1))
                wait(act, "intra", NC * (r.b - 1))
                nc.scalar.activation(ctx[r.par].rearrange("p c h v -> p (c h) v")[:, :, 0:DH],
                                     c_nat[r.par].rearrange("p c (h d) -> p (c h) d", d=DH), ACT.Copy)\
                    .then_inc(s["ctx_ready"], 1)

            def front_grow(r):
                act.wait_ge(s["gates_ps"], r.b + 1)
                wait(act, "gates_tr", r.b)
                nc.scalar.activation(g_row[0:2 * NH, :], psum[0:2 * NH, G, :], ACT.Copy)\
                    .then_inc(s["gates_row"], 1)

            def front_logf(r):
                act.wait_ge(s["nabs_ready"], r.b + 1)
                nc.scalar.activation(e_f, nabs, ACT.Exp).then_inc(s["logf_e"], 1)
                act.wait_ge(s["logf_e"], r.b + 1)
                wait(act, "logf_ready", r.b)
                nc.scalar.activation(l_f, e_f, ACT.Ln, bias=1.0).then_inc(s["logf_l"], 1)

            def front_exp(r):
                act.wait_ge(s["args_ready"], r.b + 1)
                wait(act, "num_ready", NC * (r.b - 1))
                wait(act, "kw_ready", 3 * (r.b - 1))
                wait(act, "norm_var", r.b - 1)
                nc.scalar.activation(wexp[r.par], args, ACT.Exp).then_inc(s["wexp_ready"], 1)

            def decay(r, c):
                if c == 0:
                    act.wait_ge(s["m_masked"], r.b + 1)
                wait(act, "prob_ready", 2 * (NC * (r.b - 1) + c + 1))
                for h in range(NH):
                    last = nc.scalar.activation(dec[c][:, h, :], m_bc[r.par][:, h, c * P:(c + 1) * P],
                                                ACT.Exp, scale=-1.0, bias=a_pad[r.par][:, c, h, 0:1])
                last.then_inc(s["dec_ready"], 1)

            def state_out(r, i):
                act.wait_ge(s["state_ps"], 3 * r.b + i)
                wait(act, "inter_ps", 3 * r.b + i - 1)
                for j in range(HP):
                    rows = slice(j * DH, (j + 1) * DH)
                    v = psum[rows, ST, 0:KH * HP * VA].rearrange("p (k j v) -> p k j v", k=KH, j=HP)
                    last = nc.scalar.activation(state[rows, :, j, :], v[:, :, j, :], ACT.Copy,
                                                scale=DH ** -0.5)
                last.then_inc(s["state_sb"], 1)

            def back_heads(r, c):
                if c == 0:
                    act.wait_ge(s["norm_ready"], r.b + 1)
                    wait(act, "x2tr", 2 * r.b)
                    wait(act, "x2_max", r.b)
                for h in range(NH):
                    last = nc.scalar.activation(cen[:, c, h * DH:(h + 1) * DH], num[r.par][:, c, h, 0:DH],
                                                ACT.Identity, scale=gg[:, c, h:h + 1],
                                                bias=gm[:, c, h:h + 1])
                if c == NC - 1:
                    last.then_inc(s["heads_out"], 1)

            def back_ln(r):
                act.wait_ge(s["ln2_nm"], r.b + 1)
                hold(act)
                for c in range(NC):
                    last = nc.scalar.activation(x2[:, c, :], row_of(xh, r, c), ACT.Identity,
                                                scale=rs2[:, c:c + 1], bias=nm2[:, c:c + 1])
                last.then_inc(s["ln2_out"], 1)

            def back_x2(r, k):
                wait(act, "x2tr", 2 * r.b + k + 1)
                hold(act)
                nc.scalar.activation(x2T[:, k, ds(r.b * S, S)], psum[:, T0 + k, :], ACT.Copy)\
                    .then_inc(s["x2_out"], 1)

            def step(n, f, m, b):
                if f:
                    front_k(f, 0)
                    front_k(f, 1)
                    front_q(f, 0)
                if m:
                    state_out(m, 1)
                    decay(m, 0)
                if f:
                    front_ctx(f)
                if m:
                    decay(m, 1)
                if f:
                    front_q(f, 1)
                if b:
                    back_heads(b, 0)
                    back_heads(b, 1)
                if f:
                    front_grow(f)
                if b:
                    back_heads(b, 2)
                if f:
                    front_logf(f)
                if b:
                    back_heads(b, 3)
                if m:
                    decay(m, 2)
                    state_out(m, 2)
                if n:
                    front_ln(n)
                if m:
                    decay(m, 3)
                    state_out(m, 3)
                if b:
                    back_ln(b)
                    back_x2(b, 0)
                    back_x2(b, 1)
                if f:
                    front_exp(f)
                if not f and not m and not n:
                    weights_out()

            steps(act, step)

            def evacuate(tb, t, mm, done):
                act.wait_ge(s[mm], 3 * tb + t + 1)
                hold(act)
                nc.scalar.activation(gu[:, tb, t * TW:(t + 1) * TW],
                                     psum[:, 2 * t:2 * t + 2, :].rearrange("p a b -> p (a b)"),
                                     ACT.Copy).then_inc(s[done], 1)

            with act.Fori(0, B) as tb:
                for t in range(3):
                    evacuate(tb, t, "mm_gate", "gate_out")
            act.preload_act_table_set("sigmoid_and_others")

            act.wait_ge(s["top_q"], 1)
            nc.scalar.activation(col(17), top16, ACT.Sigmoid, scale=col(16)).then_inc(s["top_sig"], 1)

            act.wait_ge(s["flag_ready"], 1)
            with act.If(act.value_load(flag[0:1, 0:1]) > 0):
                with act.Fori(0, B) as tb:
                    for t in range(3):
                        act.wait_ge(s["all_q"], 3 * tb + t + 1)
                        hold(act)
                        nc.scalar.activation(sig[0], gq[:, tb, t * TW:(t + 1) * TW], ACT.Sigmoid,
                                             scale=col(16)).then_inc(s["all_sig"], 1)

            act.wait_ge(s["gate_scale"], 1)
            act.sem_inc(s["sq_ready"], 2)
            with act.Fori(0, B // 2) as i:
                for p in range(2):
                    tb = 2 * i + p
                    nc.scalar.activation(gq[:, tb, :], gu[:, tb, :], ACT.Copy, scale=col(15))\
                        .then_inc(s["gq_ready"], 1)
                    act.wait_ge(s["gq_ready"], tb + 1)
                    for t in range(3):
                        n = 3 * tb + t
                        evacuate(tb, t, "mm_up", "up_out")
                        act.wait_ge(s["sq_ready"], n + 1)
                        hold(act)
                        nc.scalar.activation(sig[(3 * p + t) % 2], gq[:, tb, t * TW:(t + 1) * TW],
                                             ACT.Sigmoid, scale=col(16)).then_inc(s["sig_ready"], 1)
            act.wait_ge(s["up_scale"], 1)
            act.sem_inc(s["o_ready"], 2)
            with act.Fori(0, B // 2) as i:
                for p in range(2):
                    tb = 2 * i + p
                    act.wait_ge(s["o_ready"], tb + 1)
                    hold(act)
                    nc.scalar.activation(uq[:, p, :], gu[:, tb, :], ACT.Copy, scale=col(35))\
                        .then_inc(s["uq_ready"], 1)
            act.wait_ge(s["o_scale"], 1)
            act.sem_inc(s["o_split"], 2)
            with act.Fori(0, B // 2) as i:
                for p in range(2):
                    b = 2 * i + p
                    act.wait_ge(s["o_split"], b + 1)
                    hold(act)
                    nc.scalar.activation(o16[:, p, :], gu[:, b, :], ACT.Copy, scale=col(45))\
                        .then_inc(s["o_int"], 1)

        @block.tensor
        def _(pe):
            pe.wait_ge(s["const_ready"], 2)
            pe.wait_ge(s["gates_in"], 32)
            for k in range(3 * KH):
                last = nc.tensor.transpose(psum[:, G, k * 2 * NH:(k + 1) * 2 * NH],
                                           w8[0:2 * NH, k * P:(k + 1) * P], ident[0:2 * NH, 0:2 * NH])
            last.then_inc(s["gw_tr"], 1)
            def turn_weights():
                pe.wait_ge(s["w_split"], 1)
                n = 0
                for w in range(3):
                    nk, nt = (KH, FT) if w < 2 else (FT, KH)
                    width = H if w < 2 else FF
                    for part in (w_hi, w_lo):
                        for k in range(nk):
                            for t in range(nt):
                                if n % 8 == 0 and n >= 16:
                                    pe.wait_ge(s["w_tr_out"], n // 8 - 1)
                                at_t = w * FT * H + t * width + k * P
                                last = nc.tensor.transpose(psum16[:, (n // 8) % 2, (n % 8) * P:(n % 8 + 1) * P],
                                                           part[:, at_t:at_t + P], ident16)
                                n += 1
                                if n % 8 == 0:
                                    last.then_inc(s["w_tr"], 1)

            def front_k(r, k):
                pe.wait_ge(ctx_in[r.par], 16 * (r.half + 1))
                wait(pe, "q_out", 2 * r.b)
                wait(pe, "x2_out", 2 * (r.b - 2))
                for c in range(NC):
                    last = nc.tensor.transpose(psum[:, T0 + k, c * P:(c + 1) * P],
                                               c_nat[r.par][:, c, k * P:(k + 1) * P], ident)
                last.then_inc(s["ktr"], 1)

            def front_q(r, k):
                pe.wait_ge(s["ln1_out"], r.b + 1)
                pe.wait_ge(s["k_out"], 2 * r.b + k + 1)
                for c in range(NC):
                    last = nc.tensor.transpose(psum[:, T0 + k, c * P:(c + 1) * P],
                                               q_nat[:, c, k * P:(k + 1) * P], ident)
                last.then_inc(s["qtr"], 1)

            def front_kgates(r):
                pe.wait_ge(s["gw_ready"], 1)
                pe.wait_ge(s["k_out"], 2 * (r.b + 1))
                wait(pe, "args_ready", r.b)
                for k in range(KH):
                    nc.tensor.matmul(psum[0:2 * NH, G, :], wgkv[:, k, :], kT[r.par][:, k, :],
                                     start=k == 0, stop=False)

            def front_qgates(r):
                for k in range(KH):
                    pe.wait_ge(s["q_out"], 2 * r.b + k + 1)
                    last = nc.tensor.matmul(psum[0:2 * NH, G, :], wgq[:, k, :], qT[r.par][:, k, :],
                                            start=False, stop=k == KH - 1)
                last.then_inc(s["gates_ps"], 1)

            def front_gtr(r):
                pe.wait_ge(s["gates_row"], r.b + 1)
                hold(pe)
                for c in range(NC):
                    last = nc.tensor.transpose(psum[:, G, c * 2 * NH:(c + 1) * 2 * NH],
                                               g_row[0:2 * NH, c * P:(c + 1) * P], ident[0:2 * NH, 0:2 * NH])
                last.then_inc(s["gates_tr"], 1)

            def front_fsum(r):
                pe.wait_ge(s["logf_ready"], r.b + 1)
                to = psum[:, G, 0:NC * NH].rearrange("p (c h) -> p c h", h=NH)
                nc.tensor.matmul(to, tri, logf, start=True, stop=False)
                for c in range(NC - 1):
                    last = nc.tensor.matmul(to[:, c + 1:NC, :], ones,
                                            logf[:, c:c + 1, :].to_broadcast([P, NC - 1 - c, NH]),
                                            start=False, stop=c == NC - 2)
                last.then_inc(s["fsum_ps"], 1)

            def front_atr(r):
                pe.wait_ge(s["a_ready"], r.b + 1)
                for c in range(NC):
                    last = nc.tensor.transpose(psum[:, G, c * P:(c + 1) * P],
                                               a_pad[r.par][:, c, :, :].rearrange("p h z -> p (h z)"), ident)
                last.then_inc(s["a_tr"], 1)

            def front_mnat(r):
                pe.wait_ge(s["m_scan"], r.b + 1)
                for c in range(NC):
                    last = nc.tensor.matmul(psum[:, G, c * NH:(c + 1) * NH], m_row[:, c * P:(c + 1) * P],
                                            hsel, start=True, stop=True)
                last.then_inc(s["m_nat"], 1)

            def scores(r, c):
                if c == 0:
                    pe.wait_ge(s["q_out"], 2 * (r.b + 1))
                wait(pe, "prob_ready", 2 * (NC * r.b + c))
                at_c = slice(c * P, (c + 1) * P)
                for k in range(KH):
                    for j in range(HP):
                        rows = slice(j * DH, (j + 1) * DH)
                        last = nc.tensor.matmul(psum[:, SE + j, k * P:(k + 1) * P], kT[r.par][rows, k, at_c],
                                                qT[r.par][rows, k, at_c], start=True, stop=True)
                last.then_inc(s["scores"], 1)

            def intra(r, c):
                pe.wait_ge(s["ctx_ready"], r.b + 1)
                pe.wait_ge(s["prob_ready"], 2 * (NC * r.b + c + 1))
                wait(pe, "num_ready", NC * r.b + c)
                for h in range(NH):
                    last = nc.tensor.matmul(psum[:, OB, h * VA:(h + 1) * VA], prob[c % 2][:, h, :],
                                            ctx[r.par][:, c, h, :], start=True, stop=True)
                last.then_inc(s["intra"], 1)

            def states(r, i):
                pe.wait_ge(s["ctx_ready"], r.b + 1)
                pe.wait_ge(s["kw_ready"], 3 * r.b + i)
                wait(pe, "state_sb", 3 * r.b + i - 1)
                for k in range(KH):
                    for c in range(i):
                        heads = slice(k * HP, (k + 1) * HP)
                        last = nc.tensor.matmul(psum[:, ST, k * HP * VA:(k + 1) * HP * VA],
                                                kw[:, c, heads, :].rearrange("p h d -> p (h d)"),
                                                ctx[r.par][:, c, heads, :].rearrange("p h d -> p (h d)"),
                                                start=c == 0, stop=c == i - 1)
                last.then_inc(s["state_ps"], 1)

            def inter_(r, c):
                pe.wait_ge(s["state_sb"], 3 * r.b + c)
                wait(pe, "num_ready", NC * r.b + c)
                for k in range(KH):
                    last = nc.tensor.matmul(psum[:, IB, k * HP * VA:(k + 1) * HP * VA],
                                            qT[r.par][:, k, c * P:(c + 1) * P],
                                            state[:, k, :, :].rearrange("p h d -> p (h d)"),
                                            start=True, stop=True)
                last.then_inc(s["inter_ps"], 1)

            def back_x2(r, k):
                pe.wait_ge(s["ln2_out"], r.b + 1)
                for c in range(NC):
                    last = nc.tensor.transpose(psum[:, T0 + k, c * P:(c + 1) * P],
                                               x2[:, c, k * P:(k + 1) * P], ident)
                last.then_inc(s["x2tr"], 1)

            def step(n, f, m, b):
                if m:
                    scores(m, 0)
                if f:
                    front_k(f, 0)
                    front_k(f, 1)
                    front_q(f, 0)
                if m:
                    states(m, 1)
                if f:
                    front_q(f, 1)
                    front_kgates(f)
                if m:
                    scores(m, 1)
                    intra(m, 0)
                if f:
                    front_qgates(f)
                if m:
                    states(m, 2)
                if f:
                    front_gtr(f)
                if m:
                    inter_(m, 1)
                    intra(m, 1)
                if f:
                    front_fsum(f)
                if m:
                    scores(m, 2)
                if f:
                    front_atr(f)
                if m:
                    inter_(m, 2)
                    intra(m, 2)
                    states(m, 3)
                    scores(m, 3)
                if f:
                    front_mnat(f)
                if m:
                    inter_(m, 3)
                    intra(m, 3)
                if b:
                    back_x2(b, 0)
                    back_x2(b, 1)
                if not f and not m and not n:
                    turn_weights()

            steps(pe, step)

            PASSES = ((0, 0), (0, 1), (1, 0))

            def project(tb, wT, mm, out_done, before):
                for t in range(3):
                    pe.wait_ge(s[out_done], 3 * tb + t + 1 + before)
                    for m in (2 * t, 2 * t + 1):
                        n = 0
                        for wp, xp in PASSES:
                            for k in range(KH):
                                last = nc.tensor.matmul(psum[:, m, :], wT[:, wp, k, m * P:(m + 1) * P],
                                                        xs[:, xp, k, ds(tb * S, S)],
                                                        start=n == 0, stop=n == 3 * KH - 1)
                                n += 1
                    last.then_inc(s[mm], 1)

            wait(pe, "x2_out", 2 * B)
            pe.wait_ge(s["w_tr_out"], 9)
            pe.sem_inc(s["gate_out"], 3)
            with pe.Fori(0, B) as tb:
                pe.wait_ge(s["xs_ready"], tb + 1)
                project(tb, wgT, "mm_gate", "gate_out", 0)
            pe.wait_ge(s["gate_out"], 3 * B + 3)
            pe.sem_inc(s["up_out"], 3)
            with pe.Fori(0, B) as tb:
                project(tb, wuT, "mm_up", "up_out", 0)
            pe.wait_ge(s["up_out"], 3 * B + 3)
            pe.sem_inc(s["down_out"], 4)

            with pe.Fori(0, B // 2) as i:
                for p in range(2):
                    b = 2 * i + p
                    pe.wait_ge(s["o_split"], b + 1 + 2)
                    for half in range(2):
                        pe.wait_ge(s["down_out"], 2 * b + half + 1)
                        for c in (2 * half, 2 * half + 1):
                            n = 0
                            for op, wp in ((0, 0), (0, 1), (1, 0)):
                                for t in range(FT):
                                    last = nc.tensor.matmul(
                                        psum[:, 2 * p + half, (c % 2) * H:(c % 2 + 1) * H],
                                        os_[:, 2 * p + op, t * S + c * P:t * S + (c + 1) * P],
                                        wdT[:, wp, t, :], start=n == 0, stop=n == 3 * FT - 1)
                                    n += 1
                        last.then_inc(s["mm_down"], 1)

        @block.vector
        def _(dve):
            V = nc.vector
            cw = Chain(dve, "chain_w")
            dve.wait_ge(s["gw_tr"], 1)
            cw.link(V.tensor_copy(w8T.rearrange("p a b -> p (a b)"), psum[:, G, 0:3 * KH * 2 * NH]))
            cw.link(V.tensor_copy(wgq, w8T[:, 0:KH, :]))
            V.tensor_tensor(wgkv, w8T[:, KH:2 * KH, :], w8T[:, 2 * KH:3 * KH, :], ALU.add)\
                .then_inc(s["gw_ready"], 1)
            def prepare_weights():
                dve.wait_ge(s["w_in"], 48)
                wv = w_nat.rearrange("p (n e) -> p n e", e=WBLOCK)
                cw.link(V.tensor_reduce(bmax, wv, AX, ALU.max, apply_absolute_value=True))
                cw.link(V.tensor_scalar(bmax, bmax, 1.0 / WQMAX, MIN_SCALE, ALU.mult, ALU.max))
                cw.link(V.reciprocal(binv, bmax))
                V.tensor_tensor(w_int.rearrange("p (n e) -> p n e", e=WBLOCK), wv,
                                binv.unsqueeze(2).to_broadcast([P, WB, WBLOCK]), ALU.mult)
                n1 = FT * H // WBLOCK
                cw.link(V.tensor_reduce(tmx[:, 0:3], bmax.rearrange("p (w n) -> p w n", n=n1), AX, ALU.max))
                V.tensor_scalar(tmx[:, 0:3], tmx[:, 0:3], WQMAX, None, ALU.mult).then_inc(s["w_max_ready"], 1)
                cw.link(V.tensor_tensor(wv, w_int.rearrange("p (n e) -> p n e", e=WBLOCK),
                                        bmax.unsqueeze(2).to_broadcast([P, WB, WBLOCK]), ALU.mult))

            def split_weights():
                dve.wait_ge(s["w_max_all"], 1)
                cw.link(V.tensor_scalar(pw2[:, 0:3].bitcast(I32), pw2[:, 0:3].bitcast(I32), 0x7F800000, None,
                                        ALU.bitwise_and))
                cw.link(V.tensor_scalar(pw2[:, 0:3], pw2[:, 0:3], 2.0 ** -100, None, ALU.max))
                cw.link(V.reciprocal(amp[:, 0:3], pw2[:, 0:3]))
                cw.link(V.tensor_scalar(amp[:, 0:3], amp[:, 0:3], 2.0 ** 14, None, ALU.mult))
                for w in range(3):
                    cols = slice(w * FT * H, (w + 1) * FT * H)
                    last = V.tensor_scalar(w_hi[:, cols], w_nat[:, cols], amp[:, w:w + 1], None, ALU.mult)
                cw.link(last)
                for w in range(3):
                    cols = slice(w * FT * H, (w + 1) * FT * H)
                    last = V.scalar_tensor_tensor(w_lo[:, cols], w_nat[:, cols], amp[:, w:w + 1], w_hi[:, cols],
                                                  ALU.mult, ALU.subtract)
                last.then_inc(s["w_split"], 1)


            def front_stats(r, ch):
                if isinstance(r.b, int) and r.b < 2:
                    dve.wait_ge(x_in[r.par], 16)
                else:
                    dve.wait_ge(s["x_rest"], 16)
                for c in range(NC):
                    last = V.bn_stats(st1[:, c, :], row_of(xh, r, c))
                ch.link(last)
                wait(dve, "ln1_out", r.b)
                hold(dve)
                for c in range(NC):
                    last = V.bn_aggr(mv1[:, c, :], st1[:, c, :])
                ch.link(last)
                V.tensor_scalar(v1, mv1[:, :, 1], LN_EPS, None, ALU.add).then_inc(s["ln1_var"], 1)

            def front_nm(r):
                dve.wait_ge(s["ln1_rstd"], r.b + 1)
                V.scalar_tensor_tensor(nm1, mv1[:, :, 0], -1.0, rs1, ALU.mult, ALU.mult)\
                    .then_inc(s["ln1_nm"], 1)

            def front_gates(r):
                dve.wait_ge(s["gates_tr"], r.b + 1)
                dve.wait_ge(s["bias_in"], 16 * 2 * NC)
                V.tensor_tensor(gsb, psum[:, G, 0:NC * 2 * NH].rearrange("p (c g) -> p c g", g=2 * NH),
                                bias8, ALU.add)\
                    .then_inc(s["gates_sb"], 1)
                dve.wait_ge(s["gates_sb"], r.b + 1)
                f = gsb[:, :, NH:2 * NH]
                V.scalar_tensor_tensor(nabs, f, -1.0, f, ALU.mult, ALU.min)\
                    .then_inc(s["nabs_ready"], 1)

            def front_logf(r):
                dve.wait_ge(s["logf_l"], r.b + 1)
                V.scalar_tensor_tensor(logf, gsb[:, :, NH:2 * NH], 0.0, l_f, ALU.min, ALU.subtract)\
                    .then_inc(s["logf_ready"], 1)

            def front_a(r):
                dve.wait_ge(s["fsum_ps"], r.b + 1)
                wait(dve, "dec_ready", NC * (r.b - 1))
                fsum = psum[:, G, 0:NC * NH].rearrange("p (c h) -> p c h", h=NH)
                V.tensor_copy(f_sb, fsum)
                V.tensor_tensor(a_pad[r.par][:, :, :, 0], gsb[:, :, 0:NH], fsum, ALU.subtract)\
                    .then_inc(s["a_ready"], 1)

            def front_scan(r):
                dve.wait_ge(s["a_tr"], r.b + 1)
                wait(dve, "m_bcast", r.b)
                V.tensor_tensor_scan(m_row, psum[:, G, :], zeros[:, 0:1].to_broadcast([P, S]), -3.0e38, ALU.max, ALU.add)\
                    .then_inc(s["m_scan"], 1)

            def front_args(r):
                dve.wait_ge(s["m_nat"], r.b + 1)
                dve.wait_ge(s["m_masked"], r.b + 1)
                wait(dve, "wexp_ready", r.b)
                a = a_pad[r.par][:, :, :, 0]
                mn = psum[:, G, 0:NC * NH].rearrange("p (c h) -> p c h", h=NH)
                ends = m_bc[r.par].rearrange("p h (c t) -> p c h t", t=P)[:, :, :, P - 1]
                for i in range(1, NC):
                    V.tensor_tensor(args[:, W_AT[i]:W_AT[i] + i * NH].rearrange("p (c h) -> p c h", h=NH),
                                    a[:, 0:i, :], ends[:, i - 1:i, :].to_broadcast([P, i, NH]), ALU.subtract)
                V.tensor_tensor(args[:, E_AT:N_AT].rearrange("p (c h) -> p c h", h=NH),
                                ends[:, 0:NC - 1, :], mn[:, 1:NC, :], ALU.subtract)
                V.scalar_tensor_tensor(args[:, N_AT:ARGS].rearrange("p (c h) -> p c h", h=NH),
                                       mn, -1.0, f_sb, ALU.mult, ALU.subtract).then_inc(s["args_ready"], 1)

            def probs(r, c):
                dve.wait_ge(s["scores"], NC * r.b + c + 1)
                dve.wait_ge(s["dec_ready"], NC * r.b + c + 1)
                wait(dve, "intra", NC * r.b + c - 1)
                for j in range(HP):
                    V.scalar_tensor_tensor(prob[c % 2].rearrange("p (k j) t -> p j k t", j=HP)[:, j],
                                           psum[:, SE + j, 0:KH * P].rearrange("p (k t) -> p k t", t=P),
                                           DH ** -0.5,
                                           dec[c].rearrange("p (k j) t -> p j k t", j=HP)[:, j],
                                           ALU.mult, ALU.mult).then_inc(s["prob_ready"], 1)

            def weigh_keys(r, i):
                if i == 1:
                    dve.wait_ge(s["wexp_ready"], r.b + 1)
                    dve.wait_ge(ctx_in[r.par], 16 * (r.half + 1))
                wait(dve, "state_ps", 3 * r.b + i - 1)
                w = wexp[r.par][:, W_AT[i]:W_AT[i] + i * NH].rearrange("p (n o) -> p n o", o=1)
                V.tensor_tensor(kw.rearrange("p c h d -> p (c h) d")[:, 0:i * NH, :],
                                c_nat[r.par].rearrange("p c (h d) -> p (c h) d", d=DH)[:, 0:i * NH, :],
                                w.to_broadcast([P, i * NH, DH]), ALU.mult).then_inc(s["kw_ready"], 1)

            def numerators(r, c, ch):
                dve.wait_ge(s["intra"], NC * r.b + c + 1)
                if c == 0:
                    wait(dve, "heads_out", r.b - 1)
                o = psum[:, OB, 0:NH * VA].rearrange("p (h v) -> p h v", v=VA)
                if c == 0:
                    V.tensor_copy(num[r.par][:, c], o).then_inc(s["num_ready"], 1)
                else:
                    dve.wait_ge(s["inter_ps"], 3 * r.b + c)
                    e = wexp[r.par][:, E_AT + (c - 1) * NH:E_AT + c * NH].unsqueeze(2)
                    ch.link(V.tensor_tensor(inter, psum[:, IB, 0:NH * VA].rearrange("p (h v) -> p h v", v=VA),
                                            e.to_broadcast([P, NH, VA]), ALU.mult))
                    V.tensor_tensor(num[r.par][:, c], o, inter, ALU.add).then_inc(s["num_ready"], 1)
                dve.wait_ge(s["num_ready"], NC * r.b + c + 1)
                for h in range(NH):
                    last = V.bn_stats(nstat[r.par][:, c, h, :], num[r.par][:, c, h, 0:DH])
                ch.link(last)

            def normalise(r, ch):
                dve.wait_ge(s["wexp_ready"], r.b + 1)
                enm = wexp[r.par][:, N_AT:ARGS].rearrange("p (c h) -> p c h", h=NH)
                me, mo = nstat[r.par][:, :, :, 1], nstat[r.par][:, :, :, 4]
                V.scalar_tensor_tensor(t1, num[r.par][:, :, :, DH], -1.0, num[r.par][:, :, :, DH], ALU.mult, ALU.max)
                V.tensor_tensor(t2, me, mo, ALU.add)
                ch.link(V.tensor_tensor(t3, me, mo, ALU.subtract))
                V.tensor_tensor(t1, t1, enm, ALU.max)
                V.tensor_tensor(t4, nstat[r.par][:, :, :, 2], nstat[r.par][:, :, :, 5], ALU.add)
                ch.link(V.tensor_tensor(t3, t3, t3, ALU.mult))
                V.tensor_scalar(t1, t1, NORM_EPS, None, ALU.add)
                V.tensor_scalar(t2, t2, 0.5, None, ALU.mult)
                ch.link(V.tensor_scalar(t4, t4, 4.0 / DH, None, ALU.mult))
                V.reciprocal(rr, t1)
                ch.link(V.tensor_tensor(t4, t4, t3, ALU.add))
                ch.link(V.tensor_tensor(t3, rr, rr, ALU.mult))
                ch.link(V.scalar_tensor_tensor(t4, t4, 0.25, t3, ALU.mult, ALU.mult))
                V.tensor_scalar(t5, t4, LN_EPS, None, ALU.add).then_inc(s["norm_var"], 1)

            def norm_factors(r, ch):
                dve.wait_ge(s["norm_rstd"], r.b + 1)
                wait(dve, "heads_out", r.b)
                ch.link(V.tensor_tensor(gg, rr, t6, ALU.mult))
                V.scalar_tensor_tensor(gm, t2, -1.0, gg, ALU.mult, ALU.mult).then_inc(s["norm_ready"], 1)

            def residual(r, ch):
                dve.wait_ge(s["scaled_ready"], r.b + 1)
                row = xh[:, ds(r.b, 1)].rearrange("p o c h -> p (o c) h")
                V.tensor_tensor(row, cen, row, ALU.add).then_inc(s["h_ready"], 1)
                dve.wait_ge(s["h_ready"], r.b + 1)
                hold(dve)
                for c in range(NC):
                    last = V.bn_stats(st2[:, c, :], row_of(xh, r, c))
                ch.link(last)
                hold(dve)
                for c in range(NC):
                    last = V.bn_aggr(mv2[:, c, :], st2[:, c, :])
                ch.link(last)
                V.tensor_scalar(v2, mv2[:, :, 1], LN_EPS, None, ALU.add).then_inc(s["ln2_var"], 1)

            def back_nm(r):
                dve.wait_ge(s["ln2_rstd"], r.b + 1)
                V.scalar_tensor_tensor(nm2, mv2[:, :, 0], -1.0, rs2, ALU.mult, ALU.mult)\
                    .then_inc(s["ln2_nm"], 1)

            def largest(r):
                dve.wait_ge(s["ln2_out"], r.b + 1)
                V.tensor_reduce(xmax[:, ds(r.b, 1)], x2.rearrange("p c h -> p (c h)"), AX, ALU.max,
                                apply_absolute_value=True).then_inc(s["x2_max"], 1)

            NA, NB, NCB = 2, NC - 1 + NC, 9

            def step(n, f, m, b):
                ca = Chain(dve, "chain_a", NA * n.b) if n else None
                cb = Chain(dve, "chain_b", NB * m.b) if m else None
                cc = Chain(dve, "chain_c", NCB * b.b) if b else None
                if m:
                    weigh_keys(m, 1)
                if b:
                    normalise(b, cc)
                if m:
                    probs(m, 0)
                    weigh_keys(m, 2)
                if b:
                    norm_factors(b, cc)
                if n:
                    front_stats(n, ca)
                if m:
                    probs(m, 1)
                    numerators(m, 0, cb)
                if n:
                    front_nm(n)
                if f:
                    front_gates(f)
                if m:
                    weigh_keys(m, 3)
                if f:
                    front_logf(f)
                if m:
                    numerators(m, 1, cb)
                if f:
                    front_a(f)
                if m:
                    probs(m, 2)
                if f:
                    front_scan(f)
                if b:
                    residual(b, cc)
                if m:
                    numerators(m, 2, cb)
                if b:
                    back_nm(b)
                if m:
                    probs(m, 3)
                if f and not m:
                    prepare_weights()
                if f:
                    front_args(f)
                if f and not m:
                    split_weights()
                if m:
                    numerators(m, 3, cb)
                if b:
                    largest(b)
                assert not n or ca.n == NA, ca.n
                assert not m or cb.n == NB, cb.n
                assert not b or cc.n == NCB, cc.n

            steps(dve, step)

            cf = Chain(dve, "chain_f")

            wait(dve, "x2_max", B)
            V.tensor_reduce(col(0), xmax, AX, ALU.max).then_inc(s["xmax_row"], 1)
            dve.wait_ge(s["xmax_all"], 1)
            cf.link(V.tensor_scalar(col(2), col(1), 1.0 / QMAX, MIN_SCALE, ALU.mult, ALU.max))
            cf.link(V.reciprocal(col(3), col(2)))
            cf.link(V.reciprocal(amp[:, 0:3], amp[:, 0:3]))
            V.tensor_tensor(col(14), col(2), amp[:, 0:1], ALU.mult)
            cf.link(V.tensor_tensor(col(34), col(2), amp[:, 1:2], ALU.mult))

            wait(dve, "h_stored", 16 * B)
            wait(dve, "x2_out", KH * B)
            with dve.Fori(0, B // 2) as i:
                blocks = [(2 * i + p, ds((2 * i + p) * S, S)) for p in range(2)]
                for p, (tb, at_b) in enumerate(blocks):
                    V.tensor_scalar(x16[:, p], x2T[:, :, at_b], col(3), QMAX, ALU.mult, ALU.min)\
                        .then_inc(s["x16_ready"], 1)
                for p, (tb, at_b) in enumerate(blocks):
                    dve.wait_ge(s["x16_ready"], tb + 1)
                    V.tensor_copy(xs[:, 0, :, at_b], x16[:, p]).then_inc(s["xhi_ready"], 1)
                for p, (tb, at_b) in enumerate(blocks):
                    dve.wait_ge(s["xhi_ready"], tb + 1)
                    V.tensor_tensor(xs[:, 1, :, at_b], x16[:, p], xs[:, 0, :, at_b], ALU.subtract)\
                        .then_inc(s["xs_ready"], 1)
                dve.wait_ge(s["xs_ready"], 2 * i + 2)

            with dve.Fori(0, B) as tb:
                dve.wait_ge(s["gate_out"], 3 * tb + 3 + 3)
                hold(dve)
                V.tensor_reduce(gmax[:, 0, ds(tb, 1)], gu[:, tb, :], AX, ALU.max)
                V.tensor_reduce(gmax[:, 1, ds(tb, 1)], gu[:, tb, :], AX, ALU.min).then_inc(s["gate_max"], 1)
            dve.wait_ge(s["gate_max"], B)
            V.tensor_reduce(col(10), gmax[:, 0, :], AX, ALU.max)
            cf.link(V.tensor_reduce(col(9), gmax[:, 1, :], AX, ALU.min))
            V.tensor_scalar(col(11), col(9), -1.0, None, ALU.mult).then_inc(s["gmax_row"], 1)
            dve.wait_ge(s["gmax_all"], 1)
            cf.link(V.tensor_tensor(col(18), col(12), col(13), ALU.max))
            cf.link(V.tensor_tensor(col(19), col(18), col(14), ALU.mult))
            cf.link(V.tensor_scalar(col(16), col(19), 1.0 / QMAX, MIN_SCALE, ALU.mult, ALU.max))
            V.tensor_scalar(col(24), col(16), 1.0 / 65536.0, None, ALU.mult)
            cf.link(V.reciprocal(col(20), col(16)))
            cf.link(V.tensor_tensor(col(15), col(20), col(14), ALU.mult))
            V.tensor_scalar(top16, col(12), col(15), QMAX, ALU.mult, ALU.min).then_inc(s["top_q"], 1)
            dve.wait_ge(s["top_sig"], 1)
            cf.link(V.tensor_scalar(topsq, col(17), 65536.0, 65535.0, ALU.mult, ALU.min))
            cf.link(V.tensor_tensor(col(23), top16, topsq, ALU.mult))
            V.tensor_scalar(flag[:, 0:1], col(23), col(24), NEGATIVE_TOP, ALU.mult, ALU.is_lt)\
                .then_inc(s["flag_ready"], 1)
            dve.wait_ge(s["flag_ready"], 1)
            with dve.If(dve.value_load(flag[0:1, 0:1]) > 0):
                with dve.Fori(0, B) as tb:
                    for t in range(3):
                        n = 3 * tb + t
                        g = gq[:, tb, t * TW:(t + 1) * TW]
                        V.tensor_scalar(g, gu[:, tb, t * TW:(t + 1) * TW], col(15), QMAX, ALU.mult, ALU.min)\
                            .then_inc(s["all_q"], 1)
                        dve.wait_ge(s["all_sig"], n + 1)
                        V.tensor_scalar(sq[0], sig[0], 65536.0, 65535.0, ALU.mult, ALU.min)\
                            .then_inc(s["all_sq"], 1)
                        dve.wait_ge(s["all_sq"], n + 1)
                        V.tensor_tensor(sig[0], g, sq[0], ALU.mult).then_inc(s["all_p"], 1)
                        dve.wait_ge(s["all_p"], n + 1)
                        V.tensor_reduce(pmax[:, ds(n, 1)], sig[0], AX, ALU.max,
                                        apply_absolute_value=True).then_inc(s["all_max"], 1)
                        dve.wait_ge(s["all_max"], n + 1)
                V.tensor_reduce(col(22), pmax, AX, ALU.max).then_inc(s["pmax_row"], 1)
                dve.wait_ge(s["pmax_all"], 1)
            dve.sem_inc(s["gate_scale"], 1)
            cf.link(V.tensor_tensor(col(25), col(23), col(24), ALU.mult))
            cf.link(V.tensor_scalar(col(26), col(25), 1.0 / QMAX, MIN_SCALE, ALU.mult, ALU.max))
            cf.link(V.reciprocal(col(27), col(26)))
            cf.link(V.tensor_tensor(col(28), col(27), col(24), ALU.mult))

            with dve.Fori(0, B // 2) as i:
                for j in range(6):
                    tb, t, n = 2 * i + j // 3, j % 3, 6 * i + j
                    g = gq[:, tb, t * TW:(t + 1) * TW]
                    dve.wait_ge(s["sig_ready"], n + 1)
                    V.tensor_scalar(sq[j % 2], sig[j % 2], 65536.0, 65535.0, ALU.mult, ALU.min)\
                        .then_inc(s["sq_ready"], 1)
                    dve.wait_ge(s["up_out"], n + 1 + 3)
                    hold(dve)
                    V.tensor_reduce(umax[:, ds(n, 1)], gu[:, tb, t * TW:(t + 1) * TW], AX, ALU.max,
                                    apply_absolute_value=True).then_inc(s["up_max"], 1)
                    dve.wait_ge(s["sq_ready"], n + 1 + 2)
                    V.scalar_tensor_tensor(g, g, col(28), sq[j % 2], ALU.mult, ALU.mult)\
                        .then_inc(s["p_ready"], 1)
                    if j > 0:
                        dve.wait_ge(s["p_ready"], n + (j == 5))
            dve.wait_ge(s["up_max"], 3 * B)
            V.tensor_reduce(col(30), umax, AX, ALU.max).then_inc(s["umax_row"], 1)
            dve.wait_ge(s["umax_all"], 1)
            cf.link(V.tensor_tensor(col(36), col(31), col(34), ALU.mult))
            cf.link(V.tensor_scalar(col(33), col(36), 1.0 / QMAX, MIN_SCALE, ALU.mult, ALU.max))
            cf.link(V.reciprocal(col(37), col(33)))
            V.tensor_tensor(col(35), col(37), col(34), ALU.mult).then_inc(s["up_scale"], 1)
            cf.link(V.tensor_tensor(col(44), col(33), col(26), ALU.mult))
            dve.wait_ge(s["p_ready"], 3 * B)

            with dve.Fori(0, B // 2) as i:
                for p in range(2):
                    tb = 2 * i + p
                    dve.wait_ge(s["uq_ready"], tb + 1)
                    V.tensor_tensor(gu[:, tb, :], gq[:, tb, :], uq[:, p, :], ALU.mult)\
                        .then_inc(s["o_ready"], 1)
                    dve.wait_ge(s["o_ready"], tb + 1 + 2)
                    hold(dve)
                    V.tensor_reduce(omax[:, ds(tb, 1)], gu[:, tb, :], AX, ALU.max,
                                    apply_absolute_value=True).then_inc(s["o_max"], 1)
            dve.wait_ge(s["o_max"], B)
            V.tensor_reduce(col(40), omax, AX, ALU.max).then_inc(s["omax_row"], 1)
            dve.wait_ge(s["omax_all"], 1)
            cf.link(V.tensor_tensor(col(47), col(41), col(44), ALU.mult))
            cf.link(V.tensor_scalar(col(42), col(47), 1.0 / QMAX, MIN_SCALE, ALU.mult, ALU.max))
            cf.link(V.reciprocal(col(43), col(42)))
            V.tensor_tensor(col(45), col(43), col(44), ALU.mult).then_inc(s["o_scale"], 1)
            cf.link(V.tensor_tensor(col(48), col(42), amp[:, 2:3], ALU.mult))

            def split(b, p):
                dve.wait_ge(s["o_int"], b + 1)
                V.tensor_copy(os_[:, 2 * p, :], o16[:, p, :]).then_inc(s["o_hi"], 1)
                dve.wait_ge(s["o_hi"], b + 1)
                V.tensor_tensor(os_[:, 2 * p + 1, :], o16[:, p, :], os_[:, 2 * p, :],
                                ALU.subtract).then_inc(s["o_split"], 1)

            def result(i, p):
                dve.wait_ge(h_back[p], 16 * (i + 1))
                dve.wait_ge(y_stored[p], 16 * (i + 1))
                for half in range(2):
                    dve.wait_ge(s["mm_down"], 2 * (2 * i + p) + half + 1)
                    cols = slice(2 * half, 2 * half + 2)
                    V.scalar_tensor_tensor(y_buf[p][:, cols, :].rearrange("p c h -> p (c h)"),
                                           psum[:, 2 * p + half, :], col(48),
                                           h_back_buf[p][:, cols, :].rearrange("p c h -> p (c h)"),
                                           ALU.mult, ALU.add).then_inc(s["down_out"], 1)

            split(0, 0)
            split(1, 1)
            with dve.Fori(0, B // 2 - 1) as i:
                for p in range(2):
                    result(i, p)
                    split(2 * i + p + 2, p)
            for p in range(2):
                result(B // 2 - 1, p)


_INS = ["x", "ctx_1024", "L0_xattn_w_igate", "L0_xattn_b_igate", "L0_xattn_w_fgate", "L0_xattn_b_fgate",
        "L0_xattn_ln_weight", "L0_ffn_w_gate", "L0_ffn_w_up", "L0_ffn_w_down"]


def kernel(**inputs):
    import numpy as _np
    import concourse.bacc as _bacc
    from concourse import mybir as _mybir
    from concourse.bass_utils import run_bass_kernel_spmd as _run

    nc = _bacc.Bacc("TRN2", target_bir_lowering=False, num_devices=1)
    arrays, args = {}, []
    for name in _INS:
        a = _np.ascontiguousarray(inputs[name])
        arrays[f"in_{name}"] = a
        args.append(nc.dram_tensor(f"in_{name}", a.shape, _mybir.dt.from_np(a.dtype), kind="ExternalInput").ap())
    shape = inputs["x"].shape
    y = nc.dram_tensor("out_y", shape, _mybir.dt.float32, kind="ExternalOutput").ap()
    attention_ffn(nc, *args, y)
    r = _run(nc, [arrays], core_ids=[0])
    return r.results[0]["out_y"]
```

```python
import concourse.bass as bass
from concourse import mybir
from contextlib import ExitStack


def attention_ffn(nc, x, ctx_1024, w_igate, b_igate, w_fgate, b_fgate, ln_weight,
                  w_gate, w_up, w_down, out):
    F32, F16 = mybir.dt.float32, mybir.dt.float16
    I16, U16, I32 = mybir.dt.int16, mybir.dt.uint16, mybir.dt.int32
    ALU, ACT, AX = mybir.AluOpType, mybir.ActivationFunctionType, mybir.AxisListType.X
    RMAX = bass.bass_isa.ReduceOp.max
    ds = bass.ds

    P = 128
    B, S, H = x.shape
    NH = w_igate.shape[0]
    DH = H // NH
    NC = S // P
    KH = H // P
    HP = NH // KH
    FF = w_gate.shape[0]
    FT = FF // P
    BW = FT * S
    VA = DH + 1
    QMAX = 32767.0
    WBLOCK, WQMAX = 32, 7.0
    LN_EPS, NORM_EPS, MIN_SCALE = 1e-5, 1e-6, 1e-12
    NEGATIVE_TOP = 0.279

    W_AT = {1: 0, 2: NH, 3: 3 * NH}
    E_AT = 6 * NH
    N_AT = 9 * NH
    ARGS = 13 * NH

    h_dram = nc.dram_tensor("h_rows", [B, S, H], F32, kind="Internal").ap()

    with ExitStack() as stack:
        def sem(name):
            return stack.enter_context(nc.semaphore(name))

        ARENA = 53200
        arena = stack.enter_context(nc.sbuf_tensor("arena", [P, ARENA], F32))

        def view(at, *dims, dt=F32):
            n = 1
            for d in dims:
                n *= d
            words = n if dt in (F32, I32) else n // 2
            assert at + words <= ARENA, (at, words)
            v = arena[:, at:at + words]
            if dt is not F32:
                v = v.bitcast(dt)
            if len(dims) == 2:
                v = v.rearrange("p (a b) -> p a b", b=dims[1])
            if len(dims) == 3:
                v = v.rearrange("p (a b c) -> p a b c", b=dims[1], c=dims[2])
            if len(dims) == 4:
                v = v.rearrange("p (a b c d) -> p a b c d", b=dims[1], c=dims[2], d=dims[3])
            return v

        class Space:
            def __init__(self, at, end):
                self.at, self.end = at, end

            def take(self, *dims, dt=F32):
                n = 1
                for d in dims:
                    n *= d
                v = view(self.at, *dims, dt=dt)
                self.at += (n if dt in (F32, I32) else n // 2)
                self.at += self.at % 2
                assert self.at <= self.end, (self.at, self.end)
                return v

        HALF = BW // 2
        GU_AT, GQ_AT = 0, B * BW
        XS_AT = GQ_AT + B * HALF
        KEEP_AT = XS_AT + KH * B * S
        gu = view(GU_AT, B, BW)
        gq = view(GQ_AT, B, BW, dt=I16)
        x2T = view(GQ_AT, KH, B * S)
        xs = view(XS_AT, 2, KH, B * S, dt=F16)
        keep = Space(KEEP_AT, ARENA)
        wgT = keep.take(2, KH, FF, dt=F16)
        wuT = keep.take(2, KH, FF, dt=F16)
        wdT = keep.take(2, FT, H, dt=F16)
        xmax = keep.take(B)
        sc = keep.take(64)
        flag = keep.take(2, dt=I32)
        top16 = keep.take(2, dt=I16)[:, 0:1]
        topsq = keep.take(2, dt=U16)[:, 0:1]
        gmax = keep.take(2, 3 * B)
        umax = keep.take(3 * B)
        pmax = keep.take(3 * B)
        omax = keep.take(2, B)
        TW = BW // 3
        SIG_AT = keep.at
        sig = [keep.take(TW) for _ in range(2)]
        sq = [keep.take(TW, dt=U16) for _ in range(2)]
        x16 = view(GU_AT + (B - 1) * BW, 2, KH, S, dt=I16)
        uq = view(XS_AT, 2, BW, dt=I16)
        os_ = view(XS_AT, 4, BW, dt=F16)
        o16 = view(GQ_AT, 2, BW, dt=I16)
        h_back_buf = [view(GQ_AT + BW + p * NC * H, NC, H) for p in range(2)]
        y_buf = [view(GQ_AT + BW + (2 + p) * NC * H, NC, H) for p in range(2)]
        xh = view(XS_AT, B, NC, H)
        at = Space(0, GQ_AT)
        c_nat = [at.take(NC, H) for _ in range(2)]
        ctx = [at.take(NC, NH, VA) for _ in range(2)]
        q_nat = at.take(NC, H)
        qT = [at.take(KH, S) for _ in range(2)]
        kT = [at.take(KH, S) for _ in range(2)]
        gsb = at.take(NC, 2 * NH)
        nabs = at.take(NC, NH)
        e_f = at.take(NC, NH)
        l_f = at.take(NC, NH)
        logf = at.take(NC, NH)
        f_sb = at.take(NC, NH)
        a_pad = [at.take(NC, NH, P // NH) for _ in range(2)]
        m_row = at.take(S)
        g_row = at.take(S)
        m_bc = [at.take(NH, S) for _ in range(2)]
        args = at.take(ARGS)
        ends = at.take(NC, NH)
        wexp = [at.take(ARGS) for _ in range(2)]
        dec = [at.take(NH, P) for _ in range(NC)]
        prob = [at.take(NH, P) for _ in range(2)]
        kw = at.take(3, NH, DH)
        state = at.take(KH, HP, VA)
        inter = at.take(NH, VA)
        num = [at.take(NC, NH, VA) for _ in range(2)]
        nstat = [at.take(NC, NH, 6) for _ in range(2)]
        cen = at.take(NC, H)
        x2 = cen
        st1, mv1, rs1, nm1, v1 = at.take(NC, 6), at.take(NC, 2), at.take(NC), at.take(NC), at.take(NC)
        st2, mv2, rs2, nm2, v2 = at.take(NC, 6), at.take(NC, 2), at.take(NC), at.take(NC), at.take(NC)
        t1, t2, t3, t4, t5, t6 = (at.take(NC, NH) for _ in range(6))
        rr, gg, gm = at.take(NC, NH), at.take(NC, NH), at.take(NC, NH)
        mhalf = at.take(NC * NH)
        ident = at.take(P)
        tri = at.take(P)
        ones = at.take(P)
        zeros = at.take(2)
        hsel = at.take(NH)
        misc = Space(GQ_AT + KH * B * S, XS_AT)
        w8 = misc.take(3 * H)
        w8T = misc.take(3 * KH, 2 * NH)
        wgq = misc.take(KH, 2 * NH)
        wgkv = misc.take(KH, 2 * NH)
        bias8 = misc.take(2 * NH)
        lnw = misc.take(H)
        ident16 = misc.take(P, dt=F16)
        WN = 2 * FT * H + KH * FF
        WB = WN // WBLOCK
        prep = Space(GQ_AT, GQ_AT + KH * B * S)
        w_nat = prep.take(WN)
        assert WN // 2 <= 3 * TW
        w_lo = view(SIG_AT, WN, dt=F16)
        w_int = misc.take(WN, dt=I16)
        bmax = prep.take(WB)
        binv = prep.take(WB)
        w_hi = w_int.bitcast(F16)
        tmx = keep.take(4)
        pw2 = keep.take(4)
        amp = keep.take(4)

        psum = stack.enter_context(nc.psum_tensor("psum", [P, 8, 512], F32))
        T0, T1, G, SE, SO, OB, IB, ST = range(8)

        psum16 = psum[:, SE:SE + 2, :].bitcast(F16)
        wflat = [w.rearrange("p a b c -> p (a b c)") for w in (wgT, wuT, wdT)]
        w_parts = [wflat[n // 3][:, (n % 3) * 1024:(n % 3 + 1) * 1024] for n in range(9)]

        def col(n):
            return sc[:, n:n + 1]

        names = ("const_ready gates_in bias_in w_in lnw_in "
                 "w_max_ready w_max_all w_bits w_values w_amp w_high w_split w_tr w_tr_out "
                 "gw_tr gw_ready "
                 "ln1_stats ln1_var ln1_rstd ln1_nm ln1_out ktr k_out qtr q_out gates_ps gates_row gates_tr gates_sb "
                 "nabs_ready logf_e logf_l logf_ready fsum_ps a_ready a_tr m_scan m_bcast "
                 "ends_ready m_masked m_nat args_ready wexp_ready "
                 "scores dec_ready prob_ready intra kw_ready state_ps state_sb inter_ps num_ready "
                 "norm_var norm_rstd norm_ready heads_out scaled_ready h_ready ln2_var ln2_rstd ln2_nm ln2_out "
                 "x2tr x2_out x2_max "
                 "xmax_row xmax_all x16_ready xhi_ready xs_ready mm_gate gate_out gate_max "
                 "gmax_row gmax_all gate_scale top_q top_sig flag_ready "
                 "all_q all_sig all_sq all_p all_max pmax_row pmax_all "
                 "gq_ready sig_ready sq_ready p_ready mm_up up_out up_max umax_row umax_all up_scale "
                 "uq_ready o_first o_ready o_max omax_row omax_all o_scale o_int o_hi o_split mm_down down_out "
                 "lnw_ready ctx_ready held "
                 "chain_w chain_a chain_b chain_c chain_f "
                 "h_stored x_rest")
        s = {n: sem(n) for n in names.split()}
        x_in = [sem(f"x_in{p}") for p in range(2)]
        ctx_in = [sem(f"ctx_in{p}") for p in range(2)]
        START = {"x2tr": 2, "x2_max": 1, "heads_out": 1, "x2_out": 2}
        h_back = [sem(f"h_back{p}") for p in range(2)]
        y_stored = [sem(f"y_stored{p}") for p in range(2)]

        def wait(eng, sm, value):
            if isinstance(value, int) and value <= 0:
                return
            if isinstance(sm, str):
                eng.wait_ge(s[sm], value + START.get(sm, 0))
            else:
                eng.wait_ge(sm, value)

        def hold(eng):
            eng.sem_inc(s["held"], 1)

        def row_of(t, r, c):
            return t[:, ds(r.b, 1), c, :].rearrange("p o h -> p (o h)")

        class Chain:
            def __init__(self, eng, name, base=0):
                self.eng, self.name, self.base, self.n = eng, name, base, 0

            def mark(self, ins):
                self.n += 1
                ins.then_inc(s[self.name], 1)

            def wait(self):
                self.eng.wait_ge(s[self.name], self.base + self.n)

            def link(self, ins):
                self.mark(ins)
                self.wait()

        class Row:
            def __init__(self, half, par):
                self.b, self.half, self.par = 2 * half + par, half, par

        def steps(eng, step):
            last = B // 2 - 1
            step(Row(0, 0), None, None, None)
            step(Row(0, 1), Row(0, 0), None, None)
            step(Row(1, 0), Row(0, 1), Row(0, 0), None)
            with eng.Fori(0, B // 2 - 2) as i:
                step(Row(i + 1, 1), Row(i + 1, 0), Row(i, 1), Row(i, 0))
                step(Row(i + 2, 0), Row(i + 1, 1), Row(i + 1, 0), Row(i, 1))
            step(Row(last, 1), Row(last, 0), Row(last - 1, 1), Row(last - 1, 0))
            step(None, Row(last, 1), Row(last, 0), Row(last - 1, 1))
            step(None, None, Row(last, 1), Row(last, 0))
            step(None, None, None, Row(last, 1))

        block = stack.enter_context(nc.Block())

        @block.sync
        def _(sp):
            for name, n in START.items():
                sp.sem_inc(s[name], n)

            def load_x(first, n, done):
                sp.dma_start(xh[:, first:first + n].rearrange("p b c h -> p (b c) h"),
                             x[first:first + n].rearrange("b (c p) h -> p (b c) h", p=P)).then_inc(done, 16)

            def load_ctx(r):
                sp.dma_start(c_nat[r.par], ctx_1024[ds(r.b, 1)].rearrange("o (c p) h -> p (o c) h", p=P))\
                    .then_inc(ctx_in[r.par], 16)

            sp.dma_start(w8[0:NH, :], w_igate).then_inc(s["gates_in"], 16)
            sp.dma_start(w8[NH:2 * NH, :], w_fgate).then_inc(s["gates_in"], 16)
            load_x(0, 1, x_in[0])
            load_ctx(Row(0, 0))
            sp.dma_start(bias8[:, 0:NH], b_igate.rearrange("(o n) -> o n", o=1).to_broadcast([P, NH]))\
                .then_inc(s["bias_in"], 16)
            sp.dma_start(bias8[:, NH:2 * NH], b_fgate.rearrange("(o n) -> o n", o=1).to_broadcast([P, NH]))\
                .then_inc(s["bias_in"], 16)
            sp.dma_start(lnw, ln_weight.rearrange("(o n) -> o n", o=1).to_broadcast([P, H])).then_inc(s["lnw_in"], 16)
            load_x(1, 1, x_in[1])
            load_ctx(Row(0, 1))
            w3 = w_nat.rearrange("p (t c) -> p t c", c=H)
            sp.dma_start(w3[:, 0:FT, :], w_gate.rearrange("(t p) c -> p t c", p=P)).then_inc(s["w_in"], 16)
            sp.dma_start(w3[:, FT:2 * FT, :], w_up.rearrange("(t p) c -> p t c", p=P)).then_inc(s["w_in"], 16)
            sp.dma_start(w_nat[:, 2 * FT * H:WN].rearrange("p (t c) -> p t c", c=FF),
                         w_down.rearrange("(t p) c -> p t c", p=P)).then_inc(s["w_in"], 16)
            load_x(2, B - 2, s["x_rest"])

            def reload(r, half):
                wait(sp, "ktr", 2 * (r.b + 1))
                hold(sp)
                wait(sp, "ctx_ready", r.b + 1)
                hold(sp)
                load_ctx(Row(half, r.par))

            def store_h(r):
                wait(sp, "h_ready", r.b + 1)
                hold(sp)
                sp.dma_start(h_dram[ds(r.b, 1)].rearrange("o (c p) h -> p (o c) h", p=P),
                             xh[:, ds(r.b, 1)].rearrange("p o c h -> p (o c) h")).then_inc(s["h_stored"], 16)

            reload(Row(0, 0), 1)
            with sp.Fori(0, B // 2 - 2) as i:
                reload(Row(i, 1), i + 1)
                store_h(Row(i, 0))
                reload(Row(i + 1, 0), i + 2)
                store_h(Row(i, 1))
            last = B // 2 - 2
            reload(Row(last, 1), last + 1)
            for half in (last, last + 1):
                for p in range(2):
                    store_h(Row(half, p))
            wait(sp, "h_stored", 16 * B)

            def fetch(b, p):
                sp.dma_start(h_back_buf[p], h_dram[ds(b, 1)].rearrange("o (c p) h -> p (o c) h", p=P))\
                    .then_inc(h_back[p], 16)

            def store_y(b, p):
                sp.wait_ge(s["down_out"], 2 * (b + 1) + 4)
                hold(sp)
                sp.dma_start(out[ds(b, 1)].rearrange("o (c p) h -> p (o c) h", p=P), y_buf[p])\
                    .then_inc(y_stored[p], 16)

            for p in range(2):
                sp.sem_inc(y_stored[p], 16)
            sp.wait_ge(s["o_ready"], B + 2)
            for p in range(2):
                fetch(p, p)
            with sp.Fori(0, B // 2 - 1) as i:
                for p in range(2):
                    store_y(2 * i + p, p)
                    fetch(2 * i + p + 2, p)
            for p in range(2):
                store_y(B - 2 + p, p)
            for p in range(2):
                sp.wait_ge(y_stored[p], 16 * (B // 2) + 16)

        @block.gpsimd
        def _(pool):
            for t in (ident, tri, a_pad[0].rearrange("p a b c -> p (a b c)"),
                      a_pad[1].rearrange("p a b c -> p (a b c)"), zeros, hsel, ident16,
                      state.rearrange("p a b c -> p (a b c)")):
                pool.memset(t, 0.0)
            pool.memset(ones, 1.0)
            pool.memset(mhalf, -0.5)
            for p in range(2):
                pool.memset(ctx[p][:, :, :, DH:VA], 1.0)
            pool.drain().then_inc(s["const_ready"], 1)
            pool.wait_ge(s["const_ready"], 1)
            pool.affine_select(out=ident, in_=ident, compare_op=ALU.not_equal, fill=1.0, base=0,
                               pattern=[[-1, P]], channel_multiplier=1)
            pool.affine_select(out=ident16, in_=ident16, compare_op=ALU.not_equal, fill=1.0, base=0,
                               pattern=[[-1, P]], channel_multiplier=1)
            pool.affine_select(out=tri, in_=tri, compare_op=ALU.is_gt, fill=1.0, base=0,
                               pattern=[[-1, P]], channel_multiplier=1)
            pool.affine_select(out=hsel, in_=hsel, compare_op=ALU.not_equal, fill=1.0, base=0,
                               pattern=[[-(P // NH), NH]], channel_multiplier=1)
            pool.drain().then_inc(s["const_ready"], 1)

            def front(r):
                pool.wait_ge(s["ln1_var"], r.b + 1)
                wait(pool, "ln1_out", r.b)
                hold(pool)
                pool.tensor_tensor(out=rs1, in0=v1, in1=mhalf[:, 0:NC], op=ALU.pow)\
                    .then_inc(s["ln1_rstd"], 1)

            def front_bcast(r):
                pool.wait_ge(s["m_scan"], r.b + 1)
                wait(pool, "dec_ready", NC * (r.b - 1))
                hold(pool)
                for h in range(NH):
                    last = pool.partition_broadcast(m_bc[r.par][:, h, :],
                                                    m_row[h * (P // NH):h * (P // NH) + 1, :])
                last.then_inc(s["m_bcast"], 1)

            def front_mask(r):
                pool.wait_ge(s["m_bcast"], r.b + 1)
                hold(pool)
                pool.wait_ge(s["ends_ready"], r.b + 1)
                hold(pool)
                v = m_bc[r.par].rearrange("p h (c t) -> p (h c) t", t=P)
                pool.affine_select(out=v, in_=v, compare_op=ALU.is_ge, fill=1e30, base=0,
                                   pattern=[[0, NH * NC], [1, P]], channel_multiplier=-1)\
                    .then_inc(s["m_masked"], 1)

            def back_norm(r):
                pool.wait_ge(s["norm_var"], r.b + 1)
                hold(pool)
                pool.tensor_tensor(out=t6.rearrange("p a b -> p (a b)"),
                                   in0=t5.rearrange("p a b -> p (a b)"), in1=mhalf, op=ALU.pow)\
                    .then_inc(s["norm_rstd"], 1)

            def back_scale(r):
                pool.wait_ge(s["lnw_ready"], 1)
                pool.wait_ge(s["heads_out"], r.b + 1 + START["heads_out"])
                hold(pool)
                pool.tensor_tensor(out=cen, in0=cen, in1=lnw.unsqueeze(1).to_broadcast([P, NC, H]),
                                   op=ALU.mult).then_inc(s["scaled_ready"], 1)

            def back_rstd(r):
                pool.wait_ge(s["ln2_var"], r.b + 1)
                hold(pool)
                pool.tensor_tensor(out=rs2, in0=v2, in1=mhalf[:, 0:NC], op=ALU.pow)\
                    .then_inc(s["ln2_rstd"], 1)

            pool.wait_ge(s["lnw_in"], 16)
            pool.tensor_scalar(lnw, lnw, 1.0, None, ALU.add).then_inc(s["lnw_ready"], 1)

            def step(n, f, m, b):
                if b:
                    back_norm(b)
                if n:
                    front(n)
                if b:
                    back_scale(b)
                    back_rstd(b)
                    pool.wait_ge(s["ln2_rstd"], b.b + 1)
                    hold(pool)
                elif n:
                    pool.wait_ge(s["ln1_rstd"], n.b + 1)
                if f:
                    front_bcast(f)
                    front_mask(f)
                if f and not m:
                    pool.wait_ge(s["m_masked"], 1)
                    pool.wait_ge(s["w_max_ready"], 1)
                    pool.partition_all_reduce(pw2[:, 0:3], tmx[:, 0:3], P, RMAX).then_inc(s["w_max_all"], 1)
                    pool.wait_ge(s["w_max_all"], 1)

            steps(pool, step)

            def reduce_all(col, src, n, row, done, v=1):
                pool.wait_ge(s[row], v)
                pool.partition_all_reduce(sc[:, col:col + n], sc[:, src:src + n], P, RMAX)\
                    .then_inc(s[done], 1)

            reduce_all(1, 0, 1, "xmax_row", "xmax_all")
            reduce_all(12, 10, 2, "gmax_row", "gmax_all")
            pool.wait_ge(s["flag_ready"], 1)
            with pool.If(pool.value_load(flag[0:1, 0:1]) > 0):
                reduce_all(23, 22, 1, "pmax_row", "pmax_all")
            reduce_all(31, 30, 1, "umax_row", "umax_all")
            reduce_all(41, 40, 1, "omax_row", "omax_all")

        @block.scalar
        def _(act):
            act.preload_act_table_set("natural_log_exp_and_others")

            def weight_high():
                act.wait_ge(s["w_amp"], 1)
                act.wait_ge(s["w_values"], 3)
                for w in range(3):
                    cols = slice(w * FT * H, (w + 1) * FT * H)
                    nc.scalar.activation(w_hi[:, cols], w_nat[:, cols], ACT.Copy, scale=amp[:, w:w + 1])\
                        .then_inc(s["w_high"], 1)

            def weights_out(first, end):
                for n in range(first, end):
                    act.wait_ge(s["w_tr"], n + 1)
                    nc.scalar.activation(w_parts[n], psum16[:, n % 2, :], ACT.Copy)\
                        .then_inc(s["w_tr_out"], 1)

            def front_ln(r):
                act.wait_ge(s["ln1_nm"], r.b + 1)
                wait(act, "qtr", 2 * r.b)
                hold(act)
                for c in range(NC):
                    last = nc.scalar.activation(q_nat[:, c, :], row_of(xh, r, c), ACT.Identity,
                                                scale=rs1[:, c:c + 1], bias=nm1[:, c:c + 1])
                last.then_inc(s["ln1_out"], 1)

            def front_k(r, k):
                wait(act, "scores", NC * (r.b - 1))
                act.wait_ge(s["ktr"], 2 * r.b + k + 1)
                nc.scalar.activation(kT[r.par][:, k, :], psum[:, T0 + k, :], ACT.Copy)\
                    .then_inc(s["k_out"], 1)

            def front_q(r, k):
                wait(act, "inter_ps", 3 * (r.b - 1))
                wait(act, "scores", NC * (r.b - 1))
                act.wait_ge(s["qtr"], 2 * r.b + k + 1)
                nc.scalar.activation(qT[r.par][:, k, :], psum[:, T0 + k, :], ACT.Copy)\
                    .then_inc(s["q_out"], 1)

            def front_ctx(r):
                act.wait_ge(ctx_in[r.par], 16 * (r.half + 1))
                wait(act, "intra", NC * (r.b - 1))
                wait(act, "kw_ready", 3 * (r.b - 1))
                nc.scalar.activation(ctx[r.par].rearrange("p c h v -> p (c h) v")[:, :, 0:DH],
                                     c_nat[r.par].rearrange("p c (h d) -> p (c h) d", d=DH), ACT.Copy)\
                    .then_inc(s["ctx_ready"], 1)

            def front_grow(r):
                act.wait_ge(s["gates_ps"], r.b + 1)
                wait(act, "gates_tr", r.b)
                nc.scalar.activation(g_row[0:2 * NH, :], psum[0:2 * NH, G, :], ACT.Copy)\
                    .then_inc(s["gates_row"], 1)

            def front_logf(r):
                act.wait_ge(s["nabs_ready"], r.b + 1)
                nc.scalar.activation(e_f, nabs, ACT.Exp).then_inc(s["logf_e"], 1)
                act.wait_ge(s["logf_e"], r.b + 1)
                wait(act, "logf_ready", r.b)
                nc.scalar.activation(l_f, e_f, ACT.Ln, bias=1.0).then_inc(s["logf_l"], 1)

            def front_exp(r):
                act.wait_ge(s["args_ready"], r.b + 1)
                wait(act, "num_ready", NC * (r.b - 1))
                wait(act, "kw_ready", 3 * (r.b - 1))
                wait(act, "norm_var", r.b - 1)
                nc.scalar.activation(wexp[r.par], args, ACT.Exp).then_inc(s["wexp_ready"], 1)

            def decay(r, c):
                if c == 0:
                    act.wait_ge(s["m_masked"], r.b + 1)
                wait(act, "prob_ready", 2 * (NC * (r.b - 1) + c + 1))
                for h in range(NH):
                    last = nc.scalar.activation(dec[c][:, h, :], m_bc[r.par][:, h, c * P:(c + 1) * P],
                                                ACT.Exp, scale=-1.0, bias=a_pad[r.par][:, c, h, 0:1])
                last.then_inc(s["dec_ready"], 1)

            def state_out(r, i):
                act.wait_ge(s["state_ps"], 3 * r.b + i)
                wait(act, "inter_ps", 3 * r.b + i - 1)
                for j in range(HP):
                    rows = slice(j * DH, (j + 1) * DH)
                    v = psum[rows, ST, 0:KH * HP * VA].rearrange("p (k j v) -> p k j v", k=KH, j=HP)
                    last = nc.scalar.activation(state[rows, :, j, :], v[:, :, j, :], ACT.Copy,
                                                scale=DH ** -0.5)
                last.then_inc(s["state_sb"], 1)

            def back_heads(r, c):
                if c == 0:
                    act.wait_ge(s["norm_ready"], r.b + 1)
                    wait(act, "x2tr", 2 * r.b)
                    wait(act, "x2_max", r.b)
                for h in range(NH):
                    last = nc.scalar.activation(cen[:, c, h * DH:(h + 1) * DH], num[r.par][:, c, h, 0:DH],
                                                ACT.Identity, scale=gg[:, c, h:h + 1],
                                                bias=gm[:, c, h:h + 1])
                if c == NC - 1:
                    last.then_inc(s["heads_out"], 1)

            def back_ln(r):
                act.wait_ge(s["ln2_nm"], r.b + 1)
                hold(act)
                for c in range(NC):
                    last = nc.scalar.activation(x2[:, c, :], row_of(xh, r, c), ACT.Identity,
                                                scale=rs2[:, c:c + 1], bias=nm2[:, c:c + 1])
                last.then_inc(s["ln2_out"], 1)

            def back_x2(r, k):
                wait(act, "x2tr", 2 * r.b + k + 1)
                hold(act)
                nc.scalar.activation(x2T[:, k, ds(r.b * S, S)], psum[:, T0 + k, :], ACT.Copy)\
                    .then_inc(s["x2_out"], 1)

            def step(n, f, m, b):
                if m:
                    decay(m, 0)
                if f:
                    front_q(f, 0)
                if m:
                    decay(m, 1)
                    state_out(m, 1)
                if f:
                    front_q(f, 1)
                if b and not m:
                    weights_out(0, 4)
                if b:
                    back_heads(b, 0)
                    back_heads(b, 1)
                if f:
                    front_grow(f)
                if b:
                    back_heads(b, 2)
                    back_heads(b, 3)
                if m:
                    state_out(m, 2)
                if f:
                    front_logf(f)
                if m:
                    decay(m, 2)
                    decay(m, 3)
                    state_out(m, 3)
                if n:
                    front_k(n, 0)
                    front_k(n, 1)
                if f:
                    front_ctx(f)
                if b and not m:
                    weights_out(4, 9)
                if b:
                    back_ln(b)
                if n:
                    front_ln(n)
                if b:
                    back_x2(b, 0)
                if f:
                    front_exp(f)
                if b:
                    back_x2(b, 1)
                if f and not m:
                    weight_high()

            steps(act, step)

            def evacuate(tb, t, mm, done):
                act.wait_ge(s[mm], 3 * tb + t + 1)
                hold(act)
                nc.scalar.activation(gu[:, tb, t * TW:(t + 1) * TW],
                                     psum[:, 2 * t:2 * t + 2, :].rearrange("p a b -> p (a b)"),
                                     ACT.Copy).then_inc(s[done], 1)

            with act.Fori(0, B) as tb:
                for t in range(3):
                    evacuate(tb, t, "mm_gate", "gate_out")
            act.preload_act_table_set("sigmoid_and_others")

            act.wait_ge(s["top_q"], 1)
            nc.scalar.activation(col(17), top16, ACT.Sigmoid, scale=col(16)).then_inc(s["top_sig"], 1)

            act.wait_ge(s["flag_ready"], 1)
            with act.If(act.value_load(flag[0:1, 0:1]) > 0):
                with act.Fori(0, B) as tb:
                    for t in range(3):
                        act.wait_ge(s["all_q"], 3 * tb + t + 1)
                        hold(act)
                        nc.scalar.activation(sig[0], gq[:, tb, t * TW:(t + 1) * TW], ACT.Sigmoid,
                                             scale=col(16)).then_inc(s["all_sig"], 1)

            act.wait_ge(s["gate_scale"], 1)
            act.sem_inc(s["sq_ready"], 2)

            def gates16(tb):
                nc.scalar.activation(gq[:, tb, :], gu[:, tb, :], ACT.Copy, scale=col(15))\
                    .then_inc(s["gq_ready"], 1)

            def sigmoids(tb, p):
                for t in range(3):
                    n = 3 * tb + t
                    act.wait_ge(s["gq_ready"], tb + 1)
                    hold(act)
                    act.wait_ge(s["sq_ready"], n + 1)
                    hold(act)
                    nc.scalar.activation(sig[(3 * p + t) % 2], gq[:, tb, t * TW:(t + 1) * TW],
                                         ACT.Sigmoid, scale=col(16)).then_inc(s["sig_ready"], 1)
                    evacuate(tb, t, "mm_up", "up_out")

            with act.Fori(0, B // 2 - 1) as i:
                for p in range(2):
                    sigmoids(2 * i + p, p)
                    gates16(2 * i + p + 1)
            sigmoids(B - 2, 0)
            gates16(B - 1)
            sigmoids(B - 1, 1)
            act.wait_ge(s["up_scale"], 1)
            act.sem_inc(s["o_ready"], 2)
            with act.Fori(0, B // 2) as i:
                for p in range(2):
                    tb = 2 * i + p
                    act.wait_ge(s["o_ready"], tb + 1)
                    hold(act)
                    for h in range(2):
                        cols = slice(h * BW // 2, (h + 1) * BW // 2)
                        nc.scalar.activation(uq[:, p, cols], gu[:, tb, cols], ACT.Copy, scale=col(35))\
                            .then_inc(s["uq_ready"], 1)
            act.wait_ge(s["o_scale"], 1)
            act.sem_inc(s["o_split"], 2)
            with act.Fori(0, B // 2) as i:
                for p in range(2):
                    b = 2 * i + p
                    act.wait_ge(s["o_split"], b + 1)
                    hold(act)
                    nc.scalar.activation(o16[:, p, :], gu[:, b, :], ACT.Copy, scale=col(45))\
                        .then_inc(s["o_int"], 1)

        @block.tensor
        def _(pe):
            pe.wait_ge(s["const_ready"], 2)
            pe.wait_ge(s["gates_in"], 32)
            for k in range(3 * KH):
                last = nc.tensor.transpose(psum[:, G, k * 2 * NH:(k + 1) * 2 * NH],
                                           w8[0:2 * NH, k * P:(k + 1) * P], ident[0:2 * NH, 0:2 * NH])
            last.then_inc(s["gw_tr"], 1)
            def turn_weights():
                pe.wait_ge(s["w_split"], 3)
                n = 0
                for w in range(3):
                    nk, nt = (KH, FT) if w < 2 else (FT, KH)
                    width = H if w < 2 else FF
                    for part in (w_hi, w_lo):
                        for k in range(nk):
                            for t in range(nt):
                                if n % 8 == 0 and n >= 16:
                                    pe.wait_ge(s["w_tr_out"], n // 8 - 1)
                                at_t = w * FT * H + t * width + k * P
                                last = nc.tensor.transpose(psum16[:, (n // 8) % 2, (n % 8) * P:(n % 8 + 1) * P],
                                                           part[:, at_t:at_t + P], ident16)
                                n += 1
                                if n % 8 == 0:
                                    last.then_inc(s["w_tr"], 1)

            def front_k(r, k):
                pe.wait_ge(ctx_in[r.par], 16 * (r.half + 1))
                wait(pe, "q_out", 2 * r.b)
                wait(pe, "x2_out", 2 * (r.b - 3))
                for c in range(NC):
                    last = nc.tensor.transpose(psum[:, T0 + k, c * P:(c + 1) * P],
                                               c_nat[r.par][:, c, k * P:(k + 1) * P], ident)
                last.then_inc(s["ktr"], 1)

            def front_q(r, k):
                pe.wait_ge(s["ln1_out"], r.b + 1)
                pe.wait_ge(s["k_out"], 2 * r.b + k + 1)
                wait(pe, "x2_out", 2 * (r.b - 2))
                for c in range(NC):
                    last = nc.tensor.transpose(psum[:, T0 + k, c * P:(c + 1) * P],
                                               q_nat[:, c, k * P:(k + 1) * P], ident)
                last.then_inc(s["qtr"], 1)

            def front_kgates(r):
                pe.wait_ge(s["gw_ready"], 1)
                pe.wait_ge(s["k_out"], 2 * (r.b + 1))
                wait(pe, "args_ready", r.b)
                for k in range(KH):
                    nc.tensor.matmul(psum[0:2 * NH, G, :], wgkv[:, k, :], kT[r.par][:, k, :],
                                     start=k == 0, stop=False)

            def front_qgates(r):
                for k in range(KH):
                    pe.wait_ge(s["q_out"], 2 * r.b + k + 1)
                    last = nc.tensor.matmul(psum[0:2 * NH, G, :], wgq[:, k, :], qT[r.par][:, k, :],
                                            start=False, stop=k == KH - 1)
                last.then_inc(s["gates_ps"], 1)

            def front_gtr(r):
                pe.wait_ge(s["gates_row"], r.b + 1)
                hold(pe)
                for c in range(NC):
                    last = nc.tensor.transpose(psum[:, G, c * 2 * NH:(c + 1) * 2 * NH],
                                               g_row[0:2 * NH, c * P:(c + 1) * P], ident[0:2 * NH, 0:2 * NH])
                last.then_inc(s["gates_tr"], 1)

            def front_fsum(r):
                pe.wait_ge(s["logf_ready"], r.b + 1)
                to = psum[:, G, 0:NC * NH].rearrange("p (c h) -> p c h", h=NH)
                nc.tensor.matmul(to, tri, logf, start=True, stop=False)
                for c in range(NC - 1):
                    last = nc.tensor.matmul(to[:, c + 1:NC, :], ones,
                                            logf[:, c:c + 1, :].to_broadcast([P, NC - 1 - c, NH]),
                                            start=False, stop=c == NC - 2)
                last.then_inc(s["fsum_ps"], 1)

            def front_atr(r):
                pe.wait_ge(s["a_ready"], r.b + 1)
                for c in range(NC):
                    last = nc.tensor.transpose(psum[:, G, c * P:(c + 1) * P],
                                               a_pad[r.par][:, c, :, :].rearrange("p h z -> p (h z)"), ident)
                last.then_inc(s["a_tr"], 1)

            def front_mnat(r):
                pe.wait_ge(s["m_scan"], r.b + 1)
                for c in range(NC):
                    last = nc.tensor.matmul(psum[:, G, c * NH:(c + 1) * NH], m_row[:, c * P:(c + 1) * P],
                                            hsel, start=True, stop=True)
                last.then_inc(s["m_nat"], 1)

            def scores(r, c):
                if c == 0:
                    pe.wait_ge(s["q_out"], 2 * (r.b + 1))
                wait(pe, "prob_ready", 2 * (NC * r.b + c))
                at_c = slice(c * P, (c + 1) * P)
                for k in range(KH):
                    for j in range(HP):
                        rows = slice(j * DH, (j + 1) * DH)
                        last = nc.tensor.matmul(psum[:, SE + j, k * P:(k + 1) * P], kT[r.par][rows, k, at_c],
                                                qT[r.par][rows, k, at_c], start=True, stop=True)
                last.then_inc(s["scores"], 1)

            def intra(r, c):
                pe.wait_ge(s["ctx_ready"], r.b + 1)
                pe.wait_ge(s["prob_ready"], 2 * (NC * r.b + c + 1))
                wait(pe, "num_ready", NC * r.b + c)
                for h in range(NH):
                    last = nc.tensor.matmul(psum[:, OB, h * VA:(h + 1) * VA], prob[c % 2][:, h, :],
                                            ctx[r.par][:, c, h, :], start=True, stop=True)
                last.then_inc(s["intra"], 1)

            def states(r, i):
                pe.wait_ge(s["ctx_ready"], r.b + 1)
                pe.wait_ge(s["kw_ready"], 3 * r.b + i)
                wait(pe, "state_sb", 3 * r.b + i - 1)
                for k in range(KH):
                    for c in range(i):
                        heads = slice(k * HP, (k + 1) * HP)
                        last = nc.tensor.matmul(psum[:, ST, k * HP * VA:(k + 1) * HP * VA],
                                                kw[:, c, heads, :].rearrange("p h d -> p (h d)"),
                                                ctx[r.par][:, c, heads, :].rearrange("p h d -> p (h d)"),
                                                start=c == 0, stop=c == i - 1)
                last.then_inc(s["state_ps"], 1)

            def inter_(r, c):
                pe.wait_ge(s["state_sb"], 3 * r.b + c)
                wait(pe, "num_ready", NC * r.b + c)
                for k in range(KH):
                    last = nc.tensor.matmul(psum[:, IB, k * HP * VA:(k + 1) * HP * VA],
                                            qT[r.par][:, k, c * P:(c + 1) * P],
                                            state[:, k, :, :].rearrange("p h d -> p (h d)"),
                                            start=True, stop=True)
                last.then_inc(s["inter_ps"], 1)

            def back_x2(r, k):
                pe.wait_ge(s["ln2_out"], r.b + 1)
                on = r.b + 3
                if not (isinstance(on, int) and on >= B):
                    pe.wait_ge(s["k_out"], 2 * (on + 1))
                for c in range(NC):
                    last = nc.tensor.transpose(psum[:, T0 + k, c * P:(c + 1) * P],
                                               x2[:, c, k * P:(k + 1) * P], ident)
                last.then_inc(s["x2tr"], 1)

            def step(n, f, m, b):
                if m:
                    scores(m, 0)
                if f:
                    front_kgates(f)
                    front_q(f, 0)
                if m:
                    states(m, 1)
                if f:
                    front_q(f, 1)
                if m:
                    intra(m, 0)
                if f:
                    front_qgates(f)
                if m:
                    scores(m, 1)
                    states(m, 2)
                    inter_(m, 1)
                if f:
                    front_gtr(f)
                if m:
                    intra(m, 1)
                    scores(m, 2)
                if n:
                    front_k(n, 0)
                if m:
                    inter_(m, 2)
                if f:
                    front_fsum(f)
                if m:
                    states(m, 3)
                    intra(m, 2)
                if f:
                    front_atr(f)
                if m:
                    scores(m, 3)
                if n:
                    front_k(n, 1)
                if m:
                    inter_(m, 3)
                    intra(m, 3)
                if f:
                    front_mnat(f)
                if b and not m:
                    turn_weights()
                if b:
                    back_x2(b, 0)
                    back_x2(b, 1)

            steps(pe, step)

            PASSES = ((0, 0), (1, 0), (0, 1))

            def project(tb, wT, mm, out_done):
                for t in range(3):
                    pe.wait_ge(s[out_done], 3 * tb + t + 1)
                    for m in (2 * t, 2 * t + 1):
                        n = 0
                        for wp, xp in PASSES:
                            if xp == 1 and m == 0 and mm == "mm_gate":
                                pe.wait_ge(s["xs_ready"], tb + 1)
                            for k in range(KH):
                                last = nc.tensor.matmul(psum[:, m, :], wT[:, wp, k, m * P:(m + 1) * P],
                                                        xs[:, xp, k, ds(tb * S, S)],
                                                        start=n == 0, stop=n == 3 * KH - 1)
                                n += 1
                    last.then_inc(s[mm], 1)

            wait(pe, "x2_out", 2 * B)
            pe.wait_ge(s["w_tr_out"], 9)
            pe.sem_inc(s["gate_out"], 3)
            with pe.Fori(0, B) as tb:
                pe.wait_ge(s["xhi_ready"], tb + 1)
                project(tb, wgT, "mm_gate", "gate_out")
            pe.wait_ge(s["gate_out"], 3 * B + 3)
            pe.sem_inc(s["up_out"], 3)
            with pe.Fori(0, B) as tb:
                project(tb, wuT, "mm_up", "up_out")
            pe.wait_ge(s["up_out"], 3 * B + 3)
            pe.sem_inc(s["down_out"], 4)

            with pe.Fori(0, B // 2) as i:
                for p in range(2):
                    b = 2 * i + p
                    pe.wait_ge(s["o_hi"], b + 1)
                    for half in range(2):
                        pe.wait_ge(s["down_out"], 2 * b + half + 1)
                        for c in (2 * half, 2 * half + 1):
                            n = 0
                            for op, wp in ((0, 0), (0, 1), (1, 0)):
                                if op == 1 and c == 0:
                                    pe.wait_ge(s["o_split"], b + 1 + 2)
                                for t in range(FT):
                                    last = nc.tensor.matmul(
                                        psum[:, 2 * p + half, (c % 2) * H:(c % 2 + 1) * H],
                                        os_[:, 2 * p + op, t * S + c * P:t * S + (c + 1) * P],
                                        wdT[:, wp, t, :], start=n == 0, stop=n == 3 * FT - 1)
                                    n += 1
                        last.then_inc(s["mm_down"], 1)

        @block.vector
        def _(dve):
            V = nc.vector
            cw = Chain(dve, "chain_w")
            dve.wait_ge(s["gw_tr"], 1)
            cw.link(V.tensor_copy(w8T.rearrange("p a b -> p (a b)"), psum[:, G, 0:3 * KH * 2 * NH]))
            cw.link(V.tensor_copy(wgq, w8T[:, 0:KH, :]))
            V.tensor_tensor(wgkv, w8T[:, KH:2 * KH, :], w8T[:, 2 * KH:3 * KH, :], ALU.add)\
                .then_inc(s["gw_ready"], 1)
            n1 = FT * H // WBLOCK

            def blocks_of(w):
                return (slice(w * FT * H, (w + 1) * FT * H), slice(w * n1, (w + 1) * n1))

            def weight_scales():
                dve.wait_ge(s["w_in"], 48)
                wv = w_nat.rearrange("p (n e) -> p n e", e=WBLOCK)
                cw.link(V.tensor_reduce(bmax, wv, AX, ALU.max, apply_absolute_value=True))
                cw.link(V.tensor_scalar(bmax, bmax, 1.0 / WQMAX, MIN_SCALE, ALU.mult, ALU.max))
                V.reciprocal(binv, bmax)
                cw.link(V.tensor_reduce(tmx[:, 0:3], bmax.rearrange("p (w n) -> p w n", n=n1), AX, ALU.max))
                V.tensor_scalar(tmx[:, 0:3], tmx[:, 0:3], WQMAX, None, ALU.mult).then_inc(s["w_max_ready"], 1)

            def weight_bits(w):
                cols, blk = blocks_of(w)
                V.tensor_tensor(w_int[:, cols].rearrange("p (n e) -> p n e", e=WBLOCK),
                                w_nat[:, cols].rearrange("p (n e) -> p n e", e=WBLOCK),
                                binv[:, blk].unsqueeze(2).to_broadcast([P, n1, WBLOCK]), ALU.mult)\
                    .then_inc(s["w_bits"], 1)

            def weight_values(w):
                cols, blk = blocks_of(w)
                dve.wait_ge(s["w_bits"], w + 1)
                V.tensor_tensor(w_nat[:, cols].rearrange("p (n e) -> p n e", e=WBLOCK),
                                w_int[:, cols].rearrange("p (n e) -> p n e", e=WBLOCK),
                                bmax[:, blk].unsqueeze(2).to_broadcast([P, n1, WBLOCK]), ALU.mult)\
                    .then_inc(s["w_values"], 1)

            def weight_raise():
                dve.wait_ge(s["w_max_all"], 1)
                cw.link(V.tensor_scalar(pw2[:, 0:3].bitcast(I32), pw2[:, 0:3].bitcast(I32), 0x7F800000, None,
                                        ALU.bitwise_and))
                cw.link(V.tensor_scalar(pw2[:, 0:3], pw2[:, 0:3], 2.0 ** -100, None, ALU.max))
                cw.link(V.reciprocal(amp[:, 0:3], pw2[:, 0:3]))
                V.tensor_scalar(amp[:, 0:3], amp[:, 0:3], 2.0 ** 14, None, ALU.mult).then_inc(s["w_amp"], 1)

            def weight_low(w):
                cols, _ = blocks_of(w)
                dve.wait_ge(s["w_high"], w + 1)
                V.scalar_tensor_tensor(w_lo[:, cols], w_nat[:, cols], amp[:, w:w + 1], w_hi[:, cols],
                                       ALU.mult, ALU.subtract).then_inc(s["w_split"], 1)

            NB, NCB = NC - 1 + NC, 9

            def front_stats(r):
                if isinstance(r.b, int) and r.b < 2:
                    dve.wait_ge(x_in[r.par], 16)
                else:
                    dve.wait_ge(s["x_rest"], 16)
                for c in range(NC):
                    last = V.bn_stats(st1[:, c, :], row_of(xh, r, c))
                last.then_inc(s["ln1_stats"], 1)

            def front_var(r, ch):
                dve.wait_ge(s["ln1_stats"], r.b + 1)
                hold(dve)
                wait(dve, "ln1_out", r.b)
                hold(dve)
                for c in range(NC):
                    last = V.bn_aggr(mv1[:, c, :], st1[:, c, :])
                ch.link(last)
                V.tensor_scalar(v1, mv1[:, :, 1], LN_EPS, None, ALU.add).then_inc(s["ln1_var"], 1)

            def front_nm(r):
                dve.wait_ge(s["ln1_rstd"], r.b + 1)
                V.scalar_tensor_tensor(nm1, mv1[:, :, 0], -1.0, rs1, ALU.mult, ALU.mult)\
                    .then_inc(s["ln1_nm"], 1)

            def front_gates(r):
                dve.wait_ge(s["gates_tr"], r.b + 1)
                dve.wait_ge(s["bias_in"], 32)
                V.tensor_tensor(gsb, psum[:, G, 0:NC * 2 * NH].rearrange("p (c g) -> p c g", g=2 * NH),
                                bias8.unsqueeze(1).to_broadcast([P, NC, 2 * NH]), ALU.add)\
                    .then_inc(s["gates_sb"], 1)

            def front_nabs(r):
                dve.wait_ge(s["gates_sb"], r.b + 1)
                f = gsb[:, :, NH:2 * NH]
                V.scalar_tensor_tensor(nabs, f, -1.0, f, ALU.mult, ALU.min)\
                    .then_inc(s["nabs_ready"], 1)

            def front_logf(r):
                dve.wait_ge(s["logf_l"], r.b + 1)
                V.scalar_tensor_tensor(logf, gsb[:, :, NH:2 * NH], 0.0, l_f, ALU.min, ALU.subtract)\
                    .then_inc(s["logf_ready"], 1)

            def front_a(r):
                dve.wait_ge(s["fsum_ps"], r.b + 1)
                wait(dve, "dec_ready", NC * (r.b - 1))
                fsum = psum[:, G, 0:NC * NH].rearrange("p (c h) -> p c h", h=NH)
                V.tensor_copy(f_sb, fsum)
                V.tensor_tensor(a_pad[r.par][:, :, :, 0], gsb[:, :, 0:NH], fsum, ALU.subtract)\
                    .then_inc(s["a_ready"], 1)

            def front_scan(r):
                dve.wait_ge(s["a_tr"], r.b + 1)
                wait(dve, "m_bcast", r.b)
                V.tensor_tensor_scan(m_row, psum[:, G, :], zeros[:, 0:1].to_broadcast([P, S]), -3.0e38, ALU.max, ALU.add)\
                    .then_inc(s["m_scan"], 1)

            def front_ends(r):
                dve.wait_ge(s["m_bcast"], r.b + 1)
                V.tensor_copy(ends, m_bc[r.par].rearrange("p h (c t) -> p c h t", t=P)[:, :, :, P - 1])\
                    .then_inc(s["ends_ready"], 1)

            def front_args(r):
                dve.wait_ge(s["m_nat"], r.b + 1)
                dve.wait_ge(s["ends_ready"], r.b + 1)
                wait(dve, "wexp_ready", r.b)
                a = a_pad[r.par][:, :, :, 0]
                mn = psum[:, G, 0:NC * NH].rearrange("p (c h) -> p c h", h=NH)
                for i in range(1, NC):
                    V.tensor_tensor(args[:, W_AT[i]:W_AT[i] + i * NH].rearrange("p (c h) -> p c h", h=NH),
                                    a[:, 0:i, :], ends[:, i - 1:i, :].to_broadcast([P, i, NH]), ALU.subtract)
                V.tensor_tensor(args[:, E_AT:N_AT].rearrange("p (c h) -> p c h", h=NH),
                                ends[:, 0:NC - 1, :], mn[:, 1:NC, :], ALU.subtract)
                V.scalar_tensor_tensor(args[:, N_AT:ARGS].rearrange("p (c h) -> p c h", h=NH),
                                       mn, -1.0, f_sb, ALU.mult, ALU.subtract).then_inc(s["args_ready"], 1)

            def probs(r, c):
                dve.wait_ge(s["scores"], NC * r.b + c + 1)
                dve.wait_ge(s["dec_ready"], NC * r.b + c + 1)
                wait(dve, "intra", NC * r.b + c - 1)
                for j in range(HP):
                    V.scalar_tensor_tensor(prob[c % 2].rearrange("p (k j) t -> p j k t", j=HP)[:, j],
                                           psum[:, SE + j, 0:KH * P].rearrange("p (k t) -> p k t", t=P),
                                           DH ** -0.5,
                                           dec[c].rearrange("p (k j) t -> p j k t", j=HP)[:, j],
                                           ALU.mult, ALU.mult).then_inc(s["prob_ready"], 1)

            def weigh_keys(r, i):
                if i == 1:
                    dve.wait_ge(s["wexp_ready"], r.b + 1)
                    dve.wait_ge(s["ctx_ready"], r.b + 1)
                wait(dve, "state_ps", 3 * r.b + i - 1)
                w = wexp[r.par][:, W_AT[i]:W_AT[i] + i * NH].rearrange("p (n o) -> p n o", o=1)
                V.tensor_tensor(kw.rearrange("p c h d -> p (c h) d")[:, 0:i * NH, :],
                                ctx[r.par].rearrange("p c h v -> p (c h) v")[:, 0:i * NH, 0:DH],
                                w.to_broadcast([P, i * NH, DH]), ALU.mult).then_inc(s["kw_ready"], 1)

            def earlier_part(r, c, ch):
                dve.wait_ge(s["inter_ps"], 3 * r.b + c)
                e = wexp[r.par][:, E_AT + (c - 1) * NH:E_AT + c * NH].unsqueeze(2)
                ch.mark(V.tensor_tensor(inter, psum[:, IB, 0:NH * VA].rearrange("p (h v) -> p h v", v=VA),
                                        e.to_broadcast([P, NH, VA]), ALU.mult))

            def numerators(r, c, ch):
                dve.wait_ge(s["intra"], NC * r.b + c + 1)
                o = psum[:, OB, 0:NH * VA].rearrange("p (h v) -> p h v", v=VA)
                if c == 0:
                    wait(dve, "heads_out", r.b - 1)
                    V.tensor_copy(num[r.par][:, c], o).then_inc(s["num_ready"], 1)
                else:
                    ch.wait()
                    V.tensor_tensor(num[r.par][:, c], o, inter, ALU.add).then_inc(s["num_ready"], 1)

            def head_stats(r, c, ch):
                dve.wait_ge(s["num_ready"], NC * r.b + c + 1)
                for h in range(NH):
                    last = V.bn_stats(nstat[r.par][:, c, h, :], num[r.par][:, c, h, 0:DH])
                ch.mark(last)

            def normalise(r, ch):
                dve.wait_ge(s["wexp_ready"], r.b + 1)
                dve.wait_ge(s["chain_b"], NB * (r.b + 1))
                enm = wexp[r.par][:, N_AT:ARGS].rearrange("p (c h) -> p c h", h=NH)
                me, mo = nstat[r.par][:, :, :, 1], nstat[r.par][:, :, :, 4]
                V.scalar_tensor_tensor(t1, num[r.par][:, :, :, DH], -1.0, num[r.par][:, :, :, DH], ALU.mult, ALU.max)
                V.tensor_tensor(t2, me, mo, ALU.add)
                ch.link(V.tensor_tensor(t3, me, mo, ALU.subtract))
                V.tensor_tensor(t1, t1, enm, ALU.max)
                V.tensor_tensor(t4, nstat[r.par][:, :, :, 2], nstat[r.par][:, :, :, 5], ALU.add)
                ch.link(V.tensor_tensor(t3, t3, t3, ALU.mult))
                V.tensor_scalar(t1, t1, NORM_EPS, None, ALU.add)
                V.tensor_scalar(t2, t2, 0.5, None, ALU.mult)
                ch.link(V.tensor_scalar(t4, t4, 4.0 / DH, None, ALU.mult))
                V.reciprocal(rr, t1)
                ch.link(V.tensor_tensor(t4, t4, t3, ALU.add))
                ch.link(V.tensor_tensor(t3, rr, rr, ALU.mult))
                ch.link(V.scalar_tensor_tensor(t4, t4, 0.25, t3, ALU.mult, ALU.mult))
                V.tensor_scalar(t5, t4, LN_EPS, None, ALU.add).then_inc(s["norm_var"], 1)

            def norm_factors(r, ch):
                dve.wait_ge(s["norm_rstd"], r.b + 1)
                wait(dve, "heads_out", r.b)
                ch.link(V.tensor_tensor(gg, rr, t6, ALU.mult))
                V.scalar_tensor_tensor(gm, t2, -1.0, gg, ALU.mult, ALU.mult).then_inc(s["norm_ready"], 1)

            def residual(r):
                dve.wait_ge(s["scaled_ready"], r.b + 1)
                row = xh[:, ds(r.b, 1)].rearrange("p o c h -> p (o c) h")
                V.tensor_tensor(row, cen, row, ALU.add).then_inc(s["h_ready"], 1)

            def back_stats(r, ch):
                dve.wait_ge(s["h_ready"], r.b + 1)
                hold(dve)
                for c in range(NC):
                    last = V.bn_stats(st2[:, c, :], row_of(xh, r, c))
                ch.mark(last)

            def back_var(r, ch):
                ch.wait()
                hold(dve)
                for c in range(NC):
                    last = V.bn_aggr(mv2[:, c, :], st2[:, c, :])
                ch.link(last)
                V.tensor_scalar(v2, mv2[:, :, 1], LN_EPS, None, ALU.add).then_inc(s["ln2_var"], 1)

            def back_nm(r):
                dve.wait_ge(s["ln2_rstd"], r.b + 1)
                V.scalar_tensor_tensor(nm2, mv2[:, :, 0], -1.0, rs2, ALU.mult, ALU.mult)\
                    .then_inc(s["ln2_nm"], 1)

            def largest(r):
                dve.wait_ge(s["ln2_out"], r.b + 1)
                V.tensor_reduce(xmax[:, ds(r.b, 1)], x2.rearrange("p c h -> p (c h)"), AX, ALU.max,
                                apply_absolute_value=True).then_inc(s["x2_max"], 1)

            NA = 1

            def step(n, f, m, b):
                ca = Chain(dve, "chain_a", NA * n.b) if n else None
                cb = Chain(dve, "chain_b", NB * m.b) if m else None
                cc = Chain(dve, "chain_c", NCB * b.b) if b else None
                if b:
                    normalise(b, cc)
                if m:
                    weigh_keys(m, 1)
                    probs(m, 0)
                    weigh_keys(m, 2)
                if n:
                    front_stats(n)
                if b:
                    norm_factors(b, cc)
                if n:
                    front_var(n, ca)
                if m:
                    numerators(m, 0, cb)
                    probs(m, 1)
                    weigh_keys(m, 3)
                    earlier_part(m, 1, cb)
                if f and not m:
                    weight_scales()
                    weight_bits(0)
                if f:
                    front_gates(f)
                if m:
                    numerators(m, 1, cb)
                if f:
                    front_nabs(f)
                if f and not m:
                    weight_bits(1)
                if m:
                    head_stats(m, 0, cb)
                if f:
                    front_logf(f)
                if f and not m:
                    weight_bits(2)
                if m:
                    head_stats(m, 1, cb)
                    earlier_part(m, 2, cb)
                    probs(m, 2)
                if b:
                    residual(b)
                if f:
                    front_a(f)
                if b:
                    back_stats(b, cc)
                    back_var(b, cc)
                if m:
                    numerators(m, 2, cb)
                if f:
                    front_scan(f)
                if f and not m:
                    for w in range(3):
                        weight_values(w)
                if m:
                    probs(m, 3)
                if b:
                    back_nm(b)
                if m:
                    earlier_part(m, 3, cb)
                if n:
                    front_nm(n)
                if m:
                    head_stats(m, 2, cb)
                    numerators(m, 3, cb)
                    head_stats(m, 3, cb)
                if f:
                    front_ends(f)
                if b:
                    largest(b)
                if f:
                    front_args(f)
                if f and not m:
                    weight_raise()
                if m and not b and n:
                    for w in range(3):
                        weight_low(w)
                assert not n or ca.n == NA, ca.n
                assert not m or cb.n == NB, cb.n
                assert not b or cc.n == NCB, cc.n

            steps(dve, step)

            cf = Chain(dve, "chain_f")

            wait(dve, "x2_max", B)
            V.tensor_reduce(col(0), xmax, AX, ALU.max).then_inc(s["xmax_row"], 1)
            dve.wait_ge(s["xmax_all"], 1)
            cf.link(V.tensor_scalar(col(2), col(1), 1.0 / QMAX, MIN_SCALE, ALU.mult, ALU.max))
            cf.link(V.reciprocal(col(3), col(2)))
            cf.link(V.reciprocal(amp[:, 0:3], amp[:, 0:3]))
            V.tensor_tensor(col(14), col(2), amp[:, 0:1], ALU.mult)
            cf.link(V.tensor_tensor(col(34), col(2), amp[:, 1:2], ALU.mult))

            wait(dve, "h_stored", 16 * B)
            wait(dve, "x2_out", KH * B)
            with dve.Fori(0, B // 2) as i:
                blocks = [(2 * i + p, ds((2 * i + p) * S, S)) for p in range(2)]
                for p, (tb, at_b) in enumerate(blocks):
                    V.tensor_scalar(x16[:, p], x2T[:, :, at_b], col(3), QMAX, ALU.mult, ALU.min)\
                        .then_inc(s["x16_ready"], 1)
                for p, (tb, at_b) in enumerate(blocks):
                    dve.wait_ge(s["x16_ready"], tb + 1)
                    V.tensor_copy(xs[:, 0, :, at_b], x16[:, p]).then_inc(s["xhi_ready"], 1)
                for p, (tb, at_b) in enumerate(blocks):
                    dve.wait_ge(s["xhi_ready"], tb + 1)
                    V.tensor_tensor(xs[:, 1, :, at_b], x16[:, p], xs[:, 0, :, at_b], ALU.subtract)\
                        .then_inc(s["xs_ready"], 1)
                dve.wait_ge(s["xs_ready"], 2 * i + 2)

            with dve.Fori(0, B) as tb:
                for t in range(3):
                    n = 3 * tb + t
                    dve.wait_ge(s["gate_out"], n + 1 + 3)
                    hold(dve)
                    piece = gu[:, tb, t * TW:(t + 1) * TW]
                    V.tensor_reduce(gmax[:, 0, ds(n, 1)], piece, AX, ALU.max)
                    V.tensor_reduce(gmax[:, 1, ds(n, 1)], piece, AX, ALU.min).then_inc(s["gate_max"], 1)
            dve.wait_ge(s["gate_max"], 3 * B)
            V.tensor_reduce(col(10), gmax[:, 0, :], AX, ALU.max)
            cf.link(V.tensor_reduce(col(9), gmax[:, 1, :], AX, ALU.min))
            V.tensor_scalar(col(11), col(9), -1.0, None, ALU.mult).then_inc(s["gmax_row"], 1)
            dve.wait_ge(s["gmax_all"], 1)
            cf.link(V.tensor_tensor(col(18), col(12), col(13), ALU.max))
            cf.link(V.tensor_tensor(col(19), col(18), col(14), ALU.mult))
            cf.link(V.tensor_scalar(col(16), col(19), 1.0 / QMAX, MIN_SCALE, ALU.mult, ALU.max))
            V.tensor_scalar(col(24), col(16), 1.0 / 65536.0, None, ALU.mult)
            cf.link(V.reciprocal(col(20), col(16)))
            cf.link(V.tensor_tensor(col(15), col(20), col(14), ALU.mult))
            V.tensor_scalar(top16, col(12), col(15), QMAX, ALU.mult, ALU.min).then_inc(s["top_q"], 1)
            dve.wait_ge(s["top_sig"], 1)
            cf.link(V.tensor_scalar(topsq, col(17), 65536.0, 65535.0, ALU.mult, ALU.min))
            cf.link(V.tensor_tensor(col(23), top16, topsq, ALU.mult))
            V.tensor_scalar(flag[:, 0:1], col(23), col(24), NEGATIVE_TOP, ALU.mult, ALU.is_lt)\
                .then_inc(s["flag_ready"], 1)
            dve.wait_ge(s["flag_ready"], 1)
            with dve.If(dve.value_load(flag[0:1, 0:1]) > 0):
                with dve.Fori(0, B) as tb:
                    for t in range(3):
                        n = 3 * tb + t
                        g = gq[:, tb, t * TW:(t + 1) * TW]
                        V.tensor_scalar(g, gu[:, tb, t * TW:(t + 1) * TW], col(15), QMAX, ALU.mult, ALU.min)\
                            .then_inc(s["all_q"], 1)
                        dve.wait_ge(s["all_sig"], n + 1)
                        V.tensor_scalar(sq[0], sig[0], 65536.0, 65535.0, ALU.mult, ALU.min)\
                            .then_inc(s["all_sq"], 1)
                        dve.wait_ge(s["all_sq"], n + 1)
                        V.tensor_tensor(sig[0], g, sq[0], ALU.mult).then_inc(s["all_p"], 1)
                        dve.wait_ge(s["all_p"], n + 1)
                        V.tensor_reduce(pmax[:, ds(n, 1)], sig[0], AX, ALU.max,
                                        apply_absolute_value=True).then_inc(s["all_max"], 1)
                        dve.wait_ge(s["all_max"], n + 1)
                V.tensor_reduce(col(22), pmax, AX, ALU.max).then_inc(s["pmax_row"], 1)
                dve.wait_ge(s["pmax_all"], 1)
            V.tensor_scalar(gq[:, 0, :], gu[:, 0, :], col(15), QMAX, ALU.mult, ALU.min)\
                .then_inc(s["gq_ready"], 1)
            dve.sem_inc(s["gate_scale"], 1)
            cf.link(V.tensor_tensor(col(25), col(23), col(24), ALU.mult))
            cf.link(V.tensor_scalar(col(26), col(25), 1.0 / QMAX, MIN_SCALE, ALU.mult, ALU.max))
            cf.link(V.reciprocal(col(27), col(26)))
            cf.link(V.tensor_tensor(col(28), col(27), col(24), ALU.mult))

            def piece(t, row, tb):
                return t[:, tb, row * TW:(row + 1) * TW]

            def sigmoid16(j, n):
                dve.wait_ge(s["sig_ready"], n + 1)
                V.tensor_scalar(sq[j % 2], sig[j % 2], 65536.0, 65535.0, ALU.mult, ALU.min)\
                    .then_inc(s["sq_ready"], 1)

            def largest_up(j, tb, n):
                dve.wait_ge(s["up_out"], n + 1 + 3)
                hold(dve)
                V.tensor_reduce(umax[:, ds(n, 1)], piece(gu, j % 3, tb), AX, ALU.max,
                                apply_absolute_value=True).then_inc(s["up_max"], 1)

            def gated(j, tb, n):
                g = piece(gq, j % 3, tb)
                dve.wait_ge(s["sq_ready"], n + 1 + 2)
                V.scalar_tensor_tensor(g, g, col(28), sq[j % 2], ALU.mult, ALU.mult)\
                    .then_inc(s["p_ready"], 1)

            def all_three(j, tb, n):
                sigmoid16(j, n)
                largest_up(j, tb, n)
                gated(j, tb, n)
                if j > 0:
                    dve.wait_ge(s["p_ready"], n + (j == 5))

            with dve.Fori(0, B // 2 - 1) as i:
                for j in range(6):
                    all_three(j, 2 * i + j // 3, 6 * i + j)
            first = 3 * (B - 2)
            for j in range(4):
                all_three(j, B - 2 + j // 3, first + j)
            sigmoid16(4, first + 4)
            largest_up(4, B - 1, first + 4)
            dve.wait_ge(s["p_ready"], first + 4)
            sigmoid16(5, first + 5)
            largest_up(5, B - 1, first + 5)
            dve.wait_ge(s["up_max"], 3 * B)
            V.tensor_reduce(col(30), umax, AX, ALU.max).then_inc(s["umax_row"], 1)
            gated(4, B - 1, first + 4)
            dve.wait_ge(s["umax_all"], 1)
            cf.link(V.tensor_tensor(col(36), col(31), col(34), ALU.mult))
            cf.link(V.tensor_scalar(col(33), col(36), 1.0 / QMAX, MIN_SCALE, ALU.mult, ALU.max))
            cf.link(V.reciprocal(col(37), col(33)))
            V.tensor_tensor(col(35), col(37), col(34), ALU.mult).then_inc(s["up_scale"], 1)
            gated(5, B - 1, first + 5)
            cf.link(V.tensor_tensor(col(44), col(33), col(26), ALU.mult))
            dve.wait_ge(s["p_ready"], 3 * B)

            with dve.Fori(0, B // 2) as i:
                for p in range(2):
                    tb = 2 * i + p
                    halves = [slice(h * BW // 2, (h + 1) * BW // 2) for h in range(2)]
                    dve.wait_ge(s["uq_ready"], 2 * tb + 1)
                    V.tensor_tensor(gu[:, tb, halves[0]], gq[:, tb, halves[0]], uq[:, p, halves[0]], ALU.mult)\
                        .then_inc(s["o_first"], 1)
                    dve.wait_ge(s["uq_ready"], 2 * tb + 2)
                    V.tensor_tensor(gu[:, tb, halves[1]], gq[:, tb, halves[1]], uq[:, p, halves[1]], ALU.mult)\
                        .then_inc(s["o_ready"], 1)
                    dve.wait_ge(s["o_first"], tb + 1)
                    hold(dve)
                    V.tensor_reduce(omax[:, 0, ds(tb, 1)], gu[:, tb, halves[0]], AX, ALU.max,
                                    apply_absolute_value=True)
                    dve.wait_ge(s["o_ready"], tb + 1 + 2)
                    hold(dve)
                    V.tensor_reduce(omax[:, 1, ds(tb, 1)], gu[:, tb, halves[1]], AX, ALU.max,
                                    apply_absolute_value=True).then_inc(s["o_max"], 1)
            dve.wait_ge(s["o_max"], B)
            V.tensor_reduce(col(40), omax.rearrange("p a b -> p (a b)"), AX, ALU.max).then_inc(s["omax_row"], 1)
            dve.wait_ge(s["omax_all"], 1)
            cf.link(V.tensor_tensor(col(47), col(41), col(44), ALU.mult))
            cf.link(V.tensor_scalar(col(42), col(47), 1.0 / QMAX, MIN_SCALE, ALU.mult, ALU.max))
            cf.link(V.reciprocal(col(43), col(42)))
            V.tensor_tensor(col(45), col(43), col(44), ALU.mult).then_inc(s["o_scale"], 1)
            cf.link(V.tensor_tensor(col(48), col(42), amp[:, 2:3], ALU.mult))

            def split(b, p):
                dve.wait_ge(s["o_int"], b + 1)
                V.tensor_copy(os_[:, 2 * p, :], o16[:, p, :]).then_inc(s["o_hi"], 1)
                dve.wait_ge(s["o_hi"], b + 1)
                V.tensor_tensor(os_[:, 2 * p + 1, :], o16[:, p, :], os_[:, 2 * p, :],
                                ALU.subtract).then_inc(s["o_split"], 1)

            def result(i, p):
                dve.wait_ge(h_back[p], 16 * (i + 1))
                dve.wait_ge(y_stored[p], 16 * (i + 1))
                for half in range(2):
                    dve.wait_ge(s["mm_down"], 2 * (2 * i + p) + half + 1)
                    cols = slice(2 * half, 2 * half + 2)
                    V.scalar_tensor_tensor(y_buf[p][:, cols, :].rearrange("p c h -> p (c h)"),
                                           psum[:, 2 * p + half, :], col(48),
                                           h_back_buf[p][:, cols, :].rearrange("p c h -> p (c h)"),
                                           ALU.mult, ALU.add).then_inc(s["down_out"], 1)

            split(0, 0)
            split(1, 1)
            with dve.Fori(0, B // 2 - 1) as i:
                for p in range(2):
                    result(i, p)
                    split(2 * i + p + 2, p)
            for p in range(2):
                result(B // 2 - 1, p)


_INS = ["x", "ctx_1024", "L0_xattn_w_igate", "L0_xattn_b_igate", "L0_xattn_w_fgate", "L0_xattn_b_fgate",
        "L0_xattn_ln_weight", "L0_ffn_w_gate", "L0_ffn_w_up", "L0_ffn_w_down"]


def kernel(**inputs):
    import numpy as _np
    import concourse.bacc as _bacc
    from concourse import mybir as _mybir
    from concourse.bass_utils import run_bass_kernel_spmd as _run

    nc = _bacc.Bacc("TRN2", target_bir_lowering=False, num_devices=1)
    arrays, args = {}, []
    for name in _INS:
        a = _np.ascontiguousarray(inputs[name])
        arrays[f"in_{name}"] = a
        args.append(nc.dram_tensor(f"in_{name}", a.shape, _mybir.dt.from_np(a.dtype), kind="ExternalInput").ap())
    shape = inputs["x"].shape
    y = nc.dram_tensor("out_y", shape, _mybir.dt.float32, kind="ExternalOutput").ap()
    attention_ffn(nc, *args, y)
    r = _run(nc, [arrays], core_ids=[0])
    return r.results[0]["out_y"]
```
